# Optimizing a Trainium2 kernel written in Bass

```python
import numpy as np
import jax
import jax.numpy as jnp

def _softmax(x, axis=-1):
    return jax.nn.softmax(x, axis=axis)

def _gelu(x):
    return jax.nn.gelu(x, approximate=True)

def _silu(x):
    return jax.nn.silu(x)

def _sigmoid(x):
    return jax.nn.sigmoid(x)

def _layernorm(x, axis=-1, eps=1e-05):
    m = jnp.mean(x, axis=axis, keepdims=True)
    v = jnp.var(x, axis=axis, keepdims=True)
    return (x - m) / jnp.sqrt(v + eps)

def _scatter_add(tgt, idx, src, axis=0):
    return tgt.at[idx].add(src)

def _segment_sum(src, seg, n):
    return jax.ops.segment_sum(src, seg, n)
kernel_name = 'mk_gnn_resnorm_d4_gnn_r8_9f510f'

def setup_inputs(seed: int=0):
    np.random.seed(seed)
    _w = jnp.asarray

    def _rec_inputs():
        import jax
        import jax.numpy as jnp
        _gk = jax.random.key(seed)
        x = 3.059e-06 + 0.006317 * jax.random.normal(jax.random.fold_in(_gk, 1), (6250, 128), jnp.float32)
        _s = jax.random.randint(jax.random.fold_in(_gk, 2), (50000,), 0, 6250, jnp.int32)
        _d = jax.random.randint(jax.random.fold_in(_gk, 3), (50000,), 0, 6250, jnp.int32)
        _loop = jnp.arange(6250, dtype=jnp.int32)
        src = jnp.concatenate([_s, _d, _loop])
        dst = jnp.concatenate([_d, _s, _loop])
        _o = jnp.argsort(dst, stable=True)
        src = src[_o]
        dst = dst[_o]
        edge_type_16 = jax.random.randint(jax.random.fold_in(_gk, 13), (106250,), 0, 16, jnp.int32)
        edge_type_8 = jax.random.randint(jax.random.fold_in(_gk, 14), (106250,), 0, 8, jnp.int32)
        return (x, src, dst, edge_type_16, edge_type_8)
    x, src, dst, edge_type_16, edge_type_8 = _rec_inputs()

    def _L0_gnn_setup():
        import jax, jax.numpy as jnp
        import numpy as np
        N_NODES = 6250
        N_REL = 16
        D_EMB = 128
        D_HID = 128
        D_OUT = 128
        N_EDGES = 200000

        def _xavier(key, shape, fan_in, fan_out, dtype=jnp.float32):
            lim = float(np.sqrt(6.0 / (fan_in + fan_out)))
            return jax.random.uniform(key, shape, dtype, -lim, lim)

        def rgcn_conv(x, edge_index, edge_type, W, W_root, b):
            src, dst = (edge_index[0], edge_index[1])
            seg = dst * N_REL + edge_type
            x_src = x[src]
            summed = jax.ops.segment_sum(x_src, seg, num_segments=N_NODES * N_REL)
            cnt = jax.ops.segment_sum(jnp.ones((src.shape[0],), x.dtype), seg, num_segments=N_NODES * N_REL)
            agg = summed / jnp.maximum(cnt, 1.0)[:, None]
            agg = agg.reshape(N_NODES, N_REL, x.shape[1])
            return jnp.einsum('nrd,rdh->nh', agg, W) + x @ W_root + b
        key = jax.random.key(seed)
        ks = jax.random.split(key, 10)
        edge_index = jax.random.randint(ks[0], (2, N_EDGES), 0, N_NODES, dtype=jnp.int64)
        edge_type = jax.random.randint(ks[1], (N_EDGES,), 0, N_REL, dtype=jnp.int64)
        emb = _xavier(ks[2], (N_NODES, D_EMB), N_NODES, D_EMB)
        W1 = _xavier(ks[3], (N_REL, D_EMB, D_HID), D_EMB, D_HID)
        root1 = _xavier(ks[4], (D_EMB, D_HID), D_EMB, D_HID)
        b1 = jnp.zeros((D_HID,), jnp.float32)
        W2 = _xavier(ks[5], (N_REL, D_HID, D_OUT), D_HID, D_OUT)
        root2 = _xavier(ks[6], (D_HID, D_OUT), D_HID, D_OUT)
        b2 = jnp.zeros((D_OUT,), jnp.float32)
        return {'edge_index': edge_index, 'edge_type': edge_type, 'emb': emb, 'W1': W1, 'root1': root1, 'b1': b1, 'W2': W2, 'root2': root2, 'b2': b2}
    _L0_gnn_all = _L0_gnn_setup()
    _L0_gnn_in = {k: v for k, v in _L0_gnn_all.items() if k in ('W1', 'root1', 'b1', 'W2', 'root2', 'b2')}
    del _L0_gnn_all

    def _L1_gnn_setup():
        import jax, jax.numpy as jnp
        import numpy as np
        N = 6250
        E = 75000
        IN_CH = 128
        HEADS = 8
        HEAD_DIM = 16
        OUT_CH = 128
        NEG_SLOPE = 0.2
        LN_EPS = 1e-05
        key = jax.random.key(seed)
        ks = jax.random.split(key, 9)
        x = jax.random.normal(ks[0], (N, IN_CH), dtype=jnp.float32)
        edge_index = jax.random.randint(ks[1], (2, E), 0, N, dtype=jnp.int64)
        lin_w = jax.random.normal(ks[2], (HEADS * HEAD_DIM, IN_CH), dtype=jnp.float32) * 0.05
        att_src = jax.random.normal(ks[3], (1, HEADS, HEAD_DIM), dtype=jnp.float32) * 0.1
        att_dst = jax.random.normal(ks[4], (1, HEADS, HEAD_DIM), dtype=jnp.float32) * 0.1
        gat_bias = jnp.zeros((HEADS * HEAD_DIM,), dtype=jnp.float32)
        proj_w = jax.random.normal(ks[5], (OUT_CH, HEADS * HEAD_DIM), dtype=jnp.float32) * 0.05
        proj_b = jnp.zeros((OUT_CH,), dtype=jnp.float32)
        ln_gamma = jnp.ones((OUT_CH,), dtype=jnp.float32)
        ln_beta = jnp.zeros((OUT_CH,), dtype=jnp.float32)
        return {'x': x, 'edge_index': edge_index, 'lin_w': lin_w, 'att_src': att_src, 'att_dst': att_dst, 'gat_bias': gat_bias, 'proj_w': proj_w, 'proj_b': proj_b, 'ln_gamma': ln_gamma, 'ln_beta': ln_beta}
    _L1_gnn_all = _L1_gnn_setup()
    _L1_gnn_in = {k: v for k, v in _L1_gnn_all.items() if k in ('lin_w', 'att_src', 'att_dst', 'gat_bias', 'proj_w', 'proj_b', 'ln_gamma', 'ln_beta')}
    del _L1_gnn_all

    def _L2_gnn_setup():
        import jax, jax.numpy as jnp
        import numpy as np
        N, E, D, R = (6250, 200000, 128, 8)
        EPS = 1e-05
        key = jax.random.key(seed)
        ks = jax.random.split(key, 12)
        s = 1.0 / np.sqrt(D)
        return {'node_feats': jax.random.normal(ks[0], (N, D), dtype=jnp.float32), 'src': jax.random.randint(ks[1], (E,), 0, N, dtype=jnp.int32), 'dst': jax.random.randint(ks[2], (E,), 0, N, dtype=jnp.int32), 'etype': jax.random.randint(ks[3], (E,), 0, R, dtype=jnp.int32), 'basis_w': jax.random.normal(ks[4], (R, D, D), dtype=jnp.float32) * s, 'w_comp': jax.random.normal(ks[5], (R, R), dtype=jnp.float32) * (1.0 / np.sqrt(R)), 'loop_w': jax.random.normal(ks[6], (D, D), dtype=jnp.float32) * s, 'bias': jax.random.normal(ks[7], (D,), dtype=jnp.float32) * 0.01, 'res_w': jax.random.normal(ks[8], (D, D), dtype=jnp.float32) * s, 'res_b': jax.random.normal(ks[9], (D,), dtype=jnp.float32) * 0.01, 'bn_gamma': jnp.ones((D,), dtype=jnp.float32), 'bn_beta': jnp.zeros((D,), dtype=jnp.float32)}
    _L2_gnn_all = _L2_gnn_setup()
    _L2_gnn_in = {k: v for k, v in _L2_gnn_all.items() if k in ('basis_w', 'w_comp', 'loop_w', 'bias', 'res_w', 'res_b', 'bn_gamma', 'bn_beta')}
    del _L2_gnn_all

    def _L3_gnn_setup():
        import jax, jax.numpy as jnp
        import numpy as np
        N_NODES = 12500
        HIDDEN = 128
        OUT = 128
        N_EDGES = 200000

        def _sage_conv(x, src, dst, W_l, W_r, b):
            n = x.shape[0]
            msg_sum = jax.ops.segment_sum(x[src], dst, num_segments=n)
            deg = jax.ops.segment_sum(jnp.ones_like(dst, dtype=x.dtype), dst, num_segments=n)
            mean = msg_sum / jnp.maximum(deg, 1.0)[:, None]
            return mean @ W_l.T + b + x @ W_r.T
        key = jax.random.key(seed)
        ks = jax.random.split(key, 8)
        x = jax.random.normal(ks[0], (N_NODES, HIDDEN), dtype=jnp.float32)
        edge_index = jax.random.randint(ks[1], (2, N_EDGES), 0, N_NODES, dtype=jnp.int64)
        s = 1.0 / np.sqrt(HIDDEN)
        W1_l = jax.random.uniform(ks[2], (HIDDEN, HIDDEN), jnp.float32, -s, s)
        W1_r = jax.random.uniform(ks[3], (HIDDEN, HIDDEN), jnp.float32, -s, s)
        b1 = jnp.zeros((HIDDEN,), jnp.float32)
        W2_l = jax.random.uniform(ks[4], (OUT, HIDDEN), jnp.float32, -s, s)
        W2_r = jax.random.uniform(ks[5], (OUT, HIDDEN), jnp.float32, -s, s)
        b2 = jnp.zeros((OUT,), jnp.float32)
        return {'x': x, 'edge_index': edge_index, 'W1_l': W1_l, 'W1_r': W1_r, 'b1': b1, 'W2_l': W2_l, 'W2_r': W2_r, 'b2': b2}
    _L3_gnn_all = _L3_gnn_setup()
    _L3_gnn_in = {k: v for k, v in _L3_gnn_all.items() if k in ('W1_l', 'W1_r', 'b1', 'W2_l', 'W2_r', 'b2')}
    del _L3_gnn_all
    return {'x': x, 'src': src, 'dst': dst, 'edge_type_16': edge_type_16, 'edge_type_8': edge_type_8, 'L0_gnn_W1': _L0_gnn_in['W1'], 'L0_gnn_root1': _L0_gnn_in['root1'], 'L0_gnn_b1': _L0_gnn_in['b1'], 'L0_gnn_W2': _L0_gnn_in['W2'], 'L0_gnn_root2': _L0_gnn_in['root2'], 'L0_gnn_b2': _L0_gnn_in['b2'], 'L1_gnn_lin_w': _L1_gnn_in['lin_w'], 'L1_gnn_att_src': _L1_gnn_in['att_src'], 'L1_gnn_att_dst': _L1_gnn_in['att_dst'], 'L1_gnn_gat_bias': _L1_gnn_in['gat_bias'], 'L1_gnn_proj_w': _L1_gnn_in['proj_w'], 'L1_gnn_proj_b': _L1_gnn_in['proj_b'], 'L1_gnn_ln_gamma': _L1_gnn_in['ln_gamma'], 'L1_gnn_ln_beta': _L1_gnn_in['ln_beta'], 'L2_gnn_basis_w': _L2_gnn_in['basis_w'], 'L2_gnn_w_comp': _L2_gnn_in['w_comp'], 'L2_gnn_loop_w': _L2_gnn_in['loop_w'], 'L2_gnn_bias': _L2_gnn_in['bias'], 'L2_gnn_res_w': _L2_gnn_in['res_w'], 'L2_gnn_res_b': _L2_gnn_in['res_b'], 'L2_gnn_bn_gamma': _L2_gnn_in['bn_gamma'], 'L2_gnn_bn_beta': _L2_gnn_in['bn_beta'], 'L3_gnn_W1_l': _L3_gnn_in['W1_l'], 'L3_gnn_W1_r': _L3_gnn_in['W1_r'], 'L3_gnn_b1': _L3_gnn_in['b1'], 'L3_gnn_W2_l': _L3_gnn_in['W2_l'], 'L3_gnn_W2_r': _L3_gnn_in['W2_r'], 'L3_gnn_b2': _L3_gnn_in['b2']}

def reference(x, src, dst, edge_type_16, edge_type_8, L0_gnn_W1, L0_gnn_root1, L0_gnn_b1, L0_gnn_W2, L0_gnn_root2, L0_gnn_b2, L1_gnn_lin_w, L1_gnn_att_src, L1_gnn_att_dst, L1_gnn_gat_bias, L1_gnn_proj_w, L1_gnn_proj_b, L1_gnn_ln_gamma, L1_gnn_ln_beta, L2_gnn_basis_w, L2_gnn_w_comp, L2_gnn_loop_w, L2_gnn_bias, L2_gnn_res_w, L2_gnn_res_b, L2_gnn_bn_gamma, L2_gnn_bn_beta, L3_gnn_W1_l, L3_gnn_W1_r, L3_gnn_b1, L3_gnn_W2_l, L3_gnn_W2_r, L3_gnn_b2):
    import jax
    import jax.numpy as jnp

    def _L0_gnn_ref(edge_index, edge_type, emb, W1, root1, b1, W2, root2, b2):
        import jax, jax.numpy as jnp
        import numpy as np
        N_NODES = 6250
        N_REL = 16
        D_EMB = 128
        D_HID = 128
        D_OUT = 128
        N_EDGES = 200000

        def _xavier(key, shape, fan_in, fan_out, dtype=jnp.float32):
            lim = float(np.sqrt(6.0 / (fan_in + fan_out)))
            return jax.random.uniform(key, shape, dtype, -lim, lim)

        def rgcn_conv(x, edge_index, edge_type, W, W_root, b):
            src, dst = (edge_index[0], edge_index[1])
            seg = dst * N_REL + edge_type
            x_src = x[src]
            summed = jax.ops.segment_sum(x_src, seg, num_segments=N_NODES * N_REL)
            cnt = jax.ops.segment_sum(jnp.ones((src.shape[0],), x.dtype), seg, num_segments=N_NODES * N_REL)
            agg = summed / jnp.maximum(cnt, 1.0)[:, None]
            agg = agg.reshape(N_NODES, N_REL, x.shape[1])
            return jnp.einsum('nrd,rdh->nh', agg, W) + x @ W_root + b
        x = emb
        x = jax.nn.relu(rgcn_conv(x, edge_index, edge_type, W1, root1, b1))
        x = rgcn_conv(x, edge_index, edge_type, W2, root2, b2)
        return x

    def _L1_gnn_ref(x, edge_index, lin_w, att_src, att_dst, gat_bias, proj_w, proj_b, ln_gamma, ln_beta):
        import jax, jax.numpy as jnp
        import numpy as np
        N = 6250
        E = 75000
        IN_CH = 128
        HEADS = 8
        HEAD_DIM = 16
        OUT_CH = 128
        NEG_SLOPE = 0.2
        LN_EPS = 1e-05
        n = x.shape[0]
        h = (x @ lin_w.T).reshape(n, HEADS, HEAD_DIM)
        a_src = (h * att_src).sum(-1)
        a_dst = (h * att_dst).sum(-1)
        loops = jnp.arange(n, dtype=edge_index.dtype)
        src = jnp.concatenate([edge_index[0], loops])
        dst = jnp.concatenate([edge_index[1], loops])
        logits = jax.nn.leaky_relu(a_src[src] + a_dst[dst], NEG_SLOPE)
        seg_max = jax.ops.segment_max(logits, dst, num_segments=n)
        e = jnp.exp(logits - seg_max[dst])
        denom = jax.ops.segment_sum(e, dst, num_segments=n)
        alpha = e / denom[dst]
        agg = jax.ops.segment_sum(h[src] * alpha[:, :, None], dst, num_segments=n)
        gat_out = agg.reshape(n, HEADS * HEAD_DIM) + gat_bias
        out = gat_out @ proj_w.T + proj_b
        mu = out.mean(-1, keepdims=True)
        var = ((out - mu) ** 2).mean(-1, keepdims=True)
        out = (out - mu) * jax.lax.rsqrt(var + LN_EPS) * ln_gamma + ln_beta
        return out

    def _L2_gnn_ref(node_feats, src, dst, etype, basis_w, w_comp, loop_w, bias, res_w, res_b, bn_gamma, bn_beta):
        import jax, jax.numpy as jnp
        import numpy as np
        N, E, D, R = (6250, 200000, 128, 8)
        EPS = 1e-05
        x = node_feats
        W = jnp.einsum('rb,bio->rio', w_comp, basis_w)
        xW = jnp.einsum('ni,rio->nro', x, W)
        msg = xW[src, etype]
        agg = jax.ops.segment_sum(msg, dst, num_segments=N)
        h = jax.nn.relu(agg + x @ loop_w + bias)
        h = h + jax.nn.relu(x @ res_w + res_b)
        mean = jnp.mean(h, axis=0)
        var = jnp.var(h, axis=0)
        return (h - mean) * jax.lax.rsqrt(var + EPS) * bn_gamma + bn_beta

    def _L3_gnn_ref(x, edge_index, W1_l, W1_r, b1, W2_l, W2_r, b2):
        import jax, jax.numpy as jnp
        import numpy as np
        N_NODES = 12500
        HIDDEN = 128
        OUT = 128
        N_EDGES = 200000

        def _sage_conv(x, src, dst, W_l, W_r, b):
            n = x.shape[0]
            msg_sum = jax.ops.segment_sum(x[src], dst, num_segments=n)
            deg = jax.ops.segment_sum(jnp.ones_like(dst, dtype=x.dtype), dst, num_segments=n)
            mean = msg_sum / jnp.maximum(deg, 1.0)[:, None]
            return mean @ W_l.T + b + x @ W_r.T
        src, dst = (edge_index[0], edge_index[1])
        h = jax.nn.relu(_sage_conv(x, src, dst, W1_l, W1_r, b1))
        out = _sage_conv(h, src, dst, W2_l, W2_r, b2)
        return out
    edge_index = jnp.stack([src, dst])
    x = _layernorm(x + _L0_gnn_ref(edge_index, edge_type_16, x, L0_gnn_W1, L0_gnn_root1, L0_gnn_b1, L0_gnn_W2, L0_gnn_root2, L0_gnn_b2), axis=-1)
    x = _layernorm(x + _L1_gnn_ref(x, edge_index, L1_gnn_lin_w, L1_gnn_att_src, L1_gnn_att_dst, L1_gnn_gat_bias, L1_gnn_proj_w, L1_gnn_proj_b, L1_gnn_ln_gamma, L1_gnn_ln_beta), axis=-1)
    x = _layernorm(x + _L2_gnn_ref(x, src, dst, edge_type_8, L2_gnn_basis_w, L2_gnn_w_comp, L2_gnn_loop_w, L2_gnn_bias, L2_gnn_res_w, L2_gnn_res_b, L2_gnn_bn_gamma, L2_gnn_bn_beta), axis=-1)
    x = _layernorm(x + _L3_gnn_ref(x, edge_index, L3_gnn_W1_l, L3_gnn_W1_r, L3_gnn_b1, L3_gnn_W2_l, L3_gnn_W2_r, L3_gnn_b2), axis=-1)
    return x

_drawn_inputs = setup_inputs


def setup_inputs(seed=0):
    import zlib

    import numpy as np

    out = dict(_drawn_inputs(seed))
    spreads = {'L0_gnn_b1': (0.0, 0.1),
     'L0_gnn_b2': (0.0, 0.1),
     'L1_gnn_gat_bias': (0.0, 0.1),
     'L1_gnn_proj_b': (0.0, 0.1),
     'L1_gnn_ln_gamma': (1.0, 0.2),
     'L1_gnn_ln_beta': (0.0, 0.1),
     'L2_gnn_bn_gamma': (1.0, 0.2),
     'L2_gnn_bn_beta': (0.0, 0.1),
     'L3_gnn_b1': (0.0, 0.1),
     'L3_gnn_b2': (0.0, 0.1)}
    factors = {'L1_gnn_att_src': 2.801,
     'L1_gnn_att_dst': 7.69,
     'L2_gnn_bias': 40.996,
     'L2_gnn_res_b': 22.365}
    for name, (base, spread) in spreads.items():
        noise = np.random.default_rng([zlib.crc32(name.encode()), seed]).standard_normal(out[name].shape)
        drawn = base * np.exp(spread * noise) if base else spread * noise
        out[name] = jnp.asarray(drawn.astype(out[name].dtype))
    for name, factor in factors.items():
        out[name] = (out[name] * factor).astype(out[name].dtype)
    return out
```

```python
import concourse.bass as bass
from concourse import mybir
from contextlib import ExitStack

FP32 = mybir.dt.float32
BF16 = mybir.dt.bfloat16
INT32 = mybir.dt.int32
ALU = mybir.AluOpType
ACT = mybir.ActivationFunctionType

P = 128
NODES = 6250
EDGES = 106250
R16, R8 = 16, 8
HEADS = 8
HD = P // HEADS
NODES_P = 6400
BLOCKS = NODES_P // P
CHUNK = 400
CHUNKS = NODES_P // CHUNK
META = 12
G = 8
TILES = 832
BATCHES = TILES // G
ROWB = 7
FULL = EDGES // P
REST = EDGES - FULL * P
XBLOCKS = (NODES + P - 1) // P
NO_NODE = float(1 << 20)
BIG = 1e30
GATW = P + HEADS
LN_EPS = 1e-5
SLOPE = 0.2


def mid(ap, n):
    return ap.unsqueeze(1).to_broadcast([ap.shape[0], n, ap.shape[1]])


def last(ap, n):
    return ap.unsqueeze(2).to_broadcast([ap.shape[0], ap.shape[1], n])


def build(nc, a, out):
    ctx = ExitStack()
    with ctx:
        ctx.enter_context(nc.allow_non_contiguous_dma(reason="columns of indices and of biases, once"))

        def sb(name, shape, dt=FP32):
            return ctx.enter_context(nc.sbuf_tensor(name, shape, dt))

        def sem(name):
            return ctx.enter_context(nc.semaphore(name))

        table16 = nc.dram_tensor("table16", [NODES_P * R16, P], FP32, kind="Internal").ap()
        table8 = nc.dram_tensor("table8", [NODES_P * R8, P], FP32, kind="Internal").ap()
        table_gat = nc.dram_tensor("table_gat", [NODES_P, GATW], FP32, kind="Internal").ap()
        table1 = nc.dram_tensor("table1", [NODES_P, P], FP32, kind="Internal").ap()
        node_logits = nc.dram_tensor("node_logits", [NODES_P, 2 * HEADS], FP32, kind="Internal").ap()
        flag_row = nc.dram_tensor("flag_row", [TILES], INT32, kind="Internal").ap()
        first_row = nc.dram_tensor("first_row", [TILES], INT32, kind="Internal").ap()
        etype_row = nc.dram_tensor("etype_row", [(TILES + 1) * P], FP32, kind="Internal").ap()
        penalty_row = nc.dram_tensor("penalty_row", [(TILES + 1) * P], FP32, kind="Internal").ap()

        X = sb("X", [P, NODES_P])
        H = sb("H", [P, NODES_P])
        ACC = sb("ACC", [P, 2, NODES_P])
        sums, aux = ACC[:, 0, :], ACC[:, 1, :]
        WT = sb("WT", [P, 2048])
        WR = sb("WR", [P, 2112])
        TOUT = sb("TOUT", [P, 2, 2048])
        STG = sb("STG", [P, 2, P])
        iota_f = sb("iota_f", [P, P])
        pidx = sb("pidx", [P, 1])
        head_iota = sb("head_iota", [P, HEADS])
        ident = sb("ident", [P, P])
        mean_mat = sb("mean_mat", [P, P])
        ones_mat = sb("ones_mat", [P, P])
        local = sb("local", [P, ROWB * P])
        idx16 = sb("idx16", [P, ROWB * P], INT32)
        idx8 = sb("idx8", [P, ROWB * P], INT32)
        idx1 = sb("idx1", [P, ROWB * P], INT32)
        etype = sb("etype", [P, ROWB * P])
        start = sb("start", [P, ROWB * P])
        wcol = sb("wcol", [P, TILES])
        base_i = sb("base_i", [P, ROWB], INT32)
        prev_last = sb("prev_last", [P, ROWB], INT32)
        meta = sb("meta", [1, BATCHES, META], INT32)
        sel_first = sb("sel_first", [P, P])
        sel_last = sb("sel_last", [P, P])
        batch_first = sb("batch_first", [P, P])
        ends = sb("ends", [P, 2, ROWB])
        bends = sb("bends", [P, 2, ROWB])
        spans = sb("spans", [P, 3, ROWB])
        flag_i = sb("flag_i", [P, ROWB], INT32)
        first_i = sb("first_i", [P, ROWB], INT32)
        rows_i = ACC[:, 0, 0:4 * ROWB * P].bitcast(INT32).rearrange("p (a b e) -> p a b e", a=4, b=ROWB)
        rows_f = ACC[:, 1, 0:7 * ROWB * P].rearrange("p (a b e) -> p a b e", a=7, b=ROWB)
        x_rows = H[:, 0:XBLOCKS * P].rearrange("p (b f) -> p b f", f=P)
        SRC, DST, ET16, ET8 = range(4)
        F_LOCAL, F_IDX16, F_IDX8, F_SRC, F_ET, F_START, F_PEN = range(7)

        OH = sb("OH", [P, 2, G * P])
        GB = sb("GB", [P, 2, G * GATW])
        IDX = sb("IDX", [P, 2, G], INT32)
        OHR = sb("OHR", [P, 2, G, R16], BF16)
        rowbuf = sb("rowbuf", [R16, 2, G * P])
        ETR = rowbuf
        wstage = sb("wstage", [P, 2, G])

        def oh(b, j):
            return OH[:, b, j * P:(j + 1) * P]

        def oh16(b):
            return OH[:, b, 0:G * P // 2].bitcast(BF16).rearrange("p (j d) -> p j d", j=G)

        M = TOUT[:, 0, 0:G * P].rearrange("p (j f) -> p j f", j=G)
        OHT = TOUT[:, 1, 0:G * P].rearrange("p (j e) -> p j e", j=G)
        PEN = WR[0:HEADS, 0:2 * (G * P + 1)].rearrange("p (b e) -> p b e", b=2)
        AW = sb("AW", [P, 2, G, 2 * HEADS])
        AD0 = sb("AD0", [HEADS, 2, 1])
        AD = sb("AD", [P, G, 2 * HEADS])
        XS = sb("XS", [P, G, HEADS])
        FS = rowbuf[0:HEADS, 0, :]
        BS = rowbuf[0:HEADS, 1, :]
        carry = sb("carry", [HEADS, 1])
        RZ = sb("RZ", [HEADS, 2])
        RL = sb("RL", [HEADS, 2])
        RD = sb("RD", [HEADS, 1])
        RE = sb("RE", [HEADS, 1])
        RS = sb("RS", [P, 2])
        ZL = sb("ZL", [P, 3, G, HEADS])
        ZD = sb("ZD", [P, 2, G, HEADS])
        WE = sb("WE", [P, G, 2, HEADS])
        expand = sb("expand", [HEADS, P + 2 * HEADS])
        den_mat = sb("den_mat", [2 * HEADS, P])
        own_mat = sb("own_mat", [2 * HEADS, P])
        lin_cat = sb("lin_cat", [P, P + 3 * HEADS])
        cat_rhs = sb("cat_rhs", [P, P + 3 * HEADS])
        hsel = sb("hsel", [P, HEADS])
        shift = sb("shift", [P, 4])
        below = sb("below", [P, P])

        T0, T1, T2, T3, T4 = (GB[:, :, :].rearrange("p b n -> p (b n)")[:, n * CHUNK:(n + 1) * CHUNK] for n in range(5))
        T5 = OH[:, 0, 0:CHUNK]
        bn = sb("bn", [P, CHUNKS, 6])
        bnv = sb("bnv", [P, 8])
        eps = sb("eps", [P, 1])
        wcomp = sb("wcomp", [P, R8 * R8])

        MATS = ["L0_gnn_root1", "L0_gnn_root2", "L1_gnn_lin_w", "L1_gnn_proj_w", "L2_gnn_loop_w", "L2_gnn_res_w",
                "L3_gnn_W1_l", "L3_gnn_W1_r", "L3_gnn_W2_l", "L3_gnn_W2_r"]
        VECS = ["L0_gnn_b1", "L0_gnn_b2", "L1_gnn_gat_bias", "L1_gnn_proj_b", "L1_gnn_ln_gamma", "L1_gnn_ln_beta",
                "L2_gnn_bias", "L2_gnn_res_b", "L2_gnn_bn_gamma", "L2_gnn_bn_beta", "L3_gnn_b1", "L3_gnn_b2"]
        mats = sb("mats", [P, len(MATS), P])
        vecs = sb("vecs", [P, len(VECS) + 2])
        TURNED = ["L1_gnn_proj_w", "L3_gnn_W1_l", "L3_gnn_W1_r", "L3_gnn_W2_l", "L3_gnn_W2_r"]
        turned = sb("turned", [P, len(TURNED), P])

        def mat(name):
            return mats[:, MATS.index(name), :]

        def mat_t(name):
            return turned[:, TURNED.index(name), :]

        def vec(name):
            n = VECS.index(name)
            return vecs[:, n:n + 1]

        att_src, att_dst = (vecs[:, len(VECS) + n:len(VECS) + n + 1] for n in range(2))
        BASIS, MIXED = WT[:, 0:R8 * P], WT[:, R8 * P:2 * R8 * P]

        PS = ctx.enter_context(nc.psum_tensor("PS", [P, 8, 512], FP32))

        pad_zero = sem("pad_zero")
        cleared = sem("cleared")
        rows_in = sem("rows_in")
        meta_out = sem("meta_out")
        base_in = sem("base_in")
        ends_ps = sem("ends_ps")
        x_in = sem("x_in")
        w_in = sem("w_in")
        w2_in = sem("w2_in")
        basis_in = sem("basis_in")
        scratch = sem("scratch")
        prep = sem("prep")
        turn_ps = sem("turn_ps")
        turn_sb = sem("turn_sb")
        mixed = sem("mixed")
        out_ps = sem("out_ps")
        out_sb = sem("out_sb")
        out_done = sem("out_done")

        class Table:

            def __init__(self, name, source, weights, dram, ready):
                self.source, self.weights, self.dram = source, weights, dram
                self.width = weights.shape[1]
                self.rows = dram.shape[0] // NODES_P
                self.part = self.width if self.width <= 512 else self.width // 2
                self.ready = ready
                self.staged = sem(name + "_staged")
                self.made = sem(name + "_made")
                self.out_a = sem(name + "_out_a")
                self.out_d = sem(name + "_out_d")
                self.stored = [sem(f"{name}_stored{b}") for b in range(2)]
                self.zeroed = sem(name + "_zeroed")
                self.stores = 2 if dram is table_gat else 1

        class Round:

            def __init__(self, name, kind, idx=None, table=None):
                self.kind, self.idx, self.table = kind, idx, table
                self.width = table.dram.shape[1] if table else 0
                self.idx_staged = sem(name + "_idx_staged")
                self.begun = sem(name + "_begun")
                self.gathered = [sem(f"{name}_gathered{b}") for b in range(2)]
                self.oh_ready = sem(name + "_oh_ready")
                self.agg_ready = sem(name + "_agg_ready")
                self.agg_free = sem(name + "_agg_free")

        TWO = 2 * G
        LOOKS = 4

        class Stage:

            def __init__(self, name, dve, pe, act):
                self.n_dve, self.n_pe, self.n_act = dve, pe, act
                self.dve, self.pe, self.act = sem(name + "_dve"), sem(name + "_pe"), sem(name + "_act")

            def dve_at(self, i, k):
                return i * self.n_dve + (1 + k)

            def pe_at(self, i, k):
                return i * self.n_pe + (1 + k)

            def act_at(self, i, k):
                return i * self.n_act + (1 + k)

            def end(self):
                return (self.dve, self.dve_at(CHUNKS, 0))

        n_l0a = Stage("n_l0a", 2, 1, 0)
        n_l0b = Stage("n_l0b", 6, 3, 1)
        n_l1 = Stage("n_l1", 17, 6, 3)
        n_l2a = Stage("n_l2a", 3, 1, 0)
        n_l2b = Stage("n_l2b", 6, 2, 1)
        n_l3a = Stage("n_l3a", 3, 1, 0)
        n_l3b = Stage("n_l3b", 7, 3, 1)
        norm_d = sem("norm_d")
        norm_a = sem("norm_a")
        degree = sem("degree")

        N_COLS, N_XG, N_MATG, N_LIN = 6, (XBLOCKS + 3) // 4, 2, 1
        TURNS = N_COLS + N_XG + N_MATG + N_LIN

        t_l0a = Table("t_l0a", X, WT[:, :], table16, [(turn_sb, TURNS)])
        t_l0b = Table("t_l0b", H, WR[:, 0:2048], table16, [n_l0a.end(), (w2_in, 16)])
        t_gat = Table("t_gat", X, lin_cat[:, :], table_gat, [n_l0b.end()])
        t_l2 = Table("t_l2", X, MIXED, table8, [n_l1.end(), (mixed, R8 * R8)])
        t_l3a = Table("t_l3a", X, mat_t("L3_gnn_W1_l"), table1, [n_l2b.end()])
        t_l3b = Table("t_l3b", H, mat_t("L3_gnn_W2_l"), table1, [n_l3a.end()])
        count = Round("count", "count")
        r_l0a = Round("r_l0a", "weigh", idx16, t_l0a)
        r_l0b = Round("r_l0b", "weighted", idx16, t_l0b)
        r_gat = Round("r_gat", "gat", idx1, t_gat)
        r_l2 = Round("r_l2", "sum", idx8, t_l2)
        r_l3a = Round("r_l3a", "degree", idx1, t_l3a)
        r_l3b = Round("r_l3b", "sum", idx1, t_l3b)

        et_in = [sem(f"et_in{b}") for b in range(2)]
        et_hot = sem("et_hot")
        looking = sem("looking")
        look_ready = sem("look_ready")
        look_free = sem("look_free")
        rt_ready = sem("rt_ready")
        w_added = sem("w_added")

        g_in = [sem(f"g_in{b}") for b in range(2)]
        g_pe = sem("g_pe")
        g_act = sem("g_act")
        g_dve = sem("g_dve")
        G_PE, G_ACT, G_DVE = 6, 4, 21

        XFER = {DST: a["dst"], SRC: a["src"], ET16: a["edge_type_16"], ET8: a["edge_type_8"]}
        WHOLE = (ROWB - 1) * P * P
        TAIL = FULL - (ROWB - 1) * P
        N_ROWS_IN = 3 * len(XFER) + 6
        N_W_IN = 1 + len(MATS) + len(VECS) + 2 + 1
        N_PREP = 32 + 12
        ENDS = 28
        LAST_ROWS = NODES - (XBLOCKS - 1) * P

        def meta_of(engine, k, at, n):
            _, values = nc.values_load_multi_w_load_instructions(meta[0:1, bass.ds(k, 1), at:at + n].rearrange("o k m -> o (k m)"),
                                                                 engines=[engine.engine], min_val=0, max_val=NODES - 1)
            return values

        block = ctx.enter_context(nc.Block())

        @block.sync
        def _(sp):
            sp.wait_ge(cleared, 1)
            for n, v in XFER.items():
                sp.dma_start(rows_i[:, n, 0:ROWB - 1, :],
                             v[0:WHOLE].rearrange("(b t e) -> t b e", t=P, e=P)).then_inc(rows_in, 16)
                sp.dma_start(rows_i[0:TAIL, n, ROWB - 1, :],
                             v[WHOLE:FULL * P].rearrange("(t e) -> t e", e=P)).then_inc(rows_in, 16)
                sp.dma_start(rows_i[TAIL:TAIL + 1, n, ROWB - 1, 0:REST],
                             v[FULL * P:EDGES].rearrange("(t e) -> t e", t=1)).then_inc(rows_in, 16)
            dst = a["dst"]
            whole = dst[0:WHOLE].rearrange("(b t e) -> t b e", t=P, e=P)
            tail = dst[WHOLE:FULL * P].rearrange("(t e) -> t e", e=P)
            sp.dma_start(base_i[:, 0:ROWB - 1], whole[:, :, 0]).then_inc(rows_in, 16)
            sp.dma_start(base_i[0:TAIL, ROWB - 1:ROWB], tail[:, 0:1]).then_inc(rows_in, 16)
            sp.dma_start(base_i[TAIL:TAIL + 1, ROWB - 1:ROWB],
                         dst[FULL * P:FULL * P + 1].rearrange("(t e) -> t e", t=1)).then_inc(rows_in, 16)
            sp.dma_start(prev_last[1:P, 0:ROWB - 1], whole[0:P - 1, :, P - 1]).then_inc(rows_in, 16)
            sp.dma_start(prev_last[0:1, 1:ROWB], whole[P - 1:P, :, P - 1]).then_inc(rows_in, 16)
            sp.dma_start(prev_last[1:TAIL + 1, ROWB - 1:ROWB], tail[:, P - 1:P]).then_inc(rows_in, 16)
            sp.dma_start(x_rows[:, 0:XBLOCKS - 1, :],
                         a["x"][0:(XBLOCKS - 1) * P, :].rearrange("(b p) f -> p b f", p=P)).then_inc(x_in, 16)
            sp.dma_start(x_rows[0:LAST_ROWS, XBLOCKS - 1, :], a["x"][(XBLOCKS - 1) * P:NODES, :]).then_inc(x_in, 16)
            sp.wait_ge(prep, N_PREP)
            for dram, f in ((etype_row, F_ET), (penalty_row, F_PEN)):
                n = TILES + 1 - (ROWB - 1) * P
                sp.dma_start(dram[0:WHOLE].rearrange("(b t e) -> t b e", t=P, e=P),
                             rows_f[:, f, 0:ROWB - 1, :]).then_inc(scratch, 16)
                sp.dma_start(dram[WHOLE:(TILES + 1) * P].rearrange("(t e) -> t e", e=P),
                             rows_f[0:n, f, ROWB - 1, :]).then_inc(scratch, 16)
            for dram, col in ((flag_row, flag_i), (first_row, first_i)):
                sp.dma_start(dram[0:(ROWB - 1) * P].rearrange("(b t) -> t b", t=P), col[:, 0:ROWB - 1]).then_inc(meta_out, 16)
                sp.dma_start(dram[(ROWB - 1) * P:TILES].rearrange("(t o) -> t o", o=1),
                             col[0:TILES - (ROWB - 1) * P, ROWB - 1:ROWB]).then_inc(meta_out, 16)
            sp.wait_ge(meta_out, 64)
            sp.dma_start(meta[0:1, :, 0:1], flag_row.rearrange("(o k j) -> o k j", o=1, j=G)[:, :, 0:1]).then_inc(base_in, 16)
            sp.dma_start(meta[0:1, :, 1:2], first_row.rearrange("(o k j) -> o k j", o=1, j=G)[:, :, 0:1]).then_inc(base_in, 16)
            sp.dma_start(meta[0:1, :, META - G:META], first_row.rearrange("(o k j) -> o k j", o=1, j=G)).then_inc(base_in, 16)

            def store_table(t):
                wide = t.dram.shape[1] * t.rows
                with sp.Fori(0, BLOCKS // 2) as i:
                    for b in range(2):
                        blk = 2 * i + b
                        sp.wait_ge(t.out_a, blk + 3)
                        if t.part < t.width:
                            sp.wait_ge(t.out_d, blk + 3)
                        sp.dma_start(t.dram[bass.ds(blk * (P * t.rows), P * t.rows), :]
                                     .rearrange("(p r) f -> p (r f)", r=t.rows),
                                     TOUT[:, b, 0:wide]).then_inc(t.stored[b], 16)
                        if t is t_gat:
                            sp.dma_start(node_logits[bass.ds(blk * P, P), :],
                                         TOUT[:, b, GATW:GATW + 2 * HEADS]).then_inc(t.stored[b], 16)

            store_table(t_l0a)
            sp.wait_ge(t_l0a.made, 2 + BLOCKS)
            sp.dma_start(BASIS.rearrange("d (r h) -> d r h", r=R8),
                         a["L2_gnn_basis_w"].rearrange("r d h -> d r h")).then_inc(basis_in, 16)
            sp.wait_ge(scratch, 64)
            with sp.Fori(0, BATCHES // 2) as i:
                for b in range(2):
                    k = 2 * i + b
                    sp.wait_ge(r_l0a.agg_ready, k * G + G)
                    sp.dma_start(ETR[:, b, :], etype_row[bass.ds(k * (G * P), G * P)].unsqueeze(0)
                                 .to_broadcast([R16, G * P])).then_inc(et_in[b], 16)
            store_table(t_l0b)
            store_table(t_gat)
            for b in range(2):
                sp.wait_ge(t_gat.stored[b], 2 * 16 * (BLOCKS // 2))
            with sp.Fori(0, BATCHES // 2) as i:
                for b in range(2):
                    k = 2 * i + b
                    bases = meta_of(sp, k, META - G, G)
                    sp.wait_ge(r_gat.agg_ready, k * G + G)
                    for j, base in enumerate(bases):
                        sp.dma_start(AW[:, b, j, :], node_logits[bass.ds(base, P), :]).then_inc(g_in[b], 16)
                        if j == 0:
                            sp.dma_start(AD0[:, b, :], node_logits[bass.ds(base, 1), 0:HEADS].rearrange("o h -> h o"))\
                                .then_inc(g_in[b], 16)
                    sp.dma_start(PEN[:, b, :], penalty_row[bass.ds(k * (G * P), G * P + 1)].unsqueeze(0)
                                 .to_broadcast([HEADS, G * P + 1])).then_inc(g_in[b], 16)
            store_table(t_l2)
            store_table(t_l3a)
            store_table(t_l3b)
            sp.wait_ge(out_sb, N_XG)
            sp.dma_start(out[0:(XBLOCKS - 1) * P, :].rearrange("(b p) f -> p b f", p=P),
                         x_rows[:, 0:XBLOCKS - 1, :]).then_inc(out_done, 16)
            sp.dma_start(out[(XBLOCKS - 1) * P:NODES, :], x_rows[0:LAST_ROWS, XBLOCKS - 1, :]).then_inc(out_done, 16)
            sp.wait_ge(out_done, 32)

        @block.gpsimd
        def _(pool):
            pool.memset(rows_i[:, :, :, :], 0)
            pool.memset(base_i[:, :], 0)
            pool.memset(meta[:, :, :], 0)
            pool.iota(batch_first[:, :], [[G, P // G], [0, G]], base=0, channel_multiplier=0, allow_small_or_imprecise_dtypes=True)
            pool.memset(prev_last[:, :], -1)
            pool.memset(x_rows[:, XBLOCKS - 1, :], 0.0)
            pool.memset(X[:, XBLOCKS * P:NODES_P], 0.0)
            pool.iota(iota_f[:, :], [[1, P]], base=0, channel_multiplier=0, allow_small_or_imprecise_dtypes=True)
            pool.iota(pidx[:, :], [[0, 1]], base=0, channel_multiplier=1, allow_small_or_imprecise_dtypes=True)
            pool.iota(head_iota[:, :], [[HD, HEADS]], base=0, channel_multiplier=0, allow_small_or_imprecise_dtypes=True)
            pool.memset(mean_mat[:, :], 1.0 / P)
            pool.memset(ones_mat[:, :], 1.0)
            pool.memset(eps[:, :], LN_EPS)
            pool.memset(carry[:, :], -BIG).then_inc(pad_zero, 1)
            pool.wait_ge(pad_zero, 1)
            pool.memset(rows_i[:, DST, ROWB - 1, :], int(NO_NODE)).then_inc(cleared, 1)

            def stage_table(t, zero):
                for s, n in t.ready:
                    pool.wait_ge(s, n)
                for z in zero:
                    pool.memset(z, 0.0).then_inc(t.zeroed, 1)
                with pool.Fori(0, BLOCKS // 2) as i:
                    for b in range(2):
                        blk = 2 * i + b
                        pool.wait_ge(t.made, blk + 1)
                        pool.tensor_copy(STG[:, b, :], t.source[:, bass.ds(blk * P, P)]).then_inc(t.staged, 1)

            def gather(r):
                for b in range(2):
                    pool.wait_ge(r.table.stored[b], 16 * (BLOCKS // 2) * r.table.stores)
                with pool.Fori(0, BATCHES // 2) as i:
                    for b in range(2):
                        k = 2 * i + b
                        pool.wait_ge(r.idx_staged, k + 1)
                        pool.wait_ge(r.agg_ready, k * G + G)
                        pool.sem_inc(r.begun, 1)
                        for j in range(G):
                            pool.indirect_dma_start(
                                out=GB[:, b, j * r.width:(j + 1) * r.width], out_offset=None,
                                in_=r.table.dram[:, :],
                                in_offset=bass.IndirectOffsetOnAxis(ap=IDX[:, b, j:j + 1], axis=0),
                            ).then_inc(r.gathered[b], 16)

            stage_table(t_l0a, [])
            gather(r_l0a)
            stage_table(t_l0b, [sums])
            gather(r_l0b)
            stage_table(t_gat, [sums, aux[0:2 * HEADS, :]])
            gather(r_gat)
            stage_table(t_l2, [sums])
            gather(r_l2)
            stage_table(t_l3a, [sums, aux])
            gather(r_l3a)
            stage_table(t_l3b, [sums])
            gather(r_l3b)

        @block.scalar
        def _(act):
            act.sem_inc(n_l0b.act, 1)
            act.sem_inc(n_l1.act, 1)
            act.sem_inc(n_l2b.act, 1)
            act.sem_inc(n_l3b.act, 1)
            act.sem_inc(g_act, 1)
            for t in (t_l0a, t_l0b, t_gat, t_l2, t_l3a, t_l3b):
                act.sem_inc(t.out_a, 2)
            act.dma_start(WT[:, :].rearrange("d (r h) -> d r h", r=R16),
                          a["L0_gnn_W1"].rearrange("r d h -> d r h")).then_inc(w_in, 16)
            for n, name in enumerate(MATS):
                act.dma_start(mats[:, n, :], a[name]).then_inc(w_in, 16)
            for n, name in enumerate(VECS):
                act.dma_start(vecs[:, n:n + 1], a[name].rearrange("(p o) -> p o", o=1)).then_inc(w_in, 16)
            for n, name in enumerate(("L1_gnn_att_src", "L1_gnn_att_dst")):
                act.dma_start(vecs[:, len(VECS) + n:len(VECS) + n + 1],
                              a[name].rearrange("o h (k u) -> (o h k) u", u=1)).then_inc(w_in, 16)
            act.dma_start(wcomp[:, :], a["L2_gnn_w_comp"].rearrange("r b -> (r b)").unsqueeze(0)
                          .to_broadcast([P, R8 * R8])).then_inc(w_in, 16)
            act.dma_start(WR[:, 0:2048].rearrange("d (r h) -> d r h", r=R16),
                          a["L0_gnn_W2"].rearrange("r d h -> d r h")).then_inc(w2_in, 16)

            def copy_table(t):
                def one(i, b):
                    blk = 2 * i + b
                    act.wait_ge(t.made, blk + 3)
                    if not isinstance(i, int):
                        act.wait_ge(t.stored[b], i * (16 * t.stores))
                    ps = PS[:, 4 * b:4 * b + 4, :].rearrange("p a n -> p (a n)")
                    act.copy(TOUT[:, b, 0:t.part], ps[:, 0:t.part]).then_inc(t.out_a, 1)

                one(0, 0)
                one(0, 1)
                with act.Fori(1, BLOCKS // 2) as i:
                    one(i, 0)
                    one(i, 1)

            def stage_indices(r):
                with act.Fori(0, BATCHES // 2) as i:
                    for b in range(2):
                        k = 2 * i + b
                        act.wait_ge(r.agg_ready, k * G + G)
                        act.copy(IDX[:, b, :], r.idx[:, bass.ds(k * G, G)]).then_inc(r.idx_staged, 1)

            def roots(st, steps):
                with act.Fori(0, CHUNKS) as i:
                    for pe_step in steps:
                        act.wait_ge(st.pe, st.pe_at(i, pe_step))
                        act.activation(T4, PS[:, 2, 0:CHUNK], ACT.Sqrt, bias=eps[:, 0:1]).then_inc(st.act, 1)

            act.wait_ge(turn_sb, TURNS)
            copy_table(t_l0a)
            stage_indices(r_l0a)
            copy_table(t_l0b)
            stage_indices(r_l0b)
            roots(n_l0b, [3])
            copy_table(t_gat)

            with act.Fori(0, BATCHES // 2) as i:
                for b in range(2):
                    k = 2 * i + b
                    act.wait_ge(r_gat.agg_ready, k * G + G)
                    act.copy(IDX[:, b, :], r_gat.idx[:, bass.ds(k * G, G)]).then_inc(r_gat.idx_staged, 1)
                    for h in range(2):
                        act.wait_ge(g_pe, k * G_PE + (2 + h))
                        act.copy(OHT[:, 4 * h:4 * h + 4, :].rearrange("p j e -> p (j e)"), PS[:, 4 + h, :]).then_inc(g_act, 1)
                    act.wait_ge(g_dve, k * G_DVE + (1 + 10))
                    act.activation(RE[:, :], RD[:, :], ACT.Exp).then_inc(g_act, 1)
                    act.wait_ge(g_dve, k * G_DVE + (1 + 16))
                    act.activation(WE[:, :, :, :].rearrange("p j t h -> p t j h"), ZD[:, :, :, :], ACT.Exp).then_inc(g_act, 1)

            with act.Fori(0, CHUNKS) as i:
                act.wait_ge(n_l1.pe, n_l1.pe_at(i, 1))
                act.copy(T0, PS[:, 0, 0:CHUNK]).then_inc(n_l1.act, 1)
                for pe_step in (4, 6):
                    act.wait_ge(n_l1.pe, n_l1.pe_at(i, pe_step))
                    act.activation(T4, PS[:, 2, 0:CHUNK], ACT.Sqrt, bias=eps[:, 0:1]).then_inc(n_l1.act, 1)
            copy_table(t_l2)
            stage_indices(r_l2)
            act.wait_ge(norm_d, 1 + CHUNKS + 1)
            act.activation(bnv[:, 2:3], bnv[:, 1:2], ACT.Sqrt, bias=eps[:, 0:1]).then_inc(norm_a, 1)
            roots(n_l2b, [2])
            copy_table(t_l3a)
            stage_indices(r_l3a)
            copy_table(t_l3b)
            stage_indices(r_l3b)
            roots(n_l3b, [3])

        @block.tensor
        def _(pe):
            for r in (count, r_l0a, r_l0b, r_gat, r_l2, r_l3a, r_l3b):
                pe.sem_inc(r.agg_ready, TWO)
            for t in (t_l0a, t_l0b, t_gat, t_l2, t_l3a, t_l3b):
                pe.sem_inc(t.made, 2)
            for st in (n_l0a, n_l0b, n_l1, n_l2a, n_l2b, n_l3a, n_l3b):
                pe.sem_inc(st.pe, 1)
            pe.sem_inc(g_pe, 1)

            pe.wait_ge(prep, ENDS)
            nc.tensor.matmul(PS[:, 7, 0:ROWB], sel_first[:, :], ends[:, 0], start=True, stop=True)
            nc.tensor.matmul(PS[:, 7, ROWB:2 * ROWB], sel_last[:, :], ends[:, 1], start=True, stop=True).then_inc(ends_ps, 1)
            pe.wait_ge(prep, N_PREP)
            for n in range(N_COLS):
                if n >= 4:
                    pe.wait_ge(turn_sb, n - 3)
                for q in range(ROWB):
                    ins = nc.tensor.transpose(PS[:, 2 * (n % 4) + q // 4, (q % 4) * P:(q % 4 + 1) * P],
                                              rows_f[:, n, q, :], ident[:, :])
                ins.then_inc(turn_ps, 1)
            pe.wait_ge(x_in, 32)
            for n in range(N_XG):
                pe.wait_ge(turn_sb, max(n - 7, 0) + N_COLS)
                for q in range(4 * n, min(4 * n + 4, XBLOCKS)):
                    ins = nc.tensor.transpose(PS[:, n % 8, (q % 4) * P:(q % 4 + 1) * P], x_rows[:, q, :], ident[:, :])
                ins.then_inc(turn_ps, 1)
            pe.wait_ge(w_in, 16 * N_W_IN)
            pe.wait_ge(turn_sb, N_COLS + N_XG)
            for n in range(N_MATG):
                for q in range(4 * n, min(4 * n + 4, len(TURNED))):
                    ins = nc.tensor.transpose(PS[:, n, (q % 4) * P:(q % 4 + 1) * P], mat(TURNED[q]), ident[:, :])
                ins.then_inc(turn_ps, 1)
            nc.tensor.matmul(PS[:, 2, 0:P + 3 * HEADS], mat("L1_gnn_lin_w"), cat_rhs[:, :],
                             start=True, stop=True).then_inc(turn_ps, 1)

            def multiply_table(t):
                for s, n in t.ready:
                    pe.wait_ge(s, n)
                with pe.Fori(0, BLOCKS // 2) as i:
                    for b in range(2):
                        blk = 2 * i + b
                        pe.wait_ge(t.staged, blk + 1)
                        pe.wait_ge(t.out_a, blk + 1)
                        if t.part < t.width:
                            pe.wait_ge(t.out_d, blk + 1)
                        for c in range(0, t.width, 512):
                            w = min(512, t.width - c)
                            ins = nc.tensor.matmul(PS[:, 4 * b + c // 512, 0:w], STG[:, b, :], t.weights[:, c:c + w],
                                                   start=True, stop=True)
                        ins.then_inc(t.made, 1)
                pe.wait_ge(t.out_a, 2 + BLOCKS)
                if t.part < t.width:
                    pe.wait_ge(t.out_d, 2 + BLOCKS)

            def sum_tile(r, b, j, bank, first, final):
                at = dict(start=first, stop=final)
                if r.kind == "count":
                    return nc.tensor.matmul(PS[0:R16, bank, 0:P], OHR[:, b, j, :], oh16(b)[:, j, :], **at)
                rows = GB[:, b, j * r.width:j * r.width + P]
                if r.kind == "degree":
                    nc.tensor.matmul(PS[:, 2 + bank, 0:P], ones_mat[:, :], oh(b, j), **at)
                if r.kind == "gat":
                    rows = M[:, j, :]
                    nc.tensor.matmul(PS[0:2 * HEADS, 2 + bank, 0:P],
                                     WE[:, j, :, :].rearrange("p t h -> p (t h)"), oh(b, j), **at)
                return nc.tensor.matmul(PS[:, bank, 0:P], rows, oh(b, j), **at)

            def sum_tiles(r, k, b, ready, look=None):
                flag, base = meta_of(pe, k, 0, 2)
                with pe.If(flag > 0):
                    if look:
                        look([base] * G)
                    for s, n in ready:
                        pe.wait_ge(s, n)
                    pe.wait_ge(r.agg_free, k * G + G)
                    for j in range(G):
                        ins = sum_tile(r, b, j, b, j == 0, j == G - 1)
                    ins.then_inc(r.agg_ready, G)
                with pe.Else():
                    if look:
                        look(meta_of(pe, k, META - G, G))
                    for s, n in ready:
                        pe.wait_ge(s, n)
                    for j in range(G):
                        pe.wait_ge(r.agg_free, k * G + (TWO + j))
                        sum_tile(r, b, j, b, True, True).then_inc(r.agg_ready, 1)

            def sum_round(r):
                with pe.Fori(0, BATCHES // 2) as i:
                    for b in range(2):
                        k = 2 * i + b
                        ready = [(r.oh_ready, k + 1)]
                        if r.table:
                            ready.append((r.gathered[b], (i + 1) * (16 * G)))
                        sum_tiles(r, k, b, ready)

            def edges_done(r):
                return (r.agg_free, TWO + TILES)

            def node_products(st, first, first_signal, banks, later, after):
                for s, n in after:
                    pe.wait_ge(s, n)
                with pe.Fori(0, CHUNKS) as i:
                    pe.wait_ge(st.dve, st.dve_at(i, 0))
                    for n, (bank, w, v) in enumerate(first):
                        ins = nc.tensor.matmul(PS[0:w.shape[1], bank, 0:CHUNK], w, v[:, bass.ds(i * CHUNK, CHUNK)],
                                               start=True, stop=True)
                    ins.then_inc(st.pe, 1)
                    for dve_step, bank, w, v in later:
                        pe.wait_ge(st.dve, st.dve_at(i, dve_step))
                        nc.tensor.matmul(PS[:, bank, 0:CHUNK], w, v, start=True, stop=True).then_inc(st.pe, 1)

            multiply_table(t_l0a)
            pe.wait_ge(base_in, 48)
            sum_round(count)
            pe.wait_ge(rt_ready, 2)
            with pe.Fori(0, BATCHES // 2) as i:
                for b in range(2):
                    k = 2 * i + b

                    def look(bases):
                        pe.wait_ge(et_hot, k + 1)
                        for j in range(G):
                            pe.wait_ge(look_free, k * G + (j + 1))
                            pe.sem_inc(looking, 1)
                            nc.tensor.matmul(PS[:, 4 + j % LOOKS, 0:P], ETR[:, b, j * P:(j + 1) * P],
                                             aux[0:R16, bass.ds(bases[j], P)], start=True, stop=True).then_inc(look_ready, 1)

                    sum_tiles(r_l0a, k, b, [(look_free, k * G + (LOOKS + G)), (r_l0a.gathered[b], (i + 1) * (16 * G))], look)
            node_products(n_l0a, [(0, mat("L0_gnn_root1"), X)], 1, None, [], [edges_done(r_l0a)])
            multiply_table(t_l0b)
            sum_round(r_l0b)
            node_products(n_l0b, [(0, mat("L0_gnn_root2"), H)], 1, None,
                          [(2, 1, mean_mat[:, :], T1), (4, 2, mean_mat[:, :], T3)], [edges_done(r_l0b)])
            multiply_table(t_gat)
            with pe.Fori(0, BATCHES // 2) as i:
                for b in range(2):
                    k = 2 * i + b
                    r = r_gat
                    pe.wait_ge(r.oh_ready, k + 1)
                    for h in range(2):
                        for j in range(4):
                            ins = nc.tensor.transpose(PS[:, 4 + h, j * P:(j + 1) * P], oh(b, 4 * h + j), ident[:, :])
                        ins.then_inc(g_pe, 1)
                    pe.wait_ge(g_act, k * G_ACT + (1 + 2))
                    pe.wait_ge(g_in[b], (i + 1) * (16 * (G + 2)))
                    for j in range(G):
                        ins = nc.tensor.matmul(PS[:, 6, j * 2 * HEADS:(j + 1) * 2 * HEADS], OHT[:, j, :], AW[:, b, j, :],
                                               start=True, stop=True)
                    ins.then_inc(g_pe, 1)
                    pe.wait_ge(g_dve, k * G_DVE + (1 + 2))
                    for j in range(G):
                        ins = nc.tensor.transpose(PS[0:HEADS, 4 + j // 4, (j % 4) * P:(j % 4 + 1) * P], XS[:, j, :],
                                                  ident[:, :])
                    ins.then_inc(g_pe, 1)
                    pe.wait_ge(g_dve, k * G_DVE + (1 + 4))
                    for j in range(G):
                        ins = nc.tensor.matmul(PS[:, 6, P + j * HEADS:P + (j + 1) * HEADS], BS[:, j * P:(j + 1) * P],
                                               ident[0:HEADS, 0:HEADS], start=True, stop=True)
                    ins.then_inc(g_pe, 1)
                    pe.wait_ge(g_act, k * G_ACT + (1 + 3))
                    nc.tensor.matmul(PS[:, 7, 64:65], expand[:, 0:P], RE[:, :], start=True, stop=True)
                    nc.tensor.matmul(PS[0:2 * HEADS, 7, 66:67], expand[:, P:P + 2 * HEADS], RE[:, :],
                                     start=True, stop=True).then_inc(g_pe, 1)
                    sum_tiles(r, k, b, [(g_dve, k * G_DVE + (1 + 18))])
            node_products(n_l1, [(0, lin_cat[:, 0:P], X), (1, den_mat[:, :], aux[0:2 * HEADS, :]),
                                 (3, own_mat[:, :], aux[0:2 * HEADS, :])], 1, None,
                          [(6, 4, mat_t("L1_gnn_proj_w"), T3), (7, 5, mean_mat[:, :], T1), (9, 2, mean_mat[:, :], T3),
                           (13, 5, mean_mat[:, :], T1), (15, 2, mean_mat[:, :], T3)], [edges_done(r_gat)])
            multiply_table(t_l2)
            sum_round(r_l2)
            node_products(n_l2a, [(0, mat("L2_gnn_loop_w"), X), (1, mat("L2_gnn_res_w"), X)], 1, None, [],
                          [edges_done(r_l2)])
            with pe.Fori(0, CHUNKS) as i:
                for dve_step, bank, v in ((2, 1, T1), (4, 2, T3)):
                    pe.wait_ge(n_l2b.dve, n_l2b.dve_at(i, dve_step))
                    nc.tensor.matmul(PS[:, bank, 0:CHUNK], mean_mat[:, :], v, start=True, stop=True).then_inc(n_l2b.pe, 1)
            multiply_table(t_l3a)
            sum_round(r_l3a)
            node_products(n_l3a, [(0, mat_t("L3_gnn_W1_r"), X)], 1, None, [], [edges_done(r_l3a)])
            multiply_table(t_l3b)
            sum_round(r_l3b)
            node_products(n_l3b, [(0, mat_t("L3_gnn_W2_r"), H)], 1, None,
                          [(3, 1, mean_mat[:, :], T1), (5, 2, mean_mat[:, :], T3)], [edges_done(r_l3b)])
            pe.wait_ge(*n_l3b.end())
            for n in range(N_XG):
                if n >= 8:
                    pe.wait_ge(out_sb, n - 7)
                for q in range(4 * n, min(4 * n + 4, XBLOCKS)):
                    ins = nc.tensor.transpose(PS[:, n % 8, (q % 4) * P:(q % 4 + 1) * P], X[:, q * P:(q + 1) * P], ident[:, :])
                ins.then_inc(out_ps, 1)

        @block.vector
        def _(dve):
            for r in (count, r_l0a, r_l0b, r_gat, r_l2, r_l3a, r_l3b):
                dve.sem_inc(r.agg_free, TWO)
            for t in (t_l0a, t_l0b, t_gat, t_l2, t_l3a, t_l3b):
                dve.sem_inc(t.out_d, 2)
            for st in (n_l0a, n_l0b, n_l1, n_l2a, n_l2b, n_l3a, n_l3b):
                dve.sem_inc(st.dve, 1)
            dve.sem_inc(look_free, LOOKS)
            dve.sem_inc(g_dve, 1)
            dve.sem_inc(norm_d, 1)

            preps = [0]

            def link(ins):
                preps[0] += 1
                ins.then_inc(prep, 1)
                dve.wait_ge(prep, preps[0])

            dve.wait_ge(cleared, 1)
            link(dve.tensor_scalar(ident[:, :], iota_f[:, :], pidx[:, 0:1], None, ALU.is_equal))
            link(dve.tensor_scalar(below[:, 0:HEADS], head_iota[:, :], pidx[:, 0:1], 0.0, ALU.subtract, ALU.is_le))
            link(dve.tensor_scalar(hsel[:, :], head_iota[:, :], pidx[:, 0:1], -float(HD), ALU.subtract, ALU.is_gt))
            link(dve.tensor_tensor(hsel[:, :], hsel[:, :], below[:, 0:HEADS], ALU.mult))
            link(dve.tensor_scalar(shift[:, 0:1], pidx[:, 0:1], float(HD), None, ALU.mult))
            link(dve.tensor_scalar(shift[:, 1:2], pidx[:, 0:1], float(HD), -float(HD * HEADS), ALU.mult, ALU.add))
            link(dve.tensor_scalar(shift[:, 2:3], pidx[:, 0:1], float(HEADS), None, ALU.add))
            for m, rows, s in ((expand[:, 0:P], HEADS, 0), (own_mat[:, :], 2 * HEADS, 1), (den_mat[:, :], 2 * HEADS, 0)):
                link(dve.tensor_scalar(below[0:rows, :], iota_f[0:rows, :], shift[0:rows, s:s + 1], 0.0, ALU.subtract, ALU.is_ge))
                link(dve.tensor_scalar(m, iota_f[0:rows, :], shift[0:rows, s:s + 1], float(HD), ALU.subtract, ALU.is_lt))
                link(dve.tensor_tensor(m, m, below[0:rows, :], ALU.mult))
            link(dve.tensor_tensor(den_mat[:, :], den_mat[:, :], own_mat[:, :], ALU.add))
            link(dve.tensor_scalar(expand[:, P:P + 2 * HEADS], iota_f[0:HEADS, 0:2 * HEADS], pidx[0:HEADS, 0:1], None, ALU.is_equal))
            link(dve.tensor_scalar(below[0:HEADS, 0:2 * HEADS], iota_f[0:HEADS, 0:2 * HEADS], shift[0:HEADS, 2:3], None, ALU.is_equal))
            link(dve.tensor_tensor(expand[:, P:P + 2 * HEADS], expand[:, P:P + 2 * HEADS], below[0:HEADS, 0:2 * HEADS], ALU.add))
            dve.wait_ge(w_in, 16 * N_W_IN)
            link(dve.tensor_copy(cat_rhs[:, 0:P], ident[:, :]))
            for n, att in enumerate((att_src, att_dst, att_src)):
                link(dve.tensor_scalar(cat_rhs[:, P + n * HEADS:P + (n + 1) * HEADS], hsel[:, :], att, None, ALU.mult))
            link(dve.tensor_scalar(sel_first[:, :], batch_first[:, :], pidx[:, 0:1], None, ALU.is_equal))
            link(dve.tensor_scalar(sel_last[:, :], batch_first[:, :], float(G - 1), pidx[:, 0:1], ALU.add, ALU.is_equal))
            dve.wait_ge(rows_in, 16 * N_ROWS_IN)
            link(dve.tensor_copy(ends[:, 0], base_i[:, :]))
            link(dve.tensor_copy(ends[:, 1], rows_i[:, DST, :, P - 1]))
            assert preps[0] == ENDS, preps
            dve.wait_ge(ends_ps, 1)
            link(dve.tensor_copy(bends[:, :, :].rearrange("p a b -> p (a b)"), PS[:, 7, 0:2 * ROWB]))
            link(dve.tensor_tensor(spans[:, 0], bends[:, 1], bends[:, 0], ALU.subtract))
            link(dve.tensor_scalar(spans[:, 1], spans[:, 0], float(P), None, ALU.is_lt))
            link(dve.tensor_tensor(spans[:, 0], bends[:, 0], ends[:, 0], ALU.subtract))
            link(dve.tensor_tensor(spans[:, 0], spans[:, 0], spans[:, 1], ALU.mult))
            link(dve.tensor_tensor(spans[:, 2], spans[:, 0], ends[:, 0], ALU.add))
            link(dve.tensor_copy(flag_i[:, :], spans[:, 1]))
            link(dve.tensor_copy(first_i[:, :], spans[:, 2]))
            link(dve.tensor_tensor(rows_f[:, F_LOCAL], rows_i[:, DST], last(first_i[:, :], P), ALU.subtract))
            for f, v, types in ((F_IDX16, R16, ET16), (F_IDX8, R8, ET8)):
                link(dve.scalar_tensor_tensor(rows_f[:, f], rows_i[:, SRC], float(v), rows_i[:, types], ALU.mult, ALU.add))
            link(dve.tensor_copy(rows_f[:, F_SRC], rows_i[:, SRC]))
            link(dve.tensor_copy(rows_f[:, F_ET], rows_i[:, ET16]))
            link(dve.tensor_tensor(rows_f[:, F_START, :, 1:P], rows_i[:, DST, :, 1:P], rows_i[:, DST, :, 0:P - 1], ALU.not_equal))
            link(dve.tensor_tensor(rows_f[:, F_START, :, 0], rows_i[:, DST, :, 0], prev_last[:, :], ALU.not_equal))
            link(dve.tensor_scalar(rows_f[:, F_PEN], rows_f[:, F_START], -BIG, None, ALU.mult))
            assert preps[0] == N_PREP, preps

            cols = (local, idx16, idx8, idx1, etype, start)
            for n, col in enumerate(cols):
                dve.wait_ge(turn_ps, n + 1)
                ps = PS[:, 2 * (n % 4):2 * (n % 4) + 2, :].rearrange("p a n -> p (a n)")
                dve.tensor_copy(col[:, :], ps[:, 0:ROWB * P]).then_inc(turn_sb, 1)
            for n in range(N_XG):
                dve.wait_ge(turn_ps, N_COLS + n + 1)
                w = min(512, XBLOCKS * P - 512 * n)
                dve.tensor_copy(X[:, 512 * n:512 * n + w], PS[:, n % 8, 0:w]).then_inc(turn_sb, 1)
            for n in range(N_MATG):
                dve.wait_ge(turn_ps, N_COLS + N_XG + n + 1)
                m = min(4, len(TURNED) - 4 * n)
                dve.tensor_copy(turned[:, 4 * n:4 * n + m, :].rearrange("p q n -> p (q n)"), PS[:, n, 0:m * P])\
                    .then_inc(turn_sb, 1)
            dve.wait_ge(turn_ps, TURNS)
            dve.tensor_copy(lin_cat[:, :], PS[:, 2, 0:P + 3 * HEADS]).then_inc(turn_sb, 1)

            def copy_table(t):
                if t.part == t.width:
                    return

                def one(i, b):
                    blk = 2 * i + b
                    dve.wait_ge(t.made, blk + 3)
                    if not isinstance(i, int):
                        dve.wait_ge(t.stored[b], i * (16 * t.stores))
                    ps = PS[:, 4 * b:4 * b + 4, :].rearrange("p a n -> p (a n)")
                    dve.tensor_copy(TOUT[:, b, t.part:t.width], ps[:, t.part:t.width]).then_inc(t.out_d, 1)

                one(0, 0)
                one(0, 1)
                with dve.Fori(1, BLOCKS // 2) as i:
                    one(i, 0)
                    one(i, 1)

            def add_window(r, base, bank):
                if r.kind == "count":
                    dst = aux[0:R16, bass.ds(base, P)]
                    return dve.tensor_tensor(dst, dst, PS[0:R16, bank, 0:P], ALU.add)
                if r.kind == "degree":
                    dst = aux[:, bass.ds(base, P)]
                    dve.tensor_tensor(dst, dst, PS[:, 2 + bank, 0:P], ALU.add)
                if r.kind == "gat":
                    dst = aux[0:2 * HEADS, bass.ds(base, P)]
                    dve.tensor_tensor(dst, dst, PS[0:2 * HEADS, 2 + bank, 0:P], ALU.add)
                dst = sums[:, bass.ds(base, P)]
                return dve.tensor_tensor(dst, dst, PS[:, bank, 0:P], ALU.add)

            def add_tiles(r, k, b, ready=(), meta_k=None):
                flag, base = meta_k or meta_of(dve, k, 0, 2)
                with dve.If(flag > 0):
                    for s, v in ready:
                        dve.wait_ge(s, v)
                    dve.wait_ge(r.agg_ready, k * G + (TWO + G))
                    dve.wait_ge(r.agg_free, k * G + TWO)
                    add_window(r, base, b).then_inc(r.agg_free, G)
                with dve.Else():
                    bases = meta_of(dve, k, META - G, G)
                    for s, v in ready:
                        dve.wait_ge(s, v)
                    for j in range(G):
                        dve.wait_ge(r.agg_ready, k * G + (TWO + j + 1))
                        dve.wait_ge(r.agg_free, k * G + (TWO + j))
                        add_window(r, bases[j], b).then_inc(r.agg_free, 1)

            def one_hot(r, k, b):
                dve.wait_ge(r.agg_ready, k * G + G)
                dve.tensor_tensor(OH[:, b, :].rearrange("p (j d) -> p j d", j=G), mid(iota_f[:, :], G),
                                  last(local[:, bass.ds(k * G, G)], P), ALU.is_equal).then_inc(r.oh_ready, 1)

            def sum_round(r):
                with dve.Fori(0, BATCHES // 2) as i:
                    for b in range(2):
                        k = 2 * i + b
                        one_hot(r, k, b)
                        add_tiles(r, k, b)

            def layer_norm(st, i, d, p, s):
                dve.wait_ge(st.pe, st.pe_at(i, p + 1))
                dve.tensor_tensor(T2, T1, PS[:, 5 if st is n_l1 else 1, 0:CHUNK], ALU.subtract).then_inc(st.dve, 1)
                dve.wait_ge(st.dve, st.dve_at(i, d + 1))
                dve.tensor_tensor(T3, T2, T2, ALU.mult).then_inc(st.dve, 1)
                dve.wait_ge(st.act, st.act_at(i, s + 1))
                dve.reciprocal(T5, T4).then_inc(st.dve, 1)
                dve.wait_ge(st.dve, st.dve_at(i, d + 3))
                return dve.tensor_tensor

            dve.wait_ge(scratch, 64)
            dve.wait_ge(base_in, 48)
            dve.memset(sums, 0.0)
            dve.memset(aux[0:R16, :], 0.0)
            copy_table(t_l0a)
            with dve.Fori(0, BATCHES // 2) as i:
                for b in range(2):
                    k = 2 * i + b
                    dve.wait_ge(count.agg_ready, k * G + G)
                    dve.tensor_tensor(oh16(b), mid(iota_f[:, :], G), last(local[:, bass.ds(k * G, G)], P), ALU.is_equal)
                    dve.tensor_tensor(OHR[:, b, :, :], mid(iota_f[:, 0:R16], G), last(etype[:, bass.ds(k * G, G)], R16),
                                      ALU.is_equal).then_inc(count.oh_ready, 1)
                    add_tiles(count, k, b)
            dve.wait_ge(count.agg_free, TWO + TILES)
            dve.tensor_scalar(aux[0:R16, :], aux[0:R16, :], 1.0, None, ALU.max).then_inc(rt_ready, 1)
            dve.wait_ge(rt_ready, 1)
            dve.reciprocal(aux[0:R16, :], aux[0:R16, :]).then_inc(rt_ready, 1)
            with dve.Fori(0, BATCHES // 2) as i:
                for b in range(2):
                    k = 2 * i + b
                    dve.wait_ge(et_in[b], (i + 1) * 16)
                    dve.tensor_scalar(ETR[:, b, :], ETR[:, b, :], pidx[0:R16, 0:1], None, ALU.is_equal).then_inc(et_hot, 1)
                    dve.wait_ge(r_l0a.agg_ready, k * G + G)
                    for j in range(G):
                        n = k * G + j
                        dve.wait_ge(look_ready, n + 1)
                        dve.scalar_tensor_tensor(oh(b, j), iota_f[:, :], local[:, bass.ds(n, 1)], PS[:, 4 + j % LOOKS, 0:P],
                                                 ALU.is_equal, ALU.mult, accum_out=wstage[:, b, j:j + 1]).then_inc(look_free, 1)
                    dve.wait_ge(look_free, k * G + (LOOKS + G))
                    dve.tensor_copy(wcol[:, bass.ds(k * G, G)], wstage[:, b, :]).then_inc(w_added, 1)
                    add_tiles(r_l0a, k, b)
            with dve.Fori(0, CHUNKS) as i:
                st, cs = n_l0a, bass.ds(i * CHUNK, CHUNK)
                dve.wait_ge(st.pe, st.pe_at(i, 1))
                dve.scalar_tensor_tensor(T0, PS[:, 0, 0:CHUNK], vec("L0_gnn_b1"), sums[:, cs], ALU.add, ALU.add).then_inc(st.dve, 1)
                dve.wait_ge(st.dve, st.dve_at(i, 1))
                dve.tensor_scalar(H[:, cs], T0, 0.0, None, ALU.max).then_inc(st.dve, 1)
            copy_table(t_l0b)
            dve.wait_ge(t_l0b.zeroed, 1)
            dve.wait_ge(w_added, BATCHES)
            with dve.Fori(0, BATCHES // 2) as i:
                for b in range(2):
                    k = 2 * i + b
                    dve.wait_ge(r_l0b.agg_ready, k * G + G)
                    for j in range(G):
                        n = k * G + j
                        ins = dve.tensor_scalar(oh(b, j), iota_f[:, :], local[:, bass.ds(n, 1)], wcol[:, bass.ds(n, 1)],
                                                ALU.is_equal, ALU.mult)
                    ins.then_inc(r_l0b.oh_ready, 1)
                    add_tiles(r_l0b, k, b)
            with dve.Fori(0, CHUNKS) as i:
                st, cs = n_l0b, bass.ds(i * CHUNK, CHUNK)
                dve.wait_ge(st.pe, st.pe_at(i, 1))
                dve.scalar_tensor_tensor(T0, PS[:, 0, 0:CHUNK], vec("L0_gnn_b2"), sums[:, cs], ALU.add, ALU.add).then_inc(st.dve, 1)
                dve.wait_ge(st.dve, st.dve_at(i, 1))
                dve.tensor_tensor(T1, T0, X[:, cs], ALU.add).then_inc(st.dve, 1)
                layer_norm(st, i, 2, 1, 0)
                dve.tensor_tensor(X[:, cs], T2, T5, ALU.mult).then_inc(st.dve, 1)
            copy_table(t_gat)
            dve.wait_ge(t_gat.zeroed, 2)

            for b in range(2):
                dve.wait_ge(t_gat.stored[b], 2 * 16 * (BLOCKS // 2))
            with dve.Fori(0, BATCHES // 2) as i:
                for b in range(2):
                    k = 2 * i + b
                    r = r_gat

                    def own(step):
                        dve.wait_ge(g_dve, k * G_DVE + (1 + step))

                    rows = GB[:, b, :].rearrange("p (j w) -> p j w", w=GATW)
                    s_logit = rows[:, :, P:GATW]
                    one_hot(r, k, b)
                    dve.wait_ge(g_pe, k * G_PE + (1 + 3))
                    dve.tensor_copy(AD[:, :, :].rearrange("p j h -> p (j h)"), PS[:, 6, 0:G * 2 * HEADS]).then_inc(g_dve, 1)
                    own(1)
                    dve.wait_ge(r.gathered[b], (i + 1) * (16 * G))
                    dve.tensor_tensor(XS[:, :, :], s_logit, AD[:, :, HEADS:2 * HEADS], ALU.max).then_inc(g_dve, 1)
                    dve.wait_ge(g_pe, k * G_PE + (1 + 4))
                    dve.wait_ge(g_in[b], (i + 1) * (16 * (G + 2)))
                    dve.tensor_tensor_scan(FS[:, :], PEN[:, b, 0:G * P], PS[0:HEADS, 4:6, :].rearrange("p a n -> p (a n)"),
                                           carry[:, 0:1], ALU.add, ALU.max).then_inc(g_dve, 1)
                    own(3)
                    dve.tensor_tensor_scan(BS[:, ::-1], PEN[:, b, 1:G * P + 1][:, ::-1], FS[:, ::-1], -BIG,
                                           ALU.add, ALU.max).then_inc(g_dve, 1)
                    own(4)
                    dve.tensor_tensor(RZ[:, 0:1], carry[:, :], BS[:, 0:1], ALU.min).then_inc(g_dve, 1)
                    dve.tensor_copy(RZ[:, 1:2], BS[:, 0:1]).then_inc(g_dve, 1)
                    own(6)
                    dve.tensor_copy(carry[:, :], FS[:, G * P - 1:G * P]).then_inc(g_dve, 1)
                    dve.tensor_scalar(RZ[:, :], RZ[:, :], AD0[:, b, :], None, ALU.add).then_inc(g_dve, 1)
                    own(8)
                    dve.scalar_tensor_tensor(RL[:, :], RZ[:, :], SLOPE, RZ[:, :], ALU.mult, ALU.max).then_inc(g_dve, 1)
                    own(9)
                    dve.tensor_tensor(RD[:, :], RL[:, 0:1], RL[:, 1:2], ALU.subtract).then_inc(g_dve, 1)
                    t_logit = AD[:, :, 0:HEADS]
                    dve.tensor_tensor(ZL[:, 0], s_logit, t_logit, ALU.add).then_inc(g_dve, 1)
                    dve.tensor_tensor(ZL[:, 1], AD[:, :, HEADS:2 * HEADS], t_logit, ALU.add).then_inc(g_dve, 1)
                    dve.wait_ge(g_pe, k * G_PE + (1 + 5))
                    dve.tensor_tensor(ZL[:, 2], PS[:, 6, P:P + G * HEADS].rearrange("p (j h) -> p j h", h=HEADS), t_logit,
                                      ALU.add).then_inc(g_dve, 1)
                    own(13)
                    z = ZL[:, :, :, :].rearrange("p t j h -> p (t j h)")
                    dve.scalar_tensor_tensor(z, z, SLOPE, z, ALU.mult, ALU.max).then_inc(g_dve, 1)
                    own(14)
                    for t in range(2):
                        dve.tensor_tensor(ZD[:, t], ZL[:, t], ZL[:, 2], ALU.subtract).then_inc(g_dve, 1)
                    dve.wait_ge(g_act, k * G_ACT + (1 + 4))
                    dve.tensor_tensor(WE[:, :, 1, :], WE[:, :, 1, :], last(start[:, bass.ds(k * G, G)], HEADS), ALU.mult)\
                        .then_inc(g_dve, 1)
                    dve.tensor_tensor(M.rearrange("p j (h c) -> p j h c", c=HD),
                                      rows[:, :, 0:P].rearrange("p j (h c) -> p j h c", c=HD),
                                      WE[:, :, 0, :].unsqueeze(3).to_broadcast([P, G, HEADS, HD]), ALU.mult).then_inc(g_dve, 1)
                    meta_k = meta_of(dve, k, 0, 2)
                    base = meta_k[1]
                    dve.wait_ge(g_pe, k * G_PE + (1 + 6))
                    dve.wait_ge(r.agg_free, k * G + TWO)
                    dve.tensor_copy(RS[:, 0:2], PS[:, 7, 64:68:2]).then_inc(g_dve, 1)
                    own(19)
                    dve.tensor_scalar(sums[:, bass.ds(base, 1)], sums[:, bass.ds(base, 1)], RS[:, 0:1], None, ALU.mult)\
                        .then_inc(g_dve, 1)
                    dve.tensor_scalar(aux[0:2 * HEADS, bass.ds(base, 1)], aux[0:2 * HEADS, bass.ds(base, 1)],
                                      RS[0:2 * HEADS, 1:2], None, ALU.mult).then_inc(g_dve, 1)
                    add_tiles(r, k, b, [(g_dve, k * G_DVE + (1 + 21))], meta_k)

            with dve.Fori(0, CHUNKS) as i:
                st, cs = n_l1, bass.ds(i * CHUNK, CHUNK)
                dve.wait_ge(st.pe, st.pe_at(i, 1))
                dve.wait_ge(st.act, st.act_at(i, 1))
                dve.tensor_tensor(T1, PS[:, 3, 0:CHUNK], T0, ALU.mult).then_inc(st.dve, 1)
                dve.tensor_scalar(T3, PS[:, 1, 0:CHUNK], 1e-30, None, ALU.max).then_inc(st.dve, 1)
                dve.wait_ge(st.dve, st.dve_at(i, 2))
                dve.tensor_tensor(T2, T1, sums[:, cs], ALU.add).then_inc(st.dve, 1)
                dve.reciprocal(T5, T3).then_inc(st.dve, 1)
                dve.wait_ge(st.dve, st.dve_at(i, 4))
                dve.tensor_tensor(T1, T2, T5, ALU.mult).then_inc(st.dve, 1)
                dve.wait_ge(st.dve, st.dve_at(i, 5))
                dve.tensor_scalar(T3, T1, vec("L1_gnn_gat_bias"), None, ALU.add).then_inc(st.dve, 1)
                dve.wait_ge(st.pe, st.pe_at(i, 2))
                dve.tensor_scalar(T1, PS[:, 4, 0:CHUNK], vec("L1_gnn_proj_b"), None, ALU.add).then_inc(st.dve, 1)
                layer_norm(st, i, 7, 2, 1)
                dve.tensor_tensor(T0, T2, T5, ALU.mult).then_inc(st.dve, 1)
                dve.wait_ge(st.dve, st.dve_at(i, 11))
                dve.tensor_scalar(T2, T0, vec("L1_gnn_ln_gamma"), vec("L1_gnn_ln_beta"), ALU.mult, ALU.add).then_inc(st.dve, 1)
                dve.wait_ge(st.dve, st.dve_at(i, 12))
                dve.tensor_tensor(T1, T2, X[:, cs], ALU.add).then_inc(st.dve, 1)
                layer_norm(st, i, 13, 4, 2)
                dve.tensor_tensor(X[:, cs], T2, T5, ALU.mult).then_inc(st.dve, 1)

            dve.wait_ge(basis_in, 16)
            for q in range(R8):
                for r in range(R8):
                    w = wcomp[:, r * R8 + q:r * R8 + q + 1]
                    to, of = MIXED[:, r * P:(r + 1) * P], BASIS[:, q * P:(q + 1) * P]
                    if q == 0:
                        dve.tensor_scalar(to, of, w, None, ALU.mult).then_inc(mixed, 1)
                    else:
                        dve.wait_ge(mixed, (q - 1) * R8 + r + 1)
                        dve.scalar_tensor_tensor(to, of, w, to, ALU.mult, ALU.add).then_inc(mixed, 1)
            copy_table(t_l2)
            dve.wait_ge(t_l2.zeroed, 1)
            sum_round(r_l2)
            with dve.Fori(0, CHUNKS) as i:
                st, cs = n_l2a, bass.ds(i * CHUNK, CHUNK)
                dve.wait_ge(st.pe, st.pe_at(i, 1))
                dve.scalar_tensor_tensor(T0, PS[:, 0, 0:CHUNK], vec("L2_gnn_bias"), sums[:, cs], ALU.add, ALU.add).then_inc(st.dve, 1)
                dve.tensor_scalar(T1, PS[:, 1, 0:CHUNK], vec("L2_gnn_res_b"), 0.0, ALU.add, ALU.max).then_inc(st.dve, 1)
                dve.wait_ge(st.dve, st.dve_at(i, 2))
                dve.scalar_tensor_tensor(H[:, cs], T0, 0.0, T1, ALU.max, ALU.add).then_inc(st.dve, 1)
            dve.wait_ge(*n_l2a.end())
            for c in range(CHUNKS):
                w = min(CHUNK, NODES - c * CHUNK)
                dve.bn_stats(bn[:, c, :], H[:, c * CHUNK:c * CHUNK + w]).then_inc(norm_d, 1)
            dve.wait_ge(norm_d, 1 + CHUNKS)
            dve.bn_aggr(bnv[:, 0:2], bn[:, :, :].rearrange("p c s -> p (c s)")).then_inc(norm_d, 1)
            dve.wait_ge(norm_a, 1)
            dve.reciprocal(bnv[:, 3:4], bnv[:, 2:3]).then_inc(norm_d, 1)
            dve.wait_ge(norm_d, CHUNKS + 3)
            dve.tensor_tensor(bnv[:, 4:5], bnv[:, 3:4], vec("L2_gnn_bn_gamma"), ALU.mult).then_inc(norm_d, 1)
            dve.wait_ge(norm_d, CHUNKS + 4)
            dve.tensor_tensor(bnv[:, 5:6], bnv[:, 0:1], bnv[:, 4:5], ALU.mult).then_inc(norm_d, 1)
            dve.wait_ge(norm_d, CHUNKS + 5)
            dve.tensor_tensor(bnv[:, 6:7], vec("L2_gnn_bn_beta"), bnv[:, 5:6], ALU.subtract).then_inc(norm_d, 1)
            dve.wait_ge(norm_d, CHUNKS + 6)
            with dve.Fori(0, CHUNKS) as i:
                st, cs = n_l2b, bass.ds(i * CHUNK, CHUNK)
                dve.scalar_tensor_tensor(T0, H[:, cs], bnv[:, 4:5], X[:, cs], ALU.mult, ALU.add).then_inc(st.dve, 1)
                dve.wait_ge(st.dve, st.dve_at(i, 1))
                dve.tensor_scalar(T1, T0, bnv[:, 6:7], None, ALU.add).then_inc(st.dve, 1)
                layer_norm(st, i, 2, 0, 0)
                dve.tensor_tensor(X[:, cs], T2, T5, ALU.mult).then_inc(st.dve, 1)
            copy_table(t_l3a)
            dve.wait_ge(t_l3a.zeroed, 2)
            sum_round(r_l3a)
            dve.wait_ge(r_l3a.agg_free, TWO + TILES)
            dve.tensor_scalar(aux, aux, 1.0, None, ALU.max).then_inc(degree, 1)
            dve.wait_ge(degree, 1)
            dve.reciprocal(aux, aux).then_inc(degree, 1)
            dve.wait_ge(degree, 2)
            with dve.Fori(0, CHUNKS) as i:
                st, cs = n_l3a, bass.ds(i * CHUNK, CHUNK)
                dve.wait_ge(st.pe, st.pe_at(i, 1))
                dve.tensor_tensor(T0, sums[:, cs], aux[:, cs], ALU.mult).then_inc(st.dve, 1)
                dve.wait_ge(st.dve, st.dve_at(i, 1))
                dve.scalar_tensor_tensor(T1, PS[:, 0, 0:CHUNK], vec("L3_gnn_b1"), T0, ALU.add, ALU.add).then_inc(st.dve, 1)
                dve.wait_ge(st.dve, st.dve_at(i, 2))
                dve.tensor_scalar(H[:, cs], T1, 0.0, None, ALU.max).then_inc(st.dve, 1)
            copy_table(t_l3b)
            dve.wait_ge(t_l3b.zeroed, 1)
            sum_round(r_l3b)
            dve.wait_ge(r_l3b.agg_free, TWO + TILES)
            with dve.Fori(0, CHUNKS) as i:
                st, cs = n_l3b, bass.ds(i * CHUNK, CHUNK)
                dve.wait_ge(st.pe, st.pe_at(i, 1))
                dve.tensor_tensor(T0, sums[:, cs], aux[:, cs], ALU.mult).then_inc(st.dve, 1)
                dve.wait_ge(st.dve, st.dve_at(i, 1))
                dve.scalar_tensor_tensor(T2, PS[:, 0, 0:CHUNK], vec("L3_gnn_b2"), T0, ALU.add, ALU.add).then_inc(st.dve, 1)
                dve.wait_ge(st.dve, st.dve_at(i, 2))
                dve.tensor_tensor(T1, T2, X[:, cs], ALU.add).then_inc(st.dve, 1)
                layer_norm(st, i, 3, 1, 0)
                dve.tensor_tensor(X[:, cs], T2, T5, ALU.mult).then_inc(st.dve, 1)
            for n in range(N_XG):
                dve.wait_ge(out_ps, n + 1)
                w = min(512, XBLOCKS * P - 512 * n)
                dve.tensor_copy(H[:, 512 * n:512 * n + w], PS[:, n % 8, 0:w]).then_inc(out_sb, 1)


def kernel(**inputs):
    import numpy as _np
    import concourse.bacc as _bacc
    from concourse.bass_utils import run_bass_kernel_spmd as _run

    nc = _bacc.Bacc("TRN2", target_bir_lowering=False, num_devices=1)
    arrays, aps = {}, {}
    for name, value in inputs.items():
        v = _np.ascontiguousarray(value)
        arrays["in_" + name] = v
        aps[name] = nc.dram_tensor("in_" + name, v.shape, mybir.dt.from_np(v.dtype), kind="ExternalInput").ap()
    out = nc.dram_tensor("out_x", (NODES, P), FP32, kind="ExternalOutput").ap()
    build(nc, aps, out)
    r = _run(nc, [arrays], core_ids=[0])
    return r.results[0]["out_x"]
```

```python
import concourse.bass as bass
from concourse import mybir
from contextlib import ExitStack

FP32 = mybir.dt.float32
BF16 = mybir.dt.bfloat16
INT32 = mybir.dt.int32
ALU = mybir.AluOpType
ACT = mybir.ActivationFunctionType

P = 128
NODES = 6250
EDGES = 106250
R16, R8 = 16, 8
HEADS = 8
HD = P // HEADS
NODES_P = 6400
BLOCKS = NODES_P // P
CHUNK = 400
CHUNKS = NODES_P // CHUNK
META = 12
G = 8
TILES = 832
BATCHES = TILES // G
ROWB = 7
FULL = EDGES // P
REST = EDGES - FULL * P
XBLOCKS = (NODES + P - 1) // P
NO_NODE = float(1 << 20)
BIG = 1e30
GATW = P + HEADS
LN_EPS = 1e-5
SLOPE = 0.2


def mid(ap, n):
    return ap.unsqueeze(1).to_broadcast([ap.shape[0], n, ap.shape[1]])


def last(ap, n):
    return ap.unsqueeze(2).to_broadcast([ap.shape[0], ap.shape[1], n])


def build(nc, a, out):
    ctx = ExitStack()
    with ctx:
        ctx.enter_context(nc.allow_non_contiguous_dma(reason="columns of indices and of biases, once"))

        def sb(name, shape, dt=FP32):
            return ctx.enter_context(nc.sbuf_tensor(name, shape, dt))

        def sem(name):
            return ctx.enter_context(nc.semaphore(name))

        table16 = nc.dram_tensor("table16", [NODES_P * R16, P], FP32, kind="Internal").ap()
        table8 = nc.dram_tensor("table8", [NODES_P * R8, P], FP32, kind="Internal").ap()
        table_gat = nc.dram_tensor("table_gat", [NODES_P, GATW], FP32, kind="Internal").ap()
        table1 = nc.dram_tensor("table1", [NODES_P, P], FP32, kind="Internal").ap()
        node_logits = nc.dram_tensor("node_logits", [NODES_P, 3 * 2 * HEADS], BF16, kind="Internal").ap()
        flag_row = nc.dram_tensor("flag_row", [TILES], INT32, kind="Internal").ap()
        first_row = nc.dram_tensor("first_row", [TILES], INT32, kind="Internal").ap()
        etype_row = nc.dram_tensor("etype_row", [(TILES + 1) * P], FP32, kind="Internal").ap()
        seg_row = nc.dram_tensor("seg_row", [TILES + G, 2], FP32, kind="Internal").ap()

        X = sb("X", [P, NODES_P])
        H = sb("H", [P, NODES_P])
        ACC = sb("ACC", [P, 2, NODES_P])
        sums, aux = ACC[:, 0, :], ACC[:, 1, :]
        WT = sb("WT", [P, 2048])
        WR = sb("WR", [P, 2112])
        TOUT = sb("TOUT", [P, 2, 2048])
        STG = sb("STG", [P, 2, P])
        iota_f = sb("iota_f", [P, P])
        pidx = sb("pidx", [P, 1])
        head_iota = sb("head_iota", [P, HEADS])
        ident = sb("ident", [P, P])
        mean_mat = sb("mean_mat", [P, P])
        ones_mat = sb("ones_mat", [P, P])
        local = sb("local", [P, ROWB * P])
        idx16 = sb("idx16", [P, ROWB * P], INT32)
        idx8 = sb("idx8", [P, ROWB * P], INT32)
        idx1 = sb("idx1", [P, ROWB * P], INT32)
        etype = sb("etype", [P, ROWB * P])
        start = sb("start", [P, ROWB * P])
        wcol = sb("wcol", [P, TILES])
        base_i = sb("base_i", [P, ROWB], INT32)
        prev_last = sb("prev_last", [P, ROWB], INT32)
        meta = sb("meta", [1, BATCHES + 1, META], INT32)
        sel_first = sb("sel_first", [P, P])
        sel_last = sb("sel_last", [P, P])
        batch_first = sb("batch_first", [P, P])
        ends = sb("ends", [P, 2, ROWB])
        bends = sb("bends", [P, 2, ROWB])
        spans = sb("spans", [P, 3, ROWB])
        seg = sb("seg", [P, ROWB, 2])
        flag_i = sb("flag_i", [P, ROWB], INT32)
        first_i = sb("first_i", [P, ROWB], INT32)
        rows_i = ACC[:, 0, 0:4 * ROWB * P].bitcast(INT32).rearrange("p (a b e) -> p a b e", a=4, b=ROWB)
        rows_f = ACC[:, 1, 0:7 * ROWB * P].rearrange("p (a b e) -> p a b e", a=7, b=ROWB)
        x_rows = H[:, 0:XBLOCKS * P].rearrange("p (b f) -> p b f", f=P)
        SRC, DST, ET16, ET8 = range(4)
        F_LOCAL, F_IDX16, F_IDX8, F_SRC, F_ET, F_START, F_PEN = range(7)

        OH = sb("OH", [P, 2, G * P])
        GB = sb("GB", [P, 2, G * GATW])
        IDX = sb("IDX", [P, 2, G], INT32)
        OHR = sb("OHR", [P, 2, G, R16], BF16)
        ETR = H[0:R16, 0:2 * G * P].rearrange("p (b e) -> p b e", b=2)
        wstage = sb("wstage", [P, 2, G])

        def oh(b, j):
            return OH[:, b, j * P:(j + 1) * P]

        def oh16(b):
            return OH[:, b, 0:G * P // 2].bitcast(BF16).rearrange("p (j d) -> p j d", j=G)

        TH = G * HEADS
        SLOTS = 2 * G
        M = TOUT[:, :, 0:G * P].rearrange("p b (j f) -> p b j f", j=G)
        OHT = TOUT[:, 0, G * P:3 * G * P // 2].bitcast(BF16).rearrange("p (j e) -> p j e", j=G)
        NL = 2 * HEADS
        SPLIT = WR[:, 0:3 * NL * BLOCKS // 2].bitcast(BF16).rearrange("p (k s h) -> p k s h", k=BLOCKS, s=3)
        LOGITS = WR[:, 3 * NL * BLOCKS // 2:5 * NL * BLOCKS // 2]
        AW = sb("AW", [P, 2, G, 3, 2 * HEADS], BF16)
        SEG = H[0:1, 0:(BATCHES + 1) * SLOTS].rearrange("o (k x) -> o k x", x=SLOTS)
        free = [(BATCHES + 1) * SLOTS]

        def of_h(rows, columns):
            free[0] += columns
            return H[0:rows, free[0] - columns:free[0]]

        PEN = of_h(TH, 2 * (P + 1)).rearrange("p (b e) -> p b e", b=2)
        scans = of_h(TH, 4 * P).rearrange("p (n e) -> p n e", n=4)
        local_max, seg_max, from_before, all_max = (scans[:, n, :] for n in range(4))
        OH_MORE = of_h(P, 2 * G * P).rearrange("p (b n) -> p b n", b=2)

        def oh_gat(c):
            return (OH[:, c, :] if c < 2 else OH_MORE[:, c - 2, :]).rearrange("p (j d) -> p j d", j=G)

        AD = of_h(P, 4 * G * HEADS).rearrange("p (b j h) -> p b j h", b=2, j=G)
        XS = sb("XS", [P, HEADS, G])
        starts = sb("starts", [P, HEADS, G])
        CUTS = sb("CUTS", [1, 2, HEADS * SLOTS + 1])
        ROW = sb("ROW", [1, 3, HEADS * SLOTS])
        CARRY = sb("CARRY", [1, HEADS])
        ENDM = sb("ENDM", [TH, 2])
        RZ = sb("RZ", [1, 2, HEADS])
        RL = sb("RL", [1, 2, HEADS])
        RD = sb("RD", [1, HEADS])
        RE = sb("RE", [1, P + 2 * HEADS])
        one = sb("one", [1, 1])
        RS = sb("RS", [P, 2])
        ZL = sb("ZL", [P, 3, G, HEADS])
        ZD = sb("ZD", [P, 2, G, HEADS])
        WE = sb("WE", [P, 2, G, 2, HEADS])
        den_mat = sb("den_mat", [2 * HEADS, P])
        own_mat = sb("own_mat", [2 * HEADS, P])
        lin_cat = sb("lin_cat", [P, P + 3 * HEADS])
        cat_rhs = sb("cat_rhs", [P, P + 3 * HEADS])
        hsel = sb("hsel", [P, HEADS])
        shift = sb("shift", [P, 4])
        below = sb("below", [P, P])

        T0, T1, T2, T3, T4 = (GB[:, :, :].rearrange("p b n -> p (b n)")[:, n * CHUNK:(n + 1) * CHUNK] for n in range(5))
        T5 = OH[:, 0, 0:CHUNK]
        bn = sb("bn", [P, CHUNKS, 6])
        bnv = sb("bnv", [P, 8])
        eps = sb("eps", [P, 1])
        wcomp = sb("wcomp", [P, R8 * R8])

        MATS = ["L0_gnn_root1", "L0_gnn_root2", "L1_gnn_lin_w", "L1_gnn_proj_w", "L2_gnn_loop_w", "L2_gnn_res_w",
                "L3_gnn_W1_l", "L3_gnn_W1_r", "L3_gnn_W2_l", "L3_gnn_W2_r"]
        VECS = ["L0_gnn_b1", "L0_gnn_b2", "L1_gnn_gat_bias", "L1_gnn_proj_b", "L1_gnn_ln_gamma", "L1_gnn_ln_beta",
                "L2_gnn_bias", "L2_gnn_res_b", "L2_gnn_bn_gamma", "L2_gnn_bn_beta", "L3_gnn_b1", "L3_gnn_b2"]
        mats = sb("mats", [P, len(MATS), P])
        vecs = sb("vecs", [P, len(VECS) + 2])
        TURNED = ["L1_gnn_proj_w", "L3_gnn_W1_l", "L3_gnn_W1_r", "L3_gnn_W2_l", "L3_gnn_W2_r"]
        turned = sb("turned", [P, len(TURNED), P])

        def mat(name):
            return mats[:, MATS.index(name), :]

        def mat_t(name):
            return turned[:, TURNED.index(name), :]

        def vec(name):
            n = VECS.index(name)
            return vecs[:, n:n + 1]

        att_src, att_dst = (vecs[:, len(VECS) + n:len(VECS) + n + 1] for n in range(2))
        BASIS, MIXED = WT[:, 0:R8 * P], WT[:, R8 * P:2 * R8 * P]

        PS = ctx.enter_context(nc.psum_tensor("PS", [P, 8, 512], FP32))

        pad_zero = sem("pad_zero")
        cleared = sem("cleared")
        rows_in = sem("rows_in")
        meta_out = sem("meta_out")
        base_in = sem("base_in")
        ends_ps = sem("ends_ps")
        x_in = sem("x_in")
        w_in = sem("w_in")
        w2_in = sem("w2_in")
        basis_in = sem("basis_in")
        scratch = sem("scratch")
        seg_in = sem("seg_in")
        prep = sem("prep")
        turn_ps = sem("turn_ps")
        turn_sb = sem("turn_sb")
        mixed = sem("mixed")
        out_ps = sem("out_ps")
        out_sb = sem("out_sb")
        out_done = sem("out_done")

        class Table:

            def __init__(self, name, source, weights, dram, ready):
                self.source, self.weights, self.dram = source, weights, dram
                self.width = weights.shape[1]
                self.rows = dram.shape[0] // NODES_P
                self.part = dram.shape[1] if self.width <= 512 else self.width // 2
                self.ready = ready
                self.staged = sem(name + "_staged")
                self.made = sem(name + "_made")
                self.out_a = sem(name + "_out_a")
                self.out_d = sem(name + "_out_d")
                self.stored = [sem(f"{name}_stored{b}") for b in range(2)]
                self.zeroed = sem(name + "_zeroed")

        class Round:

            def __init__(self, name, kind, idx=None, table=None):
                self.kind, self.idx, self.table = kind, idx, table
                self.width = table.dram.shape[1] if table else 0
                self.idx_staged = sem(name + "_idx_staged")
                self.begun = sem(name + "_begun")
                self.gathered = [sem(f"{name}_gathered{b}") for b in range(2)]
                self.oh_ready = sem(name + "_oh_ready")
                self.agg_ready = sem(name + "_agg_ready")
                self.agg_free = sem(name + "_agg_free")

        TWO = 2 * G
        LOOKS = 4

        class Stage:

            def __init__(self, name, dve, pe, act):
                self.n_dve, self.n_pe, self.n_act = dve, pe, act
                self.dve, self.pe, self.act = sem(name + "_dve"), sem(name + "_pe"), sem(name + "_act")

            def dve_at(self, i, k):
                return i * self.n_dve + (1 + k)

            def pe_at(self, i, k):
                return i * self.n_pe + (1 + k)

            def act_at(self, i, k):
                return i * self.n_act + (1 + k)

            def end(self):
                return (self.dve, self.dve_at(CHUNKS, 0))

        n_l0a = Stage("n_l0a", 2, 1, 0)
        n_l0b = Stage("n_l0b", 6, 3, 1)
        n_l1 = Stage("n_l1", 17, 6, 3)
        n_l2a = Stage("n_l2a", 3, 1, 0)
        n_l2b = Stage("n_l2b", 6, 2, 1)
        n_l3a = Stage("n_l3a", 3, 1, 0)
        n_l3b = Stage("n_l3b", 7, 3, 1)
        norm_d = sem("norm_d")
        norm_a = sem("norm_a")
        degree = sem("degree")

        N_COLS, N_XG, N_MATG, N_LIN = 6, (XBLOCKS + 3) // 4, 2, 1
        TURNS = N_COLS + N_XG + N_MATG + N_LIN

        t_l0a = Table("t_l0a", X, WT[:, :], table16, [(turn_sb, TURNS)])
        t_l0b = Table("t_l0b", H, WR[:, 0:2048], table16, [n_l0a.end(), (w2_in, 16)])
        t_gat = Table("t_gat", X, lin_cat[:, :], table_gat, [n_l0b.end()])
        t_l2 = Table("t_l2", X, MIXED, table8, [n_l1.end(), (mixed, R8 * R8)])
        t_l3a = Table("t_l3a", X, mat_t("L3_gnn_W1_l"), table1, [n_l2b.end()])
        t_l3b = Table("t_l3b", H, mat_t("L3_gnn_W2_l"), table1, [n_l3a.end()])
        count = Round("count", "count")
        r_l0a = Round("r_l0a", "weigh", idx16, t_l0a)
        r_l0b = Round("r_l0b", "weighted", idx16, t_l0b)
        r_gat = Round("r_gat", "gat", idx1, t_gat)
        r_l2 = Round("r_l2", "sum", idx8, t_l2)
        r_l3a = Round("r_l3a", "degree", idx1, t_l3a)
        r_l3b = Round("r_l3b", "sum", idx1, t_l3b)

        et_in = [sem(f"et_in{b}") for b in range(2)]
        et_hot = sem("et_hot")
        looking = sem("looking")
        look_ready = sem("look_ready")
        look_free = sem("look_free")
        rt_ready = sem("rt_ready")
        w_added = sem("w_added")

        g_in = [sem(f"g_in{b}") for b in range(2)]
        split = sem("split")
        logits_out = sem("logits_out")
        g_starts = sem("g_starts")
        g_dve_ahead = sem("g_dve_ahead")
        g_cuts = sem("g_cuts")
        g_turned_ps = sem("g_turned_ps")
        g_turned = sem("g_turned")
        g_look = sem("g_look")
        g_pen = sem("g_pen")
        g_passed = sem("g_passed")
        g_dve, g_pe, g_act = sem("g_dve"), sem("g_pe"), sem("g_act")
        G_DVE = ("xs", "edge_logit", "own_logit", "local", "segment", "first", "row", "row_back", "ends", "old",
                 "forward", "new", "back", "carry", "max_logit", "logit_a", "lrelu", "logit_b", "diff", "scaled_logits",
                 "scaled_lrelu", "scaled_diff", "own", "m", "scale", "sums", "aux")
        G_PE = ("xs_rows", "row", "ends", "maxima", "scale")
        G_ACT = ("row", "weights", "scale", "scale2")

        def at(steps, k, step):
            return (k + 2) * len(steps) + (steps.index(step) + 1)

        XFER = {DST: a["dst"], SRC: a["src"], ET16: a["edge_type_16"], ET8: a["edge_type_8"]}
        WHOLE = (ROWB - 1) * P * P
        TAIL = FULL - (ROWB - 1) * P
        N_ROWS_IN = 3 * len(XFER) + 6
        N_W_IN = 1 + len(MATS) + len(VECS) + 2 + 1
        N_PREP = 21 + 19
        ENDS = 21
        LAST_ROWS = NODES - (XBLOCKS - 1) * P

        def meta_of(engine, k, at, n):
            _, values = nc.values_load_multi_w_load_instructions(meta[0:1, bass.ds(k, 1), at:at + n].rearrange("o k m -> o (k m)"),
                                                                 engines=[engine.engine], min_val=0, max_val=NODES - 1)
            return values

        block = ctx.enter_context(nc.Block())

        @block.sync
        def _(sp):
            sp.wait_ge(cleared, 1)
            for n, v in XFER.items():
                sp.dma_start(rows_i[:, n, 0:ROWB - 1, :],
                             v[0:WHOLE].rearrange("(b t e) -> t b e", t=P, e=P)).then_inc(rows_in, 16)
                sp.dma_start(rows_i[0:TAIL, n, ROWB - 1, :],
                             v[WHOLE:FULL * P].rearrange("(t e) -> t e", e=P)).then_inc(rows_in, 16)
                sp.dma_start(rows_i[TAIL:TAIL + 1, n, ROWB - 1, 0:REST],
                             v[FULL * P:EDGES].rearrange("(t e) -> t e", t=1)).then_inc(rows_in, 16)
            dst = a["dst"]
            whole = dst[0:WHOLE].rearrange("(b t e) -> t b e", t=P, e=P)
            tail = dst[WHOLE:FULL * P].rearrange("(t e) -> t e", e=P)
            sp.dma_start(base_i[:, 0:ROWB - 1], whole[:, :, 0]).then_inc(rows_in, 16)
            sp.dma_start(base_i[0:TAIL, ROWB - 1:ROWB], tail[:, 0:1]).then_inc(rows_in, 16)
            sp.dma_start(base_i[TAIL:TAIL + 1, ROWB - 1:ROWB],
                         dst[FULL * P:FULL * P + 1].rearrange("(t e) -> t e", t=1)).then_inc(rows_in, 16)
            sp.dma_start(prev_last[1:P, 0:ROWB - 1], whole[0:P - 1, :, P - 1]).then_inc(rows_in, 16)
            sp.dma_start(prev_last[0:1, 1:ROWB], whole[P - 1:P, :, P - 1]).then_inc(rows_in, 16)
            sp.dma_start(prev_last[1:TAIL + 1, ROWB - 1:ROWB], tail[:, P - 1:P]).then_inc(rows_in, 16)
            sp.dma_start(x_rows[:, 0:XBLOCKS - 1, :],
                         a["x"][0:(XBLOCKS - 1) * P, :].rearrange("(b p) f -> p b f", p=P)).then_inc(x_in, 16)
            sp.dma_start(x_rows[0:LAST_ROWS, XBLOCKS - 1, :], a["x"][(XBLOCKS - 1) * P:NODES, :]).then_inc(x_in, 16)
            sp.wait_ge(prep, N_PREP)
            n = TILES + 1 - (ROWB - 1) * P
            sp.dma_start(etype_row[0:WHOLE].rearrange("(b t e) -> t b e", t=P, e=P),
                         rows_f[:, F_ET, 0:ROWB - 1, :]).then_inc(scratch, 16)
            sp.dma_start(etype_row[WHOLE:(TILES + 1) * P].rearrange("(t e) -> t e", e=P),
                         rows_f[0:n, F_ET, ROWB - 1, :]).then_inc(scratch, 16)
            sp.dma_start(seg_row[0:(ROWB - 1) * P, :].rearrange("(b t) a -> t b a", t=P),
                         seg[:, 0:ROWB - 1, :]).then_inc(scratch, 16)
            sp.dma_start(seg_row[(ROWB - 1) * P:TILES + G, :], seg[0:n - 1 + G, ROWB - 1, :]).then_inc(scratch, 16)
            for dram, col in ((flag_row, flag_i), (first_row, first_i)):
                sp.dma_start(dram[0:(ROWB - 1) * P].rearrange("(b t) -> t b", t=P), col[:, 0:ROWB - 1]).then_inc(meta_out, 16)
                sp.dma_start(dram[(ROWB - 1) * P:TILES].rearrange("(t o) -> t o", o=1),
                             col[0:TILES - (ROWB - 1) * P, ROWB - 1:ROWB]).then_inc(meta_out, 16)
            sp.wait_ge(meta_out, 64)
            sp.dma_start(meta[0:1, 0:BATCHES, 0:1], flag_row.rearrange("(o k j) -> o k j", o=1, j=G)[:, :, 0:1]).then_inc(base_in, 16)
            sp.dma_start(meta[0:1, 0:BATCHES, 1:2], first_row.rearrange("(o k j) -> o k j", o=1, j=G)[:, :, 0:1]).then_inc(base_in, 16)
            sp.dma_start(meta[0:1, 0:BATCHES, META - G:META], first_row.rearrange("(o k j) -> o k j", o=1, j=G)).then_inc(base_in, 16)

            def store_table(t):
                wide = t.dram.shape[1] * t.rows
                with sp.Fori(0, BLOCKS // 2) as i:
                    for b in range(2):
                        blk = 2 * i + b
                        sp.wait_ge(t.out_a, blk + 3)
                        if t.width > 512:
                            sp.wait_ge(t.out_d, blk + 3)
                        sp.dma_start(t.dram[bass.ds(blk * (P * t.rows), P * t.rows), :]
                                     .rearrange("(p r) f -> p (r f)", r=t.rows),
                                     TOUT[:, b, 0:wide]).then_inc(t.stored[b], 16)

            store_table(t_l0a)
            sp.wait_ge(t_l0a.made, 2 + BLOCKS)
            sp.dma_start(BASIS.rearrange("d (r h) -> d r h", r=R8),
                         a["L2_gnn_basis_w"].rearrange("r d h -> d r h")).then_inc(basis_in, 16)
            sp.wait_ge(scratch, 64)
            with sp.Fori(0, BATCHES // 2) as i:
                for b in range(2):
                    k = 2 * i + b
                    sp.wait_ge(r_l0a.agg_ready, k * G + G)
                    sp.dma_start(ETR[:, b, :], etype_row[bass.ds(k * (G * P), G * P)].unsqueeze(0)
                                 .to_broadcast([R16, G * P])).then_inc(et_in[b], 16)
            store_table(t_l0b)
            store_table(t_gat)
            sp.wait_ge(*n_l0b.end())
            sp.dma_start(SEG, seg_row.rearrange("(o k j) a -> o k (j a)", o=1, j=G)).then_inc(seg_in, 16)
            sp.wait_ge(split, 5)
            sp.dma_start(node_logits.rearrange("(k p) c -> p k c", p=P), SPLIT.rearrange("p k s h -> p k (s h)"))\
                .then_inc(logits_out, 16)
            sp.wait_ge(logits_out, 16)

            def windows(k, b):
                flag, base = meta_of(sp, k, 0, 2)
                sp.wait_ge(g_dve, at(G_DVE, k - 2, "scaled_logits"))
                sp.dma_start(AW[:, b, 0, :, :].rearrange("p s h -> p (s h)"), node_logits[bass.ds(base, P), :]).then_inc(g_in[b], 16)
                with sp.If(flag > 0):
                    sp.sem_inc(g_in[b], 16 * (G - 1))
                with sp.Else():
                    bases = meta_of(sp, k, META - G, G)
                    for j in range(1, G):
                        sp.dma_start(AW[:, b, j, :, :].rearrange("p s h -> p (s h)"), node_logits[bass.ds(bases[j], P), :]).then_inc(g_in[b], 16)

            with sp.Fori(0, BATCHES // 2) as i:
                for b in range(2):
                    windows(2 * i + b, b)
            windows(BATCHES, 0)
            store_table(t_l2)
            store_table(t_l3a)
            store_table(t_l3b)
            sp.wait_ge(out_sb, N_XG)
            sp.dma_start(out[0:(XBLOCKS - 1) * P, :].rearrange("(b p) f -> p b f", p=P),
                         x_rows[:, 0:XBLOCKS - 1, :]).then_inc(out_done, 16)
            sp.dma_start(out[(XBLOCKS - 1) * P:NODES, :], x_rows[0:LAST_ROWS, XBLOCKS - 1, :]).then_inc(out_done, 16)
            sp.wait_ge(out_done, 32)

        @block.gpsimd
        def _(pool):
            pool.memset(rows_i[:, :, :, :], 0)
            pool.memset(base_i[:, :], 0)
            pool.memset(meta[:, :, :], 0)
            pool.iota(batch_first[:, :], [[G, P // G], [0, G]], base=0, channel_multiplier=0, allow_small_or_imprecise_dtypes=True)
            pool.memset(prev_last[:, :], -1)
            pool.memset(x_rows[:, XBLOCKS - 1, :], 0.0)
            pool.memset(X[:, XBLOCKS * P:NODES_P], 0.0)
            pool.iota(iota_f[:, :], [[1, P]], base=0, channel_multiplier=0, allow_small_or_imprecise_dtypes=True)
            pool.iota(pidx[:, :], [[0, 1]], base=0, channel_multiplier=1, allow_small_or_imprecise_dtypes=True)
            pool.iota(head_iota[:, :], [[HD, HEADS]], base=0, channel_multiplier=0, allow_small_or_imprecise_dtypes=True)
            pool.memset(mean_mat[:, :], 1.0 / P)
            pool.memset(ones_mat[:, :], 1.0)
            pool.memset(eps[:, :], LN_EPS)
            pool.memset(CARRY[:, :], -BIG)
            pool.memset(CUTS[:, :, :], -BIG)
            pool.memset(one[:, :], 1.0).then_inc(pad_zero, 1)
            pool.wait_ge(pad_zero, 1)
            pool.memset(rows_i[:, DST, ROWB - 1, :], int(NO_NODE)).then_inc(cleared, 1)

            def stage_table(t, zero):
                for s, n in t.ready:
                    pool.wait_ge(s, n)
                for z in zero:
                    pool.memset(z, 0.0).then_inc(t.zeroed, 1)
                with pool.Fori(0, BLOCKS // 2) as i:
                    for b in range(2):
                        blk = 2 * i + b
                        pool.wait_ge(t.made, blk + 1)
                        pool.tensor_copy(STG[:, b, :], t.source[:, bass.ds(blk * P, P)]).then_inc(t.staged, 1)

            def gather(r):
                for b in range(2):
                    pool.wait_ge(r.table.stored[b], 16 * (BLOCKS // 2))
                with pool.Fori(0, BATCHES // 2) as i:
                    for b in range(2):
                        k = 2 * i + b
                        pool.wait_ge(r.idx_staged, k + 1)
                        if r.kind == "gat":
                            pool.wait_ge(g_dve, at(G_DVE, k - 2, "m"))
                        else:
                            pool.wait_ge(r.agg_ready, k * G + G)
                        pool.sem_inc(r.begun, 1)
                        for j in range(G):
                            pool.indirect_dma_start(
                                out=GB[:, b, j * r.width:(j + 1) * r.width], out_offset=None,
                                in_=r.table.dram[:, :],
                                in_offset=bass.IndirectOffsetOnAxis(ap=IDX[:, b, j:j + 1], axis=0),
                            ).then_inc(r.gathered[b], 16)

            stage_table(t_l0a, [])
            gather(r_l0a)
            stage_table(t_l0b, [sums])
            gather(r_l0b)
            stage_table(t_gat, [sums, aux[0:2 * HEADS, :], PEN])
            gather(r_gat)
            stage_table(t_l2, [sums])
            gather(r_l2)
            stage_table(t_l3a, [sums, aux])
            gather(r_l3a)
            stage_table(t_l3b, [sums])
            gather(r_l3b)

        @block.scalar
        def _(act):
            act.sem_inc(n_l0b.act, 1)
            act.sem_inc(n_l1.act, 1)
            act.sem_inc(n_l2b.act, 1)
            act.sem_inc(n_l3b.act, 1)
            act.sem_inc(g_act, 2 * len(G_ACT))
            act.sem_inc(g_pen, 1)
            for t in (t_l0a, t_l0b, t_gat, t_l2, t_l3a, t_l3b):
                act.sem_inc(t.out_a, 2)
            act.dma_start(WT[:, :].rearrange("d (r h) -> d r h", r=R16),
                          a["L0_gnn_W1"].rearrange("r d h -> d r h")).then_inc(w_in, 16)
            for n, name in enumerate(MATS):
                act.dma_start(mats[:, n, :], a[name]).then_inc(w_in, 16)
            for n, name in enumerate(VECS):
                act.dma_start(vecs[:, n:n + 1], a[name].rearrange("(p o) -> p o", o=1)).then_inc(w_in, 16)
            for n, name in enumerate(("L1_gnn_att_src", "L1_gnn_att_dst")):
                act.dma_start(vecs[:, len(VECS) + n:len(VECS) + n + 1],
                              a[name].rearrange("o h (k u) -> (o h k) u", u=1)).then_inc(w_in, 16)
            act.dma_start(wcomp[:, :], a["L2_gnn_w_comp"].rearrange("r b -> (r b)").unsqueeze(0)
                          .to_broadcast([P, R8 * R8])).then_inc(w_in, 16)
            act.dma_start(WR[:, 0:2048].rearrange("d (r h) -> d r h", r=R16),
                          a["L0_gnn_W2"].rearrange("r d h -> d r h")).then_inc(w2_in, 16)

            def copy_table(t):
                def one(i, b):
                    blk = 2 * i + b
                    act.wait_ge(t.made, blk + 3)
                    if not isinstance(i, int):
                        act.wait_ge(t.stored[b], i * 16)
                    ps = PS[:, 4 * b:4 * b + 4, :].rearrange("p a n -> p (a n)")
                    if t is t_gat:
                        act.copy(LOGITS[:, bass.ds(blk * NL, NL)], ps[:, GATW:GATW + NL])
                    act.copy(TOUT[:, b, 0:t.part], ps[:, 0:t.part]).then_inc(t.out_a, 1)

                one(0, 0)
                one(0, 1)
                with act.Fori(1, BLOCKS // 2) as i:
                    one(i, 0)
                    one(i, 1)

            def stage_indices(r):
                with act.Fori(0, BATCHES // 2) as i:
                    for b in range(2):
                        k = 2 * i + b
                        act.wait_ge(r.agg_ready, k * G + G)
                        act.copy(IDX[:, b, :], r.idx[:, bass.ds(k * G, G)]).then_inc(r.idx_staged, 1)

            def roots(st, steps):
                with act.Fori(0, CHUNKS) as i:
                    for pe_step in steps:
                        act.wait_ge(st.pe, st.pe_at(i, pe_step))
                        act.activation(T4, PS[:, 2, 0:CHUNK], ACT.Sqrt, bias=eps[:, 0:1]).then_inc(st.act, 1)

            act.wait_ge(turn_sb, TURNS)
            copy_table(t_l0a)
            stage_indices(r_l0a)
            copy_table(t_l0b)
            stage_indices(r_l0b)
            roots(n_l0b, [3])
            copy_table(t_gat)

            def starts_of(k, b):
                act.copy(starts[:, :, :], mid(start[:, bass.ds(k * G, G)], HEADS)).then_inc(g_starts, 1)
                act.copy(CUTS[:, b, 0:HEADS * SLOTS].rearrange("o (h x) -> o h x", x=SLOTS)[:, :, 1:SLOTS],
                         SEG[:, bass.ds(k, 1), 1:SLOTS].to_broadcast([1, HEADS, SLOTS - 1])).then_inc(g_cuts, 1)

            def turn(k):
                for h in range(2):
                    act.wait_ge(g_turned_ps, 2 * k + (1 + h))
                    act.copy(OHT[:, 4 * h:4 * h + 4, :].rearrange("p j e -> p (j e)"), PS[:, 6 + h, :]).then_inc(g_turned, 1)

            def penalties(k, b):
                act.wait_ge(g_look, k + 1)
                act.mul(PEN[:, b, 1:P], PS[0:TH, 7, 1:P], -BIG).then_inc(g_pen, 1)

            def attend(k, b):
                starts_of(k + 1, 1 - b)
                act.wait_ge(g_pe, at(G_PE, k, "row"))
                act.copy(ROW[:, 0, :].rearrange("o (x a) -> o a x", a=2),
                         PS[0:1, 5, 0:2 * TH].rearrange("o (a x) -> o a x", a=2)).then_inc(g_act, 1)
                turn(k + 1)
                penalties(k + 1, 1 - b)
                act.wait_ge(g_dve, at(G_DVE, k, "diff"))
                act.activation(WE[:, b, :, :, :].rearrange("p j t h -> p t j h"), ZD[:, :, :, :], ACT.Exp).then_inc(g_act, 1)
                act.wait_ge(g_dve, at(G_DVE, k, "scaled_diff"))
                act.activation(RE[:, 0:P].rearrange("o (h c) -> o h c", c=HD), last(RD[:, :], HD), ACT.Exp).then_inc(g_act, 1)
                act.activation(RE[:, P:P + 2 * HEADS].rearrange("o (t h) -> o t h", t=2), mid(RD[:, :], 2), ACT.Exp)\
                    .then_inc(g_act, 1)
                act.copy(IDX[:, b, :], r_gat.idx[:, bass.ds((k + 2) * G, G)]).then_inc(r_gat.idx_staged, 1)

            act.activation(RE[:, 0:1], one[:, :], ACT.Exp)
            act.wait_ge(seg_in, 16)
            act.wait_ge(t_gat.zeroed, 3)
            for k in range(2):
                act.copy(IDX[:, k, :], r_gat.idx[:, k * G:(k + 1) * G]).then_inc(r_gat.idx_staged, 1)
            starts_of(0, 0)
            turn(0)
            penalties(0, 0)
            with act.Fori(0, BATCHES // 2) as i:
                for b in range(2):
                    attend(2 * i + b, b)

            with act.Fori(0, CHUNKS) as i:
                act.wait_ge(n_l1.pe, n_l1.pe_at(i, 1))
                act.copy(T0, PS[:, 0, 0:CHUNK]).then_inc(n_l1.act, 1)
                for pe_step in (4, 6):
                    act.wait_ge(n_l1.pe, n_l1.pe_at(i, pe_step))
                    act.activation(T4, PS[:, 2, 0:CHUNK], ACT.Sqrt, bias=eps[:, 0:1]).then_inc(n_l1.act, 1)
            copy_table(t_l2)
            stage_indices(r_l2)
            act.wait_ge(norm_d, 1 + CHUNKS + 1)
            act.activation(bnv[:, 2:3], bnv[:, 1:2], ACT.Sqrt, bias=eps[:, 0:1]).then_inc(norm_a, 1)
            roots(n_l2b, [2])
            copy_table(t_l3a)
            stage_indices(r_l3a)
            copy_table(t_l3b)
            stage_indices(r_l3b)
            roots(n_l3b, [3])

        @block.tensor
        def _(pe):
            for r in (count, r_l0a, r_l0b, r_gat, r_l2, r_l3a, r_l3b):
                pe.sem_inc(r.agg_ready, TWO)
            for t in (t_l0a, t_l0b, t_gat, t_l2, t_l3a, t_l3b):
                pe.sem_inc(t.made, 2)
            for st in (n_l0a, n_l0b, n_l1, n_l2a, n_l2b, n_l3a, n_l3b):
                pe.sem_inc(st.pe, 1)
            pe.sem_inc(g_pe, 2 * len(G_PE))

            pe.wait_ge(prep, ENDS)
            nc.tensor.matmul(PS[:, 7, 0:ROWB], sel_first[:, :], ends[:, 0], start=True, stop=True)
            nc.tensor.matmul(PS[:, 7, ROWB:2 * ROWB], sel_last[:, :], ends[:, 1], start=True, stop=True).then_inc(ends_ps, 1)
            pe.wait_ge(prep, N_PREP)
            for n in range(N_COLS):
                if n >= 4:
                    pe.wait_ge(turn_sb, n - 3)
                for q in range(ROWB):
                    ins = nc.tensor.transpose(PS[:, 2 * (n % 4) + q // 4, (q % 4) * P:(q % 4 + 1) * P],
                                              rows_f[:, n, q, :], ident[:, :])
                ins.then_inc(turn_ps, 1)
            pe.wait_ge(x_in, 32)
            for n in range(N_XG):
                pe.wait_ge(turn_sb, max(n - 7, 0) + N_COLS)
                for q in range(4 * n, min(4 * n + 4, XBLOCKS)):
                    ins = nc.tensor.transpose(PS[:, n % 8, (q % 4) * P:(q % 4 + 1) * P], x_rows[:, q, :], ident[:, :])
                ins.then_inc(turn_ps, 1)
            pe.wait_ge(w_in, 16 * N_W_IN)
            pe.wait_ge(turn_sb, N_COLS + N_XG)
            for n in range(N_MATG):
                for q in range(4 * n, min(4 * n + 4, len(TURNED))):
                    ins = nc.tensor.transpose(PS[:, n, (q % 4) * P:(q % 4 + 1) * P], mat(TURNED[q]), ident[:, :])
                ins.then_inc(turn_ps, 1)
            nc.tensor.matmul(PS[:, 2, 0:P + 3 * HEADS], mat("L1_gnn_lin_w"), cat_rhs[:, :],
                             start=True, stop=True).then_inc(turn_ps, 1)

            def multiply_table(t):
                for s, n in t.ready:
                    pe.wait_ge(s, n)
                with pe.Fori(0, BLOCKS // 2) as i:
                    for b in range(2):
                        blk = 2 * i + b
                        pe.wait_ge(t.staged, blk + 1)
                        pe.wait_ge(t.out_a, blk + 1)
                        if t.width > 512:
                            pe.wait_ge(t.out_d, blk + 1)
                        for c in range(0, t.width, 512):
                            w = min(512, t.width - c)
                            ins = nc.tensor.matmul(PS[:, 4 * b + c // 512, 0:w], STG[:, b, :], t.weights[:, c:c + w],
                                                   start=True, stop=True)
                        ins.then_inc(t.made, 1)
                pe.wait_ge(t.out_a, 2 + BLOCKS)
                if t.width > 512:
                    pe.wait_ge(t.out_d, 2 + BLOCKS)

            def sum_tile(r, b, j, bank, first, final):
                at = dict(start=first, stop=final)
                if r.kind == "count":
                    return nc.tensor.matmul(PS[0:R16, bank, 0:P], OHR[:, b, j, :], oh16(b)[:, j, :], **at)
                if r.kind == "degree":
                    nc.tensor.matmul(PS[:, 2 + bank, 0:P], ones_mat[:, :], oh(b, j), **at)
                if r.kind == "gat":
                    hot = oh_gat(b)[:, j, :]
                    nc.tensor.matmul(PS[0:2 * HEADS, 2 + bank, 0:P],
                                     WE[:, b % 2, j, :, :].rearrange("p t h -> p (t h)"), hot, **at)
                    return nc.tensor.matmul(PS[:, bank, 0:P], M[:, b % 2, j, :], hot, **at)
                return nc.tensor.matmul(PS[:, bank, 0:P], GB[:, b, j * r.width:j * r.width + P], oh(b, j), **at)

            def sum_tiles(r, k, b, ready, look=None, bank=None):
                bank = b if bank is None else bank
                flag, base = meta_of(pe, k, 0, 2)
                with pe.If(flag > 0):
                    if look:
                        look([base] * G)
                    for s, n in ready:
                        pe.wait_ge(s, n)
                    pe.wait_ge(r.agg_free, k * G + G)
                    for j in range(G):
                        ins = sum_tile(r, b, j, bank, j == 0, j == G - 1)
                    ins.then_inc(r.agg_ready, G)
                with pe.Else():
                    if look:
                        look(meta_of(pe, k, META - G, G))
                    for s, n in ready:
                        pe.wait_ge(s, n)
                    for j in range(G):
                        pe.wait_ge(r.agg_free, k * G + (TWO + j))
                        sum_tile(r, b, j, bank, True, True).then_inc(r.agg_ready, 1)

            def sum_round(r):
                with pe.Fori(0, BATCHES // 2) as i:
                    for b in range(2):
                        k = 2 * i + b
                        ready = [(r.oh_ready, k + 1)]
                        if r.table:
                            ready.append((r.gathered[b], (i + 1) * (16 * G)))
                        sum_tiles(r, k, b, ready)

            def edges_done(r):
                return (r.agg_free, TWO + TILES)

            def node_products(st, first, first_signal, banks, later, after):
                for s, n in after:
                    pe.wait_ge(s, n)
                with pe.Fori(0, CHUNKS) as i:
                    pe.wait_ge(st.dve, st.dve_at(i, 0))
                    for n, (bank, w, v) in enumerate(first):
                        ins = nc.tensor.matmul(PS[0:w.shape[1], bank, 0:CHUNK], w, v[:, bass.ds(i * CHUNK, CHUNK)],
                                               start=True, stop=True)
                    ins.then_inc(st.pe, 1)
                    for dve_step, bank, w, v in later:
                        pe.wait_ge(st.dve, st.dve_at(i, dve_step))
                        nc.tensor.matmul(PS[:, bank, 0:CHUNK], w, v, start=True, stop=True).then_inc(st.pe, 1)

            multiply_table(t_l0a)
            pe.wait_ge(base_in, 48)
            sum_round(count)
            pe.wait_ge(rt_ready, 2)
            with pe.Fori(0, BATCHES // 2) as i:
                for b in range(2):
                    k = 2 * i + b

                    def look(bases):
                        pe.wait_ge(et_hot, k + 1)
                        for j in range(G):
                            pe.wait_ge(look_free, k * G + (j + 1))
                            pe.sem_inc(looking, 1)
                            nc.tensor.matmul(PS[:, 4 + j % LOOKS, 0:P], ETR[:, b, j * P:(j + 1) * P],
                                             aux[0:R16, bass.ds(bases[j], P)], start=True, stop=True).then_inc(look_ready, 1)

                    sum_tiles(r_l0a, k, b, [(look_free, k * G + (LOOKS + G)), (r_l0a.gathered[b], (i + 1) * (16 * G))], look)
            node_products(n_l0a, [(0, mat("L0_gnn_root1"), X)], 1, None, [], [edges_done(r_l0a)])
            multiply_table(t_l0b)
            sum_round(r_l0b)
            node_products(n_l0b, [(0, mat("L0_gnn_root2"), H)], 1, None,
                          [(2, 1, mean_mat[:, :], T1), (4, 2, mean_mat[:, :], T3)], [edges_done(r_l0b)])
            multiply_table(t_gat)
            def absorb(s, n):
                pe.wait_ge(s, n)
                pe.sem_inc(g_passed, 1)

            def turn(k, c):
                pe.wait_ge(r_gat.oh_ready, k + 1)
                pe.wait_ge(g_pen, k + 1)
                for h in range(2):
                    for j in range(4):
                        ins = nc.tensor.transpose(PS[:, 6 + h, j * P:(j + 1) * P], oh_gat(c)[:, 4 * h + j, :], ident[:, :])
                    ins.then_inc(g_turned_ps, 1)

            def look_up(k, c, i1, flag):
                absorb(g_starts, k + 1)
                absorb(g_turned, 2 * k + 2)
                nc.tensor.transpose(PS[0:TH, 7, 0:P], starts[:, :, :].rearrange("p h j -> p (h j)"), ident[:, :])
                absorb(g_in[c % 2], i1 * (16 * G))

                def products(windows):
                    for j, window in enumerate(windows):
                        ins = nc.tensor.matmul(PS[:, 6, j * 3 * NL:(j + 1) * 3 * NL], OHT[:, j, :],
                                               AW[:, c % 2, window, :, :].rearrange("p s h -> p (s h)"), start=True, stop=True)
                    ins.then_inc(g_look, 1)

                with pe.If(flag > 0):
                    products([0] * G)
                with pe.Else():
                    products(range(G))

            def attend(i, c):
                k, b = 4 * i + c, c % 2
                before = not (isinstance(i, int) and c == 0)
                if before:
                    flag_before, = meta_of(pe, k - 1, 0, 1)
                flag_next, = meta_of(pe, k + 1, 0, 1)

                def sum_part(part):
                    if not before:
                        return
                    with pe.If(flag_before > 0):
                        if part == 0:
                            pe.wait_ge(g_dve, at(G_DVE, k - 1, "m"))
                            pe.wait_ge(r_gat.agg_free, (k - 1) * G + G)
                        for j in (2 * part, 2 * part + 1):
                            ins = sum_tile(r_gat, (c - 1) % 4, j, 1 - b, j == 0, j == G - 1)
                        if part == 3:
                            ins.then_inc(r_gat.agg_ready, G)
                    if part == 3:
                        with pe.Else():
                            pe.wait_ge(g_dve, at(G_DVE, k - 1, "m"))
                            for j in range(G):
                                pe.wait_ge(r_gat.agg_free, (k - 1) * G + (TWO + j))
                                sum_tile(r_gat, (c - 1) % 4, j, 1 - b, True, True).then_inc(r_gat.agg_ready, 1)

                absorb(g_dve, at(G_DVE, k, "xs"))
                nc.tensor.transpose(PS[0:TH, 4, 0:P], XS[:, :, :].rearrange("p h j -> p (h j)"), ident[:, :]).then_inc(g_pe, 1)
                turn(k + 1, (c + 1) % 4)
                absorb(g_dve, at(G_DVE, k, "segment"))
                for n, part in enumerate((seg_max[:, 0:1], local_max[:, P - 1:P])):
                    ins = nc.tensor.matmul(PS[0:1, 5, n * TH:(n + 1) * TH], part, ident[0:TH, 0:TH], start=True, stop=True)
                ins.then_inc(g_pe, 1)
                sum_part(0)
                absorb(g_dve, at(G_DVE, k, "row_back"))
                for n in range(2):
                    ins = nc.tensor.matmul(PS[0:TH, 5, P + n:P + n + 1], ROW[:, 2, n::2],
                                           one[:, :], start=True, stop=True)
                ins.then_inc(g_pe, 1)
                look_up(k + 1, (c + 1) % 4, 2 * i + ((c + 1) // 2 + 1), flag_next)
                absorb(g_dve, at(G_DVE, k, "back"))
                nc.tensor.transpose(PS[:, 4, 0:TH], all_max, ident[0:TH, 0:TH]).then_inc(g_pe, 1)
                sum_part(1)
                sum_part(2)
                absorb(g_act, at(G_ACT, k, "scale2"))
                nc.tensor.matmul(PS[:, 5, 256:257], RE[:, 0:P], one[:, :], start=True, stop=True)
                nc.tensor.matmul(PS[0:2 * HEADS, 5, 258:259], RE[:, P:P + 2 * HEADS], one[:, :],
                                 start=True, stop=True).then_inc(g_pe, 1)
                sum_part(3)

            flag_first, = meta_of(pe, 0, 0, 1)
            turn(0, 0)
            look_up(0, 0, 1, flag_first)
            for c in range(4):
                attend(0, c)
            with pe.Fori(1, BATCHES // 4) as i:
                for c in range(4):
                    attend(i, c)
            sum_tiles(r_gat, BATCHES - 1, 3, [(g_dve, at(G_DVE, BATCHES - 1, "m"))], bank=1)
            node_products(n_l1, [(0, lin_cat[:, 0:P], X), (1, den_mat[:, :], aux[0:2 * HEADS, :]),
                                 (3, own_mat[:, :], aux[0:2 * HEADS, :])], 1, None,
                          [(6, 4, mat_t("L1_gnn_proj_w"), T3), (7, 5, mean_mat[:, :], T1), (9, 2, mean_mat[:, :], T3),
                           (13, 5, mean_mat[:, :], T1), (15, 2, mean_mat[:, :], T3)], [edges_done(r_gat)])
            multiply_table(t_l2)
            sum_round(r_l2)
            node_products(n_l2a, [(0, mat("L2_gnn_loop_w"), X), (1, mat("L2_gnn_res_w"), X)], 1, None, [],
                          [edges_done(r_l2)])
            with pe.Fori(0, CHUNKS) as i:
                for dve_step, bank, v in ((2, 1, T1), (4, 2, T3)):
                    pe.wait_ge(n_l2b.dve, n_l2b.dve_at(i, dve_step))
                    nc.tensor.matmul(PS[:, bank, 0:CHUNK], mean_mat[:, :], v, start=True, stop=True).then_inc(n_l2b.pe, 1)
            multiply_table(t_l3a)
            sum_round(r_l3a)
            node_products(n_l3a, [(0, mat_t("L3_gnn_W1_r"), X)], 1, None, [], [edges_done(r_l3a)])
            multiply_table(t_l3b)
            sum_round(r_l3b)
            node_products(n_l3b, [(0, mat_t("L3_gnn_W2_r"), H)], 1, None,
                          [(3, 1, mean_mat[:, :], T1), (5, 2, mean_mat[:, :], T3)], [edges_done(r_l3b)])
            pe.wait_ge(*n_l3b.end())
            for n in range(N_XG):
                if n >= 8:
                    pe.wait_ge(out_sb, n - 7)
                for q in range(4 * n, min(4 * n + 4, XBLOCKS)):
                    ins = nc.tensor.transpose(PS[:, n % 8, (q % 4) * P:(q % 4 + 1) * P], X[:, q * P:(q + 1) * P], ident[:, :])
                ins.then_inc(out_ps, 1)

        @block.vector
        def _(dve):
            for r in (count, r_l0a, r_l0b, r_gat, r_l2, r_l3a, r_l3b):
                dve.sem_inc(r.agg_free, TWO)
            for t in (t_l0a, t_l0b, t_gat, t_l2, t_l3a, t_l3b):
                dve.sem_inc(t.out_d, 2)
            for st in (n_l0a, n_l0b, n_l1, n_l2a, n_l2b, n_l3a, n_l3b):
                dve.sem_inc(st.dve, 1)
            dve.sem_inc(look_free, LOOKS)
            dve.sem_inc(g_dve, 2 * len(G_DVE))
            dve.sem_inc(norm_d, 1)

            preps = [0]

            def link(ins):
                preps[0] += 1
                ins.then_inc(prep, 1)
                dve.wait_ge(prep, preps[0])

            dve.wait_ge(cleared, 1)
            link(dve.tensor_scalar(ident[:, :], iota_f[:, :], pidx[:, 0:1], None, ALU.is_equal))
            link(dve.tensor_scalar(below[:, 0:HEADS], head_iota[:, :], pidx[:, 0:1], 0.0, ALU.subtract, ALU.is_le))
            link(dve.tensor_scalar(hsel[:, :], head_iota[:, :], pidx[:, 0:1], -float(HD), ALU.subtract, ALU.is_gt))
            link(dve.tensor_tensor(hsel[:, :], hsel[:, :], below[:, 0:HEADS], ALU.mult))
            link(dve.tensor_scalar(shift[:, 0:1], pidx[:, 0:1], float(HD), None, ALU.mult))
            link(dve.tensor_scalar(shift[:, 1:2], pidx[:, 0:1], float(HD), -float(HD * HEADS), ALU.mult, ALU.add))
            for m, rows, s in ((own_mat[:, :], 2 * HEADS, 1), (den_mat[:, :], 2 * HEADS, 0)):
                link(dve.tensor_scalar(below[0:rows, :], iota_f[0:rows, :], shift[0:rows, s:s + 1], 0.0, ALU.subtract, ALU.is_ge))
                link(dve.tensor_scalar(m, iota_f[0:rows, :], shift[0:rows, s:s + 1], float(HD), ALU.subtract, ALU.is_lt))
                link(dve.tensor_tensor(m, m, below[0:rows, :], ALU.mult))
            link(dve.tensor_tensor(den_mat[:, :], den_mat[:, :], own_mat[:, :], ALU.add))
            dve.wait_ge(w_in, 16 * N_W_IN)
            link(dve.tensor_copy(cat_rhs[:, 0:P], ident[:, :]))
            for n, att in enumerate((att_src, att_dst, att_src)):
                link(dve.tensor_scalar(cat_rhs[:, P + n * HEADS:P + (n + 1) * HEADS], hsel[:, :], att, None, ALU.mult))
            link(dve.tensor_scalar(sel_first[:, :], batch_first[:, :], pidx[:, 0:1], None, ALU.is_equal))
            link(dve.tensor_scalar(sel_last[:, :], batch_first[:, :], float(G - 1), pidx[:, 0:1], ALU.add, ALU.is_equal))
            dve.wait_ge(rows_in, 16 * N_ROWS_IN)
            link(dve.tensor_copy(ends[:, 0], base_i[:, :]))
            link(dve.tensor_copy(ends[:, 1], rows_i[:, DST, :, P - 1]))
            assert preps[0] == ENDS, preps
            dve.wait_ge(ends_ps, 1)
            link(dve.tensor_copy(bends[:, :, :].rearrange("p a b -> p (a b)"), PS[:, 7, 0:2 * ROWB]))
            link(dve.tensor_tensor(spans[:, 0], bends[:, 1], bends[:, 0], ALU.subtract))
            link(dve.tensor_scalar(spans[:, 1], spans[:, 0], float(P), None, ALU.is_lt))
            link(dve.tensor_tensor(spans[:, 0], bends[:, 0], ends[:, 0], ALU.subtract))
            link(dve.tensor_tensor(spans[:, 0], spans[:, 0], spans[:, 1], ALU.mult))
            link(dve.tensor_tensor(spans[:, 2], spans[:, 0], ends[:, 0], ALU.add))
            link(dve.tensor_copy(flag_i[:, :], spans[:, 1]))
            link(dve.tensor_copy(first_i[:, :], spans[:, 2]))
            link(dve.tensor_tensor(rows_f[:, F_LOCAL], rows_i[:, DST], last(first_i[:, :], P), ALU.subtract))
            for f, v, types in ((F_IDX16, R16, ET16), (F_IDX8, R8, ET8)):
                link(dve.scalar_tensor_tensor(rows_f[:, f], rows_i[:, SRC], float(v), rows_i[:, types], ALU.mult, ALU.add))
            link(dve.tensor_copy(rows_f[:, F_SRC], rows_i[:, SRC]))
            link(dve.tensor_copy(rows_f[:, F_ET], rows_i[:, ET16]))
            link(dve.tensor_tensor(rows_f[:, F_START, :, 1:P], rows_i[:, DST, :, 1:P], rows_i[:, DST, :, 0:P - 1], ALU.not_equal))
            link(dve.tensor_tensor(rows_f[:, F_START, :, 0], rows_i[:, DST, :, 0], prev_last[:, :], ALU.not_equal))
            link(dve.tensor_scalar(rows_f[:, F_PEN], rows_f[:, F_START], -BIG, None, ALU.mult))
            link(dve.tensor_copy(seg[:, :, 0], rows_f[:, F_PEN, :, 0]))
            link(dve.tensor_tensor(seg[:, :, 1], ends[:, 0], ends[:, 1], ALU.not_equal))
            link(dve.tensor_scalar(seg[:, :, 1], seg[:, :, 1], -BIG, None, ALU.mult))
            assert preps[0] == N_PREP, preps

            cols = (local, idx16, idx8, idx1, etype, start)
            for n, col in enumerate(cols):
                dve.wait_ge(turn_ps, n + 1)
                ps = PS[:, 2 * (n % 4):2 * (n % 4) + 2, :].rearrange("p a n -> p (a n)")
                dve.tensor_copy(col[:, :], ps[:, 0:ROWB * P]).then_inc(turn_sb, 1)
            for n in range(N_XG):
                dve.wait_ge(turn_ps, N_COLS + n + 1)
                w = min(512, XBLOCKS * P - 512 * n)
                dve.tensor_copy(X[:, 512 * n:512 * n + w], PS[:, n % 8, 0:w]).then_inc(turn_sb, 1)
            for n in range(N_MATG):
                dve.wait_ge(turn_ps, N_COLS + N_XG + n + 1)
                m = min(4, len(TURNED) - 4 * n)
                dve.tensor_copy(turned[:, 4 * n:4 * n + m, :].rearrange("p q n -> p (q n)"), PS[:, n, 0:m * P])\
                    .then_inc(turn_sb, 1)
            dve.wait_ge(turn_ps, TURNS)
            dve.tensor_copy(lin_cat[:, :], PS[:, 2, 0:P + 3 * HEADS]).then_inc(turn_sb, 1)

            def copy_table(t):
                if t.width <= 512:
                    return

                def one(i, b):
                    blk = 2 * i + b
                    dve.wait_ge(t.made, blk + 3)
                    if not isinstance(i, int):
                        dve.wait_ge(t.stored[b], i * 16)
                    ps = PS[:, 4 * b:4 * b + 4, :].rearrange("p a n -> p (a n)")
                    dve.tensor_copy(TOUT[:, b, t.part:t.width], ps[:, t.part:t.width]).then_inc(t.out_d, 1)

                one(0, 0)
                one(0, 1)
                with dve.Fori(1, BLOCKS // 2) as i:
                    one(i, 0)
                    one(i, 1)

            def add_window(r, base, bank):
                if r.kind == "count":
                    dst = aux[0:R16, bass.ds(base, P)]
                    return dve.tensor_tensor(dst, dst, PS[0:R16, bank, 0:P], ALU.add)
                if r.kind == "degree":
                    dst = aux[:, bass.ds(base, P)]
                    dve.tensor_tensor(dst, dst, PS[:, 2 + bank, 0:P], ALU.add)
                if r.kind == "gat":
                    dst = aux[0:2 * HEADS, bass.ds(base, P)]
                    dve.tensor_tensor(dst, dst, PS[0:2 * HEADS, 2 + bank, 0:P], ALU.add)
                dst = sums[:, bass.ds(base, P)]
                return dve.tensor_tensor(dst, dst, PS[:, bank, 0:P], ALU.add)

            def add_tiles(r, k, b, ready=(), meta_k=None):
                flag, base = meta_k or meta_of(dve, k, 0, 2)
                with dve.If(flag > 0):
                    for s, v in ready:
                        dve.wait_ge(s, v)
                    dve.wait_ge(r.agg_ready, k * G + (TWO + G))
                    dve.wait_ge(r.agg_free, k * G + TWO)
                    add_window(r, base, b).then_inc(r.agg_free, G)
                with dve.Else():
                    bases = meta_of(dve, k, META - G, G)
                    for s, v in ready:
                        dve.wait_ge(s, v)
                    for j in range(G):
                        dve.wait_ge(r.agg_ready, k * G + (TWO + j + 1))
                        dve.wait_ge(r.agg_free, k * G + (TWO + j))
                        add_window(r, bases[j], b).then_inc(r.agg_free, 1)

            def one_hot(r, k, b):
                dve.wait_ge(r.agg_ready, k * G + G)
                dve.tensor_tensor(OH[:, b, :].rearrange("p (j d) -> p j d", j=G), mid(iota_f[:, :], G),
                                  last(local[:, bass.ds(k * G, G)], P), ALU.is_equal).then_inc(r.oh_ready, 1)

            def sum_round(r):
                with dve.Fori(0, BATCHES // 2) as i:
                    for b in range(2):
                        k = 2 * i + b
                        one_hot(r, k, b)
                        add_tiles(r, k, b)

            def layer_norm(st, i, d, p, s):
                dve.wait_ge(st.pe, st.pe_at(i, p + 1))
                dve.tensor_tensor(T2, T1, PS[:, 5 if st is n_l1 else 1, 0:CHUNK], ALU.subtract).then_inc(st.dve, 1)
                dve.wait_ge(st.dve, st.dve_at(i, d + 1))
                dve.tensor_tensor(T3, T2, T2, ALU.mult).then_inc(st.dve, 1)
                dve.wait_ge(st.act, st.act_at(i, s + 1))
                dve.reciprocal(T5, T4).then_inc(st.dve, 1)
                dve.wait_ge(st.dve, st.dve_at(i, d + 3))
                return dve.tensor_tensor

            dve.wait_ge(scratch, 64)
            dve.wait_ge(base_in, 48)
            dve.memset(sums, 0.0)
            dve.memset(aux[0:R16, :], 0.0)
            copy_table(t_l0a)
            with dve.Fori(0, BATCHES // 2) as i:
                for b in range(2):
                    k = 2 * i + b
                    dve.wait_ge(count.agg_ready, k * G + G)
                    dve.tensor_tensor(oh16(b), mid(iota_f[:, :], G), last(local[:, bass.ds(k * G, G)], P), ALU.is_equal)
                    dve.tensor_tensor(OHR[:, b, :, :], mid(iota_f[:, 0:R16], G), last(etype[:, bass.ds(k * G, G)], R16),
                                      ALU.is_equal).then_inc(count.oh_ready, 1)
                    add_tiles(count, k, b)
            dve.wait_ge(count.agg_free, TWO + TILES)
            dve.tensor_scalar(aux[0:R16, :], aux[0:R16, :], 1.0, None, ALU.max).then_inc(rt_ready, 1)
            dve.wait_ge(rt_ready, 1)
            dve.reciprocal(aux[0:R16, :], aux[0:R16, :]).then_inc(rt_ready, 1)
            with dve.Fori(0, BATCHES // 2) as i:
                for b in range(2):
                    k = 2 * i + b
                    dve.wait_ge(et_in[b], (i + 1) * 16)
                    dve.tensor_scalar(ETR[:, b, :], ETR[:, b, :], pidx[0:R16, 0:1], None, ALU.is_equal).then_inc(et_hot, 1)
                    dve.wait_ge(r_l0a.agg_ready, k * G + G)
                    for j in range(G):
                        n = k * G + j
                        dve.wait_ge(look_ready, n + 1)
                        dve.scalar_tensor_tensor(oh(b, j), iota_f[:, :], local[:, bass.ds(n, 1)], PS[:, 4 + j % LOOKS, 0:P],
                                                 ALU.is_equal, ALU.mult, accum_out=wstage[:, b, j:j + 1]).then_inc(look_free, 1)
                    dve.wait_ge(look_free, k * G + (LOOKS + G))
                    dve.tensor_copy(wcol[:, bass.ds(k * G, G)], wstage[:, b, :]).then_inc(w_added, 1)
                    add_tiles(r_l0a, k, b)
            with dve.Fori(0, CHUNKS) as i:
                st, cs = n_l0a, bass.ds(i * CHUNK, CHUNK)
                dve.wait_ge(st.pe, st.pe_at(i, 1))
                dve.scalar_tensor_tensor(T0, PS[:, 0, 0:CHUNK], vec("L0_gnn_b1"), sums[:, cs], ALU.add, ALU.add).then_inc(st.dve, 1)
                dve.wait_ge(st.dve, st.dve_at(i, 1))
                dve.tensor_scalar(H[:, cs], T0, 0.0, None, ALU.max).then_inc(st.dve, 1)
            copy_table(t_l0b)
            dve.wait_ge(t_l0b.zeroed, 1)
            dve.wait_ge(w_added, BATCHES)
            with dve.Fori(0, BATCHES // 2) as i:
                for b in range(2):
                    k = 2 * i + b
                    dve.wait_ge(r_l0b.agg_ready, k * G + G)
                    for j in range(G):
                        n = k * G + j
                        ins = dve.tensor_scalar(oh(b, j), iota_f[:, :], local[:, bass.ds(n, 1)], wcol[:, bass.ds(n, 1)],
                                                ALU.is_equal, ALU.mult)
                    ins.then_inc(r_l0b.oh_ready, 1)
                    add_tiles(r_l0b, k, b)
            with dve.Fori(0, CHUNKS) as i:
                st, cs = n_l0b, bass.ds(i * CHUNK, CHUNK)
                dve.wait_ge(st.pe, st.pe_at(i, 1))
                dve.scalar_tensor_tensor(T0, PS[:, 0, 0:CHUNK], vec("L0_gnn_b2"), sums[:, cs], ALU.add, ALU.add).then_inc(st.dve, 1)
                dve.wait_ge(st.dve, st.dve_at(i, 1))
                dve.tensor_tensor(T1, T0, X[:, cs], ALU.add).then_inc(st.dve, 1)
                layer_norm(st, i, 2, 1, 0)
                dve.tensor_tensor(X[:, cs], T2, T5, ALU.mult).then_inc(st.dve, 1)
            copy_table(t_gat)
            dve.wait_ge(t_gat.zeroed, 3)

            for b in range(2):
                dve.wait_ge(t_gat.stored[b], 16 * (BLOCKS // 2))
            dve.wait_ge(seg_in, 16)

            dve.wait_ge(t_gat.out_a, 2 + BLOCKS)
            logits = LOGITS.rearrange("p (k h) -> p k h", h=NL)
            dve.tensor_copy(SPLIT[:, :, 0, :], logits).then_inc(split, 1)
            for n in range(2):
                dve.wait_ge(split, 2 * n + 1)
                dve.tensor_tensor(logits, logits, SPLIT[:, :, n, :], ALU.subtract).then_inc(split, 1)
                dve.wait_ge(split, 2 * n + 2)
                dve.tensor_copy(SPLIT[:, :, n + 1, :], logits).then_inc(split, 1)

            def one_hot_gat(k, c):
                dve.tensor_tensor(oh_gat(c), mid(iota_f[:, :], G), last(local[:, bass.ds(k * G, G)], P),
                                  ALU.is_equal).then_inc(r_gat.oh_ready, 1)

            def target_logits(k, b):
                look = PS[:, 6, 0:3 * NL * G].rearrange("p (j s h) -> p j s h", j=G, s=3)
                dve.wait_ge(g_look, k + 1)
                dve.tensor_copy(AD[:, b, :, :], look[:, :, 0, :]).then_inc(g_dve_ahead, 1)
                for n in (1, 2):
                    dve.wait_ge(g_dve_ahead, 3 * k + n)
                    dve.tensor_tensor(AD[:, b, :, :], AD[:, b, :, :], look[:, :, n, :], ALU.add).then_inc(g_dve_ahead, 1)

            def attend(i, c):
                k, b = 4 * i + c, c % 2
                r = r_gat

                def own(step):
                    dve.wait_ge(g_dve, at(G_DVE, k, step))

                rows = GB[:, b, :].rearrange("p (j w) -> p j w", w=GATW)
                s_logit = rows[:, :, P:GATW]
                t_logit, loop_logit = AD[:, b, :, 0:HEADS], AD[:, b, :, HEADS:2 * HEADS]
                row, row_f, row_b = (ROW[:, n, :] for n in range(3))
                final_first, final_last = row_b[:, 0::SLOTS], row_b[:, SLOTS - 1::SLOTS]
                dve.wait_ge(g_pen, k + 2)
                dve.wait_ge(g_dve_ahead, 3 * (k + 1))
                dve.wait_ge(r.gathered[b], 2 * (16 * G) * i + (c // 2 + 1) * (16 * G))
                dve.tensor_tensor(XS[:, :, :].rearrange("p h j -> p j h"), s_logit, loop_logit, ALU.max).then_inc(g_dve, 1)
                dve.tensor_tensor(ZL[:, 0], s_logit, t_logit, ALU.add).then_inc(g_dve, 1)
                dve.tensor_tensor(ZL[:, 1], loop_logit, t_logit, ALU.add).then_inc(g_dve, 1)
                dve.wait_ge(g_pe, at(G_PE, k, "xs_rows"))
                dve.tensor_tensor_scan(local_max, PEN[:, b, 0:P], PS[0:TH, 4, 0:P], -BIG, ALU.add, ALU.max).then_inc(g_dve, 1)
                own("local")
                dve.tensor_tensor_scan(seg_max[:, ::-1], PEN[:, b, 1:P + 1][:, ::-1], local_max[:, ::-1], -BIG,
                                       ALU.add, ALU.max).then_inc(g_dve, 1)
                one_hot_gat(k + 2, (c + 2) % 4)
                dve.wait_ge(g_cuts, k + 1)
                dve.wait_ge(g_act, at(G_ACT, k, "row"))
                dve.scalar_tensor_tensor(row[:, 0::SLOTS], CARRY[:, :], SEG[:, bass.ds(k, 1), 0], row[:, 0::SLOTS],
                                         ALU.add, ALU.max).then_inc(g_dve, 1)
                own("first")
                dve.tensor_tensor_scan(row_f, CUTS[:, b, 0:HEADS * SLOTS], row, -BIG, ALU.add, ALU.max).then_inc(g_dve, 1)
                own("row")
                dve.tensor_tensor_scan(row_b[:, ::-1], CUTS[:, b, 1:HEADS * SLOTS + 1][:, ::-1], row_f[:, ::-1], -BIG,
                                       ALU.add, ALU.max).then_inc(g_dve, 1)
                dve.wait_ge(g_pe, at(G_PE, k, "ends"))
                dve.tensor_copy(ENDM[:, :], PS[0:TH, 5, P:P + 2]).then_inc(g_dve, 1)
                dve.tensor_tensor(RZ[:, 0], CARRY[:, :], final_first, ALU.min).then_inc(g_dve, 1)
                own("ends")
                dve.tensor_tensor_scan(from_before, PEN[:, b, 0:P], seg_max, ENDM[:, 0:1], ALU.add, ALU.max).then_inc(g_dve, 1)
                dve.tensor_copy(RZ[:, 1], final_first).then_inc(g_dve, 1)
                own("forward")
                dve.tensor_tensor_scan(all_max[:, ::-1], PEN[:, b, 1:P + 1][:, ::-1], from_before[:, ::-1], ENDM[:, 1:2],
                                       ALU.add, ALU.max).then_inc(g_dve, 1)
                own("old")
                dve.tensor_copy(CARRY[:, :], final_last).then_inc(g_dve, 1)
                if not (isinstance(i, int) and c == 0):
                    meta_before = meta_of(dve, k - 1, 0, 2)
                base, = meta_of(dve, k, 1, 1)

                def shifted(n, before):
                    own(before)
                    dve.tensor_tensor(RZ[:, :, :], RZ[:, :, :], mid(AW[0:1, b, 0, n, 0:HEADS], 2), ALU.add).then_inc(g_dve, 1)

                dve.wait_ge(g_pe, at(G_PE, k, "maxima"))
                dve.tensor_tensor(ZL[:, 2], PS[:, 4, 0:TH].rearrange("p (h j) -> p j h", h=HEADS), t_logit,
                                  ALU.add).then_inc(g_dve, 1)
                shifted(0, "new")
                own("max_logit")
                z = ZL[:, :, :, :].rearrange("p t j h -> p (t j h)")
                dve.scalar_tensor_tensor(z, z, SLOPE, z, ALU.mult, ALU.max).then_inc(g_dve, 1)
                shifted(1, "logit_a")
                own("lrelu")
                zf = ZL[:, :, :, :].rearrange("p t j h -> p t (j h)")
                dve.tensor_tensor(ZD[:, :, :, :].rearrange("p t j h -> p t (j h)"), zf[:, 0:2], mid(zf[:, 2], 2),
                                  ALU.subtract).then_inc(g_dve, 1)
                shifted(2, "logit_b")
                own("scaled_logits")
                dve.scalar_tensor_tensor(RL[:, :, :], RZ[:, :, :], SLOPE, RZ[:, :, :], ALU.mult, ALU.max).then_inc(g_dve, 1)
                own("scaled_lrelu")
                dve.tensor_tensor(RD[:, :], RL[:, 0], RL[:, 1], ALU.subtract).then_inc(g_dve, 1)
                dve.wait_ge(g_act, at(G_ACT, k, "weights"))
                dve.tensor_tensor(WE[:, b, :, 1, :], WE[:, b, :, 1, :], last(start[:, bass.ds(k * G, G)], HEADS), ALU.mult)\
                    .then_inc(g_dve, 1)
                dve.tensor_tensor(M[:, b, :, :].rearrange("p j (h c) -> p j h c", c=HD),
                                  rows[:, :, 0:P].rearrange("p j (h c) -> p j h c", c=HD),
                                  WE[:, b, :, 0, :].unsqueeze(3).to_broadcast([P, G, HEADS, HD]), ALU.mult).then_inc(g_dve, 1)
                target_logits(k + 1, 1 - b)
                dve.wait_ge(g_pe, at(G_PE, k, "scale"))
                dve.tensor_copy(RS[:, 0:2], PS[:, 5, 256:260:2]).then_inc(g_dve, 1)
                if not (isinstance(i, int) and c == 0):
                    add_tiles(r, k - 1, 1 - b, [(g_dve, at(G_DVE, k - 1, "aux"))], meta_before)
                    dve.wait_ge(r.agg_free, k * G + TWO)
                own("scale")
                dve.tensor_scalar(sums[:, bass.ds(base, 1)], sums[:, bass.ds(base, 1)], RS[:, 0:1], None, ALU.mult)\
                    .then_inc(g_dve, 1)
                dve.tensor_scalar(aux[0:2 * HEADS, bass.ds(base, 1)], aux[0:2 * HEADS, bass.ds(base, 1)],
                                  RS[0:2 * HEADS, 1:2], None, ALU.mult).then_inc(g_dve, 1)

            one_hot_gat(0, 0)
            one_hot_gat(1, 1)
            target_logits(0, 0)
            for c in range(4):
                attend(0, c)
            with dve.Fori(1, BATCHES // 4) as i:
                for c in range(4):
                    attend(i, c)
            dve.wait_ge(g_dve, at(G_DVE, BATCHES - 1, "aux"))
            add_tiles(r_gat, BATCHES - 1, 1)

            with dve.Fori(0, CHUNKS) as i:
                st, cs = n_l1, bass.ds(i * CHUNK, CHUNK)
                dve.wait_ge(st.pe, st.pe_at(i, 1))
                dve.wait_ge(st.act, st.act_at(i, 1))
                dve.tensor_tensor(T1, PS[:, 3, 0:CHUNK], T0, ALU.mult).then_inc(st.dve, 1)
                dve.tensor_scalar(T3, PS[:, 1, 0:CHUNK], 1e-30, None, ALU.max).then_inc(st.dve, 1)
                dve.wait_ge(st.dve, st.dve_at(i, 2))
                dve.tensor_tensor(T2, T1, sums[:, cs], ALU.add).then_inc(st.dve, 1)
                dve.reciprocal(T5, T3).then_inc(st.dve, 1)
                dve.wait_ge(st.dve, st.dve_at(i, 4))
                dve.tensor_tensor(T1, T2, T5, ALU.mult).then_inc(st.dve, 1)
                dve.wait_ge(st.dve, st.dve_at(i, 5))
                dve.tensor_scalar(T3, T1, vec("L1_gnn_gat_bias"), None, ALU.add).then_inc(st.dve, 1)
                dve.wait_ge(st.pe, st.pe_at(i, 2))
                dve.tensor_scalar(T1, PS[:, 4, 0:CHUNK], vec("L1_gnn_proj_b"), None, ALU.add).then_inc(st.dve, 1)
                layer_norm(st, i, 7, 2, 1)
                dve.tensor_tensor(T0, T2, T5, ALU.mult).then_inc(st.dve, 1)
                dve.wait_ge(st.dve, st.dve_at(i, 11))
                dve.tensor_scalar(T2, T0, vec("L1_gnn_ln_gamma"), vec("L1_gnn_ln_beta"), ALU.mult, ALU.add).then_inc(st.dve, 1)
                dve.wait_ge(st.dve, st.dve_at(i, 12))
                dve.tensor_tensor(T1, T2, X[:, cs], ALU.add).then_inc(st.dve, 1)
                layer_norm(st, i, 13, 4, 2)
                dve.tensor_tensor(X[:, cs], T2, T5, ALU.mult).then_inc(st.dve, 1)

            dve.wait_ge(basis_in, 16)
            for q in range(R8):
                for r in range(R8):
                    w = wcomp[:, r * R8 + q:r * R8 + q + 1]
                    to, of = MIXED[:, r * P:(r + 1) * P], BASIS[:, q * P:(q + 1) * P]
                    if q == 0:
                        dve.tensor_scalar(to, of, w, None, ALU.mult).then_inc(mixed, 1)
                    else:
                        dve.wait_ge(mixed, (q - 1) * R8 + r + 1)
                        dve.scalar_tensor_tensor(to, of, w, to, ALU.mult, ALU.add).then_inc(mixed, 1)
            copy_table(t_l2)
            dve.wait_ge(t_l2.zeroed, 1)
            sum_round(r_l2)
            with dve.Fori(0, CHUNKS) as i:
                st, cs = n_l2a, bass.ds(i * CHUNK, CHUNK)
                dve.wait_ge(st.pe, st.pe_at(i, 1))
                dve.scalar_tensor_tensor(T0, PS[:, 0, 0:CHUNK], vec("L2_gnn_bias"), sums[:, cs], ALU.add, ALU.add).then_inc(st.dve, 1)
                dve.tensor_scalar(T1, PS[:, 1, 0:CHUNK], vec("L2_gnn_res_b"), 0.0, ALU.add, ALU.max).then_inc(st.dve, 1)
                dve.wait_ge(st.dve, st.dve_at(i, 2))
                dve.scalar_tensor_tensor(H[:, cs], T0, 0.0, T1, ALU.max, ALU.add).then_inc(st.dve, 1)
            dve.wait_ge(*n_l2a.end())
            for c in range(CHUNKS):
                w = min(CHUNK, NODES - c * CHUNK)
                dve.bn_stats(bn[:, c, :], H[:, c * CHUNK:c * CHUNK + w]).then_inc(norm_d, 1)
            dve.wait_ge(norm_d, 1 + CHUNKS)
            dve.bn_aggr(bnv[:, 0:2], bn[:, :, :].rearrange("p c s -> p (c s)")).then_inc(norm_d, 1)
            dve.wait_ge(norm_a, 1)
            dve.reciprocal(bnv[:, 3:4], bnv[:, 2:3]).then_inc(norm_d, 1)
            dve.wait_ge(norm_d, CHUNKS + 3)
            dve.tensor_tensor(bnv[:, 4:5], bnv[:, 3:4], vec("L2_gnn_bn_gamma"), ALU.mult).then_inc(norm_d, 1)
            dve.wait_ge(norm_d, CHUNKS + 4)
            dve.tensor_tensor(bnv[:, 5:6], bnv[:, 0:1], bnv[:, 4:5], ALU.mult).then_inc(norm_d, 1)
            dve.wait_ge(norm_d, CHUNKS + 5)
            dve.tensor_tensor(bnv[:, 6:7], vec("L2_gnn_bn_beta"), bnv[:, 5:6], ALU.subtract).then_inc(norm_d, 1)
            dve.wait_ge(norm_d, CHUNKS + 6)
            with dve.Fori(0, CHUNKS) as i:
                st, cs = n_l2b, bass.ds(i * CHUNK, CHUNK)
                dve.scalar_tensor_tensor(T0, H[:, cs], bnv[:, 4:5], X[:, cs], ALU.mult, ALU.add).then_inc(st.dve, 1)
                dve.wait_ge(st.dve, st.dve_at(i, 1))
                dve.tensor_scalar(T1, T0, bnv[:, 6:7], None, ALU.add).then_inc(st.dve, 1)
                layer_norm(st, i, 2, 0, 0)
                dve.tensor_tensor(X[:, cs], T2, T5, ALU.mult).then_inc(st.dve, 1)
            copy_table(t_l3a)
            dve.wait_ge(t_l3a.zeroed, 2)
            sum_round(r_l3a)
            dve.wait_ge(r_l3a.agg_free, TWO + TILES)
            dve.tensor_scalar(aux, aux, 1.0, None, ALU.max).then_inc(degree, 1)
            dve.wait_ge(degree, 1)
            dve.reciprocal(aux, aux).then_inc(degree, 1)
            dve.wait_ge(degree, 2)
            with dve.Fori(0, CHUNKS) as i:
                st, cs = n_l3a, bass.ds(i * CHUNK, CHUNK)
                dve.wait_ge(st.pe, st.pe_at(i, 1))
                dve.tensor_tensor(T0, sums[:, cs], aux[:, cs], ALU.mult).then_inc(st.dve, 1)
                dve.wait_ge(st.dve, st.dve_at(i, 1))
                dve.scalar_tensor_tensor(T1, PS[:, 0, 0:CHUNK], vec("L3_gnn_b1"), T0, ALU.add, ALU.add).then_inc(st.dve, 1)
                dve.wait_ge(st.dve, st.dve_at(i, 2))
                dve.tensor_scalar(H[:, cs], T1, 0.0, None, ALU.max).then_inc(st.dve, 1)
            copy_table(t_l3b)
            dve.wait_ge(t_l3b.zeroed, 1)
            sum_round(r_l3b)
            dve.wait_ge(r_l3b.agg_free, TWO + TILES)
            with dve.Fori(0, CHUNKS) as i:
                st, cs = n_l3b, bass.ds(i * CHUNK, CHUNK)
                dve.wait_ge(st.pe, st.pe_at(i, 1))
                dve.tensor_tensor(T0, sums[:, cs], aux[:, cs], ALU.mult).then_inc(st.dve, 1)
                dve.wait_ge(st.dve, st.dve_at(i, 1))
                dve.scalar_tensor_tensor(T2, PS[:, 0, 0:CHUNK], vec("L3_gnn_b2"), T0, ALU.add, ALU.add).then_inc(st.dve, 1)
                dve.wait_ge(st.dve, st.dve_at(i, 2))
                dve.tensor_tensor(T1, T2, X[:, cs], ALU.add).then_inc(st.dve, 1)
                layer_norm(st, i, 3, 1, 0)
                dve.tensor_tensor(X[:, cs], T2, T5, ALU.mult).then_inc(st.dve, 1)
            for n in range(N_XG):
                dve.wait_ge(out_ps, n + 1)
                w = min(512, XBLOCKS * P - 512 * n)
                dve.tensor_copy(H[:, 512 * n:512 * n + w], PS[:, n % 8, 0:w]).then_inc(out_sb, 1)


def kernel(**inputs):
    import numpy as _np
    import concourse.bacc as _bacc
    from concourse.bass_utils import run_bass_kernel_spmd as _run

    nc = _bacc.Bacc("TRN2", target_bir_lowering=False, num_devices=1)
    arrays, aps = {}, {}
    for name, value in inputs.items():
        v = _np.ascontiguousarray(value)
        arrays["in_" + name] = v
        aps[name] = nc.dram_tensor("in_" + name, v.shape, mybir.dt.from_np(v.dtype), kind="ExternalInput").ap()
    out = nc.dram_tensor("out_x", (NODES, P), FP32, kind="ExternalOutput").ap()
    build(nc, aps, out)
    r = _run(nc, [arrays], core_ids=[0])
    return r.results[0]["out_x"]
```

```python
import concourse.bass as bass
from concourse import mybir
from contextlib import ExitStack

FP32 = mybir.dt.float32
BF16 = mybir.dt.bfloat16
INT32 = mybir.dt.int32
ALU = mybir.AluOpType
ACT = mybir.ActivationFunctionType

P = 128
NODES = 6250
EDGES = 106250
R16, R8 = 16, 8
HEADS = 8
HD = P // HEADS
NODES_P = 6400
BLOCKS = NODES_P // P
CHUNK = 400
CHUNKS = NODES_P // CHUNK
META = 12
GROUP = 5
G = 8
TILES = 832
BATCHES = TILES // G
ROWB = 7
FULL = EDGES // P
REST = EDGES - FULL * P
XBLOCKS = (NODES + P - 1) // P
NO_NODE = float(1 << 20)
BIG = 1e30
GATW = P + HEADS
LN_EPS = 1e-5
SLOPE = 0.2


def mid(ap, n):
    return ap.unsqueeze(1).to_broadcast([ap.shape[0], n, ap.shape[1]])


def last(ap, n):
    return ap.unsqueeze(2).to_broadcast([ap.shape[0], ap.shape[1], n])


def build(nc, a, out):
    ctx = ExitStack()
    with ctx:
        ctx.enter_context(nc.allow_non_contiguous_dma(reason="columns of indices and of biases, once"))

        def sb(name, shape, dt=FP32):
            return ctx.enter_context(nc.sbuf_tensor(name, shape, dt))

        def sem(name):
            return ctx.enter_context(nc.semaphore(name))

        table16 = nc.dram_tensor("table16", [NODES_P * R16, P], FP32, kind="Internal").ap()
        table8 = nc.dram_tensor("table8", [NODES_P * R8, P], FP32, kind="Internal").ap()
        table_gat = nc.dram_tensor("table_gat", [NODES_P, GATW], FP32, kind="Internal").ap()
        table1 = nc.dram_tensor("table1", [NODES_P, P], FP32, kind="Internal").ap()
        node_logits = nc.dram_tensor("node_logits", [NODES_P, 3 * 2 * HEADS], BF16, kind="Internal").ap()
        flag_row = nc.dram_tensor("flag_row", [TILES], INT32, kind="Internal").ap()
        first_row = nc.dram_tensor("first_row", [TILES], INT32, kind="Internal").ap()
        etype_row = nc.dram_tensor("etype_row", [(TILES + G) * P], FP32, kind="Internal").ap()
        seg_row = nc.dram_tensor("seg_row", [TILES + G, 2], FP32, kind="Internal").ap()

        X = sb("X", [P, NODES_P])
        H = sb("H", [P, NODES_P])
        ACC = sb("ACC", [P, 2, NODES_P])
        sums, aux = ACC[:, 0, :], ACC[:, 1, :]
        WT = sb("WT", [P, 2048])
        WR = sb("WR", [P, 2112])
        TOUT = sb("TOUT", [P, 2, 2048])
        STG = sb("STG", [P, 2, P])
        iota_f = sb("iota_f", [P, P])
        pidx = sb("pidx", [P, 1])
        head_iota = sb("head_iota", [P, HEADS])
        ident = sb("ident", [P, P])
        mean_mat = sb("mean_mat", [P, P])
        center_mat = sb("center_mat", [P, P])
        ones_mat = sb("ones_mat", [P, P])
        local = sb("local", [P, ROWB * P])
        idx16 = sb("idx16", [P, ROWB * P], INT32)
        idx8 = sb("idx8", [P, ROWB * P], INT32)
        idx1 = sb("idx1", [P, ROWB * P], INT32)
        etype = sb("etype", [P, ROWB * P])
        start = sb("start", [P, ROWB * P])
        wcol = sb("wcol", [P, TILES])
        base_i = sb("base_i", [P, ROWB], INT32)
        prev_last = sb("prev_last", [P, ROWB], INT32)
        meta = sb("meta", [1, BATCHES + 1, META], INT32)
        sel_first = sb("sel_first", [P, P])
        sel_last = sb("sel_last", [P, P])
        batch_first = sb("batch_first", [P, P])
        ends = sb("ends", [P, 2, ROWB])
        bends = sb("bends", [P, 2, ROWB])
        spans = sb("spans", [P, 3, ROWB])
        seg = sb("seg", [P, ROWB, 2])
        flag_i = sb("flag_i", [P, ROWB], INT32)
        first_i = sb("first_i", [P, ROWB], INT32)
        rows_i = ACC[:, 0, 0:4 * ROWB * P].bitcast(INT32).rearrange("p (a b e) -> p a b e", a=4, b=ROWB)
        rows_f = ACC[:, 1, 0:7 * ROWB * P].rearrange("p (a b e) -> p a b e", a=7, b=ROWB)
        x_rows = H[:, 0:XBLOCKS * P].rearrange("p (b f) -> p b f", f=P)
        SRC, DST, ET16, ET8 = range(4)
        F_LOCAL, F_IDX16, F_IDX8, F_SRC, F_ET, F_START, F_PEN = range(7)

        OH = sb("OH", [P, 2, G * P])
        GB = sb("GB", [P, 2, G * GATW])
        IDX = sb("IDX", [P, 2, G], INT32)
        OHR = sb("OHR", [P, 2, G, R16], BF16)
        ETR = H[0:R16, 0:2 * G * P].rearrange("p (b e) -> p b e", b=2)
        wstage = sb("wstage", [P, 2, G])

        def oh(b, j):
            return OH[:, b, j * P:(j + 1) * P]

        def oh16(b):
            return OH[:, b, 0:G * P // 2].bitcast(BF16).rearrange("p (j d) -> p j d", j=G)

        TH = G * HEADS
        SLOTS = 2 * G
        M = TOUT[:, :, 0:G * P].rearrange("p b (j f) -> p b j f", j=G)
        OHT = TOUT[:, 0, G * P:3 * G * P // 2].bitcast(BF16).rearrange("p (j e) -> p j e", j=G)
        NL = 2 * HEADS
        SPLIT = WR[:, 0:3 * NL * BLOCKS // 2].bitcast(BF16).rearrange("p (k s h) -> p k s h", k=BLOCKS, s=3)
        LOGITS = WR[:, 3 * NL * BLOCKS // 2:5 * NL * BLOCKS // 2]
        AW = sb("AW", [P, 2, G, 3, 2 * HEADS], BF16)
        SEG = H[0:1, 0:(BATCHES + 1) * SLOTS].rearrange("o (k x) -> o k x", x=SLOTS)
        free = [(BATCHES + 1) * SLOTS]

        def of_h(rows, columns):
            free[0] += columns
            return H[0:rows, free[0] - columns:free[0]]

        PEN = of_h(TH, 2 * (P + 1)).rearrange("p (b e) -> p b e", b=2)
        scans = of_h(TH, 4 * P).rearrange("p (n e) -> p n e", n=4)
        local_max, seg_max, from_before, all_max = (scans[:, n, :] for n in range(4))
        OH_MORE = of_h(P, 2 * G * P).rearrange("p (b n) -> p b n", b=2)

        def oh_gat(c):
            return (OH[:, c, :] if c < 2 else OH_MORE[:, c - 2, :]).rearrange("p (j d) -> p j d", j=G)

        AD = of_h(P, 4 * G * HEADS).rearrange("p (b j h) -> p b j h", b=2, j=G)
        XS = sb("XS", [P, HEADS, G])
        starts = sb("starts", [P, HEADS, G])
        CUTS = sb("CUTS", [1, 2, HEADS * SLOTS + 1])
        ROW = sb("ROW", [1, 3, HEADS * SLOTS])
        CARRY = sb("CARRY", [1, HEADS])
        ENDM = sb("ENDM", [TH, 2])
        RZ = sb("RZ", [1, 2, HEADS])
        RL = sb("RL", [1, 2, HEADS])
        RD = sb("RD", [1, HEADS])
        RE = sb("RE", [1, P + 2 * HEADS])
        one = sb("one", [1, 1])
        unused = sb("unused", [1, 2])
        RS = sb("RS", [P, 2])
        ZL = sb("ZL", [P, 3, G, HEADS])
        ZD = sb("ZD", [P, 2, G, HEADS])
        WE = sb("WE", [P, 2, G, 2, HEADS])
        den_mat = sb("den_mat", [2 * HEADS, P])
        own_mat = sb("own_mat", [2 * HEADS, P])
        lin_cat = sb("lin_cat", [P, P + 3 * HEADS])
        cat_rhs = sb("cat_rhs", [P, P + 3 * HEADS])
        hsel = sb("hsel", [P, HEADS])
        shift = sb("shift", [P, 4])
        below = sb("below", [P, P])

        PAIRS = CHUNKS // 2
        T0, T1, T2, T3 = ([TOUT[:, h, n * CHUNK:(n + 1) * CHUNK] for h in range(2)] for n in range(4))
        T5 = [OH[:, h, 0:CHUNK] for h in range(2)]
        QUARTER = CHUNK // 4
        DEV = sb("DEV", [QUARTER, 2, 4])
        INV = sb("INV", [QUARTER, 2, 4])
        inv_degree = sb("inv_degree", [QUARTER, NODES_P // QUARTER])
        INVD = sb("INVD", [QUARTER, 2, 4])
        bn = sb("bn", [P, CHUNKS, 6])
        bnv = sb("bnv", [P, 8])
        eps = sb("eps", [P, 1])
        wcomp = sb("wcomp", [P, R8 * R8])

        MATS = ["L0_gnn_root1", "L0_gnn_root2", "L1_gnn_lin_w", "L1_gnn_proj_w", "L2_gnn_loop_w", "L2_gnn_res_w",
                "L3_gnn_W1_l", "L3_gnn_W1_r", "L3_gnn_W2_l", "L3_gnn_W2_r"]
        VECS = ["L0_gnn_b1", "L0_gnn_b2", "L1_gnn_gat_bias", "L1_gnn_proj_b", "L1_gnn_ln_gamma", "L1_gnn_ln_beta",
                "L2_gnn_bias", "L2_gnn_res_b", "L2_gnn_bn_gamma", "L2_gnn_bn_beta", "L3_gnn_b1", "L3_gnn_b2"]
        mats = sb("mats", [P, len(MATS), P])
        vecs = sb("vecs", [P, len(VECS) + 2])
        TURNED = ["L1_gnn_proj_w", "L3_gnn_W1_l", "L3_gnn_W1_r", "L3_gnn_W2_l", "L3_gnn_W2_r"]
        turned = sb("turned", [P, len(TURNED), P])

        def mat(name):
            return mats[:, MATS.index(name), :]

        def mat_t(name):
            return turned[:, TURNED.index(name), :]

        def vec(name):
            n = VECS.index(name)
            return vecs[:, n:n + 1]

        att_src, att_dst = (vecs[:, len(VECS) + n:len(VECS) + n + 1] for n in range(2))
        BASIS, MIXED = WT[:, 0:R8 * P], WT[:, R8 * P:2 * R8 * P]

        PS = ctx.enter_context(nc.psum_tensor("PS", [P, 8, 512], FP32))

        pad_zero = sem("pad_zero")
        cleared = sem("cleared")
        rows_in = sem("rows_in")
        meta_out = sem("meta_out")
        base_in = sem("base_in")
        ends_ps = sem("ends_ps")
        x_in = sem("x_in")
        w_in = sem("w_in")
        w2_in = sem("w2_in")
        basis_in = sem("basis_in")
        scratch = sem("scratch")
        seg_in = sem("seg_in")
        prep = sem("prep")
        turn_ps = sem("turn_ps")
        turn_sb = sem("turn_sb")
        mixed = sem("mixed")
        out_ps = sem("out_ps")
        out_sb = sem("out_sb")
        out_done = sem("out_done")

        class Table:

            def __init__(self, name, source, weights, dram, ready):
                self.source, self.weights, self.dram = source, weights, dram
                self.width = weights.shape[1]
                self.rows = dram.shape[0] // NODES_P
                self.part = dram.shape[1] if self.width <= 512 else self.width // 2
                self.banks = 4 if dram is not table16 or source is H else 0
                self.group = GROUP if self.width <= 512 else 1
                self.stores = BLOCKS // self.group // 2
                self.ready = ready
                self.staged = sem(name + "_staged")
                self.made = sem(name + "_made")
                self.out_a = sem(name + "_out_a")
                self.out_d = sem(name + "_out_d")
                self.stored = [sem(f"{name}_stored{b}") for b in range(2)]
                self.zeroed = sem(name + "_zeroed")

        class Round:

            def __init__(self, name, kind, idx=None, table=None):
                self.kind, self.idx, self.table = kind, idx, table
                self.width = table.dram.shape[1] if table else 0
                if table:
                    self.idx_staged = sem(name + "_idx_staged")
                    self.begun = sem(name + "_begun")
                    self.gathered = [sem(f"{name}_gathered{b}") for b in range(2)]
                self.oh_ready = sem(name + "_oh_ready")
                self.agg_ready = sem(name + "_agg_ready")
                self.agg_free = sem(name + "_agg_free")

        TWO = 2 * G
        LOOKS = 4

        class Stage:

            def __init__(self, name, dve, pe, act):
                self.n_dve, self.n_pe, self.n_act = dve, pe, act
                self.dve, self.pe = sem(name + "_dve"), sem(name + "_pe")
                self.act = sem(name + "_act") if act else None

            def dve_at(self, i, k, h=1):
                return i * (2 * self.n_dve) + (2 * k + h)

            def pe_at(self, i, k, h=1):
                return i * (2 * self.n_pe) + (2 * k + h)

            def act_at(self, i, k, h=1):
                return i * (2 * self.n_act) + (2 * k + h)

            def end(self):
                return (self.dve, self.dve_at(PAIRS, 0))

        def chunk(i, h):
            return bass.ds(i * (2 * CHUNK) + h * CHUNK, CHUNK)

        def bank(n, h):
            return PS[:, 4 * h + n, 0:CHUNK]

        n_l0a = Stage("n_l0a", 2, 1, 0)
        n_l0b = Stage("n_l0b", 4, 4, 3)
        n_l1 = Stage("n_l1", 10, 8, 10)
        n_l2a = Stage("n_l2a", 3, 1, 0)
        n_l2b = Stage("n_l2b", 4, 3, 3)
        n_l3a = Stage("n_l3a", 3, 1, 1)
        n_l3b = Stage("n_l3b", 5, 4, 4)
        norm_d = sem("norm_d")
        norm_a = sem("norm_a")
        degree_ps = sem("degree_ps")
        degree = sem("degree")

        N_COLS, N_XG, N_MATG, N_LIN = 6, (XBLOCKS + 3) // 4, 2, 1
        TURNS = N_COLS + N_XG + N_MATG + N_LIN

        t_l0a = Table("t_l0a", X, WT[:, :], table16, [(turn_sb, TURNS)])
        t_l0b = Table("t_l0b", H, WR[:, 0:2048], table16, [n_l0a.end(), (w2_in, 16)])
        t_gat = Table("t_gat", X, lin_cat[:, :], table_gat, [n_l0b.end()])
        t_l2 = Table("t_l2", X, MIXED, table8, [n_l1.end(), (mixed, R8 * R8)])
        t_l3a = Table("t_l3a", X, mat_t("L3_gnn_W1_l"), table1, [n_l2b.end()])
        t_l3b = Table("t_l3b", H, mat_t("L3_gnn_W2_l"), table1, [n_l3a.end()])
        count = Round("count", "count")
        r_l0a = Round("r_l0a", "weigh", idx16, t_l0a)
        r_l0b = Round("r_l0b", "weighted", idx16, t_l0b)
        r_gat = Round("r_gat", "gat", idx1, t_gat)
        r_l2 = Round("r_l2", "sum", idx8, t_l2)
        r_l3a = Round("r_l3a", "sum", idx1, t_l3a)
        r_l3b = Round("r_l3b", "sum", idx1, t_l3b)

        et_in = [sem(f"et_in{b}") for b in range(2)]
        et_hot = sem("et_hot")
        looking = sem("looking")
        look_ready = sem("look_ready")
        look_free = sem("look_free")
        rt_ready = sem("rt_ready")
        w_added = sem("w_added")

        g_in = [sem(f"g_in{b}") for b in range(2)]
        split = sem("split")
        logits_out = sem("logits_out")
        g_starts = sem("g_starts")
        g_dve_ahead = sem("g_dve_ahead")
        g_cuts = sem("g_cuts")
        g_turned_ps = sem("g_turned_ps")
        g_turned = sem("g_turned")
        g_look = sem("g_look")
        g_pen = sem("g_pen")
        g_passed = sem("g_passed")
        g_dve, g_pe, g_act = sem("g_dve"), sem("g_pe"), sem("g_act")
        G_DVE = ("xs", "edge_logit", "own_logit", "local", "segment", "first", "row", "row_back", "ends", "old",
                 "forward", "new", "back", "carry", "max_logit", "logit_a", "lrelu", "logit_b", "diff", "scaled_logits",
                 "scaled_lrelu", "scaled_diff", "own", "m", "scale", "sums", "aux")
        G_PE = ("xs_rows", "row", "ends", "maxima", "scale")
        G_ACT = ("row", "weights", "scale", "scale2")

        def at(steps, k, step):
            return (k + 2) * len(steps) + (steps.index(step) + 1)

        XFER = {DST: a["dst"], SRC: a["src"], ET16: a["edge_type_16"], ET8: a["edge_type_8"]}
        WHOLE = (ROWB - 1) * P * P
        TAIL = FULL - (ROWB - 1) * P
        N_ROWS_IN = 3 * len(XFER) + 6
        N_W_IN = 1 + len(MATS) + len(VECS) + 2 + 1
        N_PREP = 22 + 19
        ENDS = 22
        LAST_ROWS = NODES - (XBLOCKS - 1) * P

        def meta_of(engine, k, at, n):
            _, values = nc.values_load_multi_w_load_instructions(meta[0:1, bass.ds(k, 1), at:at + n].rearrange("o k m -> o (k m)"),
                                                                 engines=[engine.engine], min_val=0, max_val=NODES - 1)
            return values

        block = ctx.enter_context(nc.Block())

        @block.sync
        def _(sp):
            sp.wait_ge(cleared, 1)
            for n, v in XFER.items():
                sp.dma_start(rows_i[:, n, 0:ROWB - 1, :],
                             v[0:WHOLE].rearrange("(b t e) -> t b e", t=P, e=P)).then_inc(rows_in, 16)
                sp.dma_start(rows_i[0:TAIL, n, ROWB - 1, :],
                             v[WHOLE:FULL * P].rearrange("(t e) -> t e", e=P)).then_inc(rows_in, 16)
                sp.dma_start(rows_i[TAIL:TAIL + 1, n, ROWB - 1, 0:REST],
                             v[FULL * P:EDGES].rearrange("(t e) -> t e", t=1)).then_inc(rows_in, 16)
            dst = a["dst"]
            whole = dst[0:WHOLE].rearrange("(b t e) -> t b e", t=P, e=P)
            tail = dst[WHOLE:FULL * P].rearrange("(t e) -> t e", e=P)
            sp.dma_start(base_i[:, 0:ROWB - 1], whole[:, :, 0]).then_inc(rows_in, 16)
            sp.dma_start(base_i[0:TAIL, ROWB - 1:ROWB], tail[:, 0:1]).then_inc(rows_in, 16)
            sp.dma_start(base_i[TAIL:TAIL + 1, ROWB - 1:ROWB],
                         dst[FULL * P:FULL * P + 1].rearrange("(t e) -> t e", t=1)).then_inc(rows_in, 16)
            sp.dma_start(prev_last[1:P, 0:ROWB - 1], whole[0:P - 1, :, P - 1]).then_inc(rows_in, 16)
            sp.dma_start(prev_last[0:1, 1:ROWB], whole[P - 1:P, :, P - 1]).then_inc(rows_in, 16)
            sp.dma_start(prev_last[1:TAIL + 1, ROWB - 1:ROWB], tail[:, P - 1:P]).then_inc(rows_in, 16)
            sp.dma_start(x_rows[:, 0:XBLOCKS - 1, :],
                         a["x"][0:(XBLOCKS - 1) * P, :].rearrange("(b p) f -> p b f", p=P)).then_inc(x_in, 16)
            sp.dma_start(x_rows[0:LAST_ROWS, XBLOCKS - 1, :], a["x"][(XBLOCKS - 1) * P:NODES, :]).then_inc(x_in, 16)
            sp.wait_ge(prep, N_PREP)
            n = TILES + G - (ROWB - 1) * P
            sp.dma_start(etype_row[0:WHOLE].rearrange("(b t e) -> t b e", t=P, e=P),
                         rows_f[:, F_ET, 0:ROWB - 1, :]).then_inc(scratch, 16)
            sp.dma_start(etype_row[WHOLE:(TILES + G) * P].rearrange("(t e) -> t e", e=P),
                         rows_f[0:n, F_ET, ROWB - 1, :]).then_inc(scratch, 16)
            sp.dma_start(seg_row[0:(ROWB - 1) * P, :].rearrange("(b t) a -> t b a", t=P),
                         seg[:, 0:ROWB - 1, :]).then_inc(scratch, 16)
            sp.dma_start(seg_row[(ROWB - 1) * P:TILES + G, :], seg[0:n, ROWB - 1, :]).then_inc(scratch, 16)
            for dram, col in ((flag_row, flag_i), (first_row, first_i)):
                sp.dma_start(dram[0:(ROWB - 1) * P].rearrange("(b t) -> t b", t=P), col[:, 0:ROWB - 1]).then_inc(meta_out, 16)
                sp.dma_start(dram[(ROWB - 1) * P:TILES].rearrange("(t o) -> t o", o=1),
                             col[0:TILES - (ROWB - 1) * P, ROWB - 1:ROWB]).then_inc(meta_out, 16)
            sp.wait_ge(meta_out, 64)
            sp.dma_start(meta[0:1, 0:BATCHES, 0:1], flag_row.rearrange("(o k j) -> o k j", o=1, j=G)[:, :, 0:1]).then_inc(base_in, 16)
            sp.dma_start(meta[0:1, 0:BATCHES, 1:2], first_row.rearrange("(o k j) -> o k j", o=1, j=G)[:, :, 0:1]).then_inc(base_in, 16)
            sp.dma_start(meta[0:1, 1:BATCHES + 1, 2:3], flag_row.rearrange("(o k j) -> o k j", o=1, j=G)[:, :, 0:1]).then_inc(base_in, 16)
            sp.dma_start(meta[0:1, 1:BATCHES + 1, 3:4], first_row.rearrange("(o k j) -> o k j", o=1, j=G)[:, :, 0:1]).then_inc(base_in, 16)
            sp.dma_start(meta[0:1, 0:BATCHES, META - G:META], first_row.rearrange("(o k j) -> o k j", o=1, j=G)).then_inc(base_in, 16)

            def store_table(t):
                wide = t.dram.shape[1] * t.rows
                with sp.Fori(0, t.stores) as i:
                    for b in range(2):
                        group = 2 * i + b
                        sp.wait_ge(t.out_a, group * t.group + (t.group + 2))
                        if t.width > 512:
                            sp.wait_ge(t.out_d, group + 3)
                        rows = t.group * P * t.rows
                        sp.dma_start(t.dram[bass.ds(group * rows, rows), :]
                                     .rearrange("(n p r) f -> p n (r f)", n=t.group, r=t.rows),
                                     TOUT[:, b, 0:t.group * wide].rearrange("p (n f) -> p n f", n=t.group)).then_inc(t.stored[b], 16)

            store_table(t_l0a)
            sp.wait_ge(t_l0a.made, 2 + BLOCKS)
            sp.dma_start(BASIS.rearrange("d (r h) -> d r h", r=R8),
                         a["L2_gnn_basis_w"].rearrange("r d h -> d r h")).then_inc(basis_in, 16)
            sp.wait_ge(scratch, 64)
            def relations(k, b):
                sp.wait_ge(r_l0a.agg_ready, k * G + G)
                sp.dma_start(ETR[:, b, :], etype_row[bass.ds(k * (G * P), G * P)].unsqueeze(0)
                             .to_broadcast([R16, G * P])).then_inc(et_in[b], 16)

            with sp.Fori(0, BATCHES // 2) as i:
                for b in range(2):
                    relations(2 * i + b, b)
            relations(BATCHES, 0)
            store_table(t_l0b)
            store_table(t_gat)
            sp.wait_ge(*n_l0b.end())
            sp.dma_start(SEG, seg_row.rearrange("(o k j) a -> o k (j a)", o=1, j=G)).then_inc(seg_in, 16)
            sp.wait_ge(split, 5)
            sp.dma_start(node_logits.rearrange("(k p) c -> p k c", p=P), SPLIT.rearrange("p k s h -> p k (s h)"))\
                .then_inc(logits_out, 16)
            sp.wait_ge(logits_out, 16)

            def windows(k, b):
                flag, base = meta_of(sp, k, 0, 2)
                sp.wait_ge(g_dve, at(G_DVE, k - 2, "scaled_logits"))
                sp.dma_start(AW[:, b, 0, :, :].rearrange("p s h -> p (s h)"), node_logits[bass.ds(base, P), :]).then_inc(g_in[b], 16)
                with sp.If(flag > 0):
                    sp.sem_inc(g_in[b], 16 * (G - 1))
                with sp.Else():
                    bases = meta_of(sp, k, META - G, G)
                    for j in range(1, G):
                        sp.dma_start(AW[:, b, j, :, :].rearrange("p s h -> p (s h)"), node_logits[bass.ds(bases[j], P), :]).then_inc(g_in[b], 16)

            with sp.Fori(0, BATCHES // 2) as i:
                for b in range(2):
                    windows(2 * i + b, b)
            windows(BATCHES, 0)
            store_table(t_l2)
            store_table(t_l3a)
            store_table(t_l3b)
            sp.wait_ge(out_sb, N_XG)
            sp.dma_start(out[0:(XBLOCKS - 1) * P, :].rearrange("(b p) f -> p b f", p=P),
                         x_rows[:, 0:XBLOCKS - 1, :]).then_inc(out_done, 16)
            sp.dma_start(out[(XBLOCKS - 1) * P:NODES, :], x_rows[0:LAST_ROWS, XBLOCKS - 1, :]).then_inc(out_done, 16)
            sp.wait_ge(out_done, 32)

        @block.gpsimd
        def _(pool):
            pool.memset(rows_i[:, :, :, :], 0)
            pool.memset(base_i[:, :], 0)
            pool.memset(meta[:, :, :], 0)
            pool.iota(batch_first[:, :], [[G, P // G], [0, G]], base=0, channel_multiplier=0, allow_small_or_imprecise_dtypes=True)
            pool.memset(prev_last[:, :], -1)
            pool.memset(x_rows[:, XBLOCKS - 1, :], 0.0)
            pool.memset(X[:, XBLOCKS * P:NODES_P], 0.0)
            pool.iota(iota_f[:, :], [[1, P]], base=0, channel_multiplier=0, allow_small_or_imprecise_dtypes=True)
            pool.iota(pidx[:, :], [[0, 1]], base=0, channel_multiplier=1, allow_small_or_imprecise_dtypes=True)
            pool.iota(head_iota[:, :], [[HD, HEADS]], base=0, channel_multiplier=0, allow_small_or_imprecise_dtypes=True)
            pool.memset(mean_mat[:, :], 1.0 / P)
            pool.memset(ones_mat[:, :], 1.0)
            pool.memset(eps[:, :], LN_EPS)
            pool.memset(CARRY[:, :], -BIG)
            pool.memset(CUTS[:, :, :], -BIG)
            pool.memset(one[:, :], 1.0).then_inc(pad_zero, 1)
            pool.wait_ge(pad_zero, 1)
            pool.memset(rows_i[:, DST, ROWB - 1, :], int(NO_NODE)).then_inc(cleared, 1)

            def stage_table(t, zero):
                for s, n in t.ready:
                    pool.wait_ge(s, n)
                with pool.Fori(0, BLOCKS // 2) as i:
                    for b in range(2):
                        blk = 2 * i + b
                        pool.wait_ge(t.made, blk + 1)
                        pool.tensor_copy(STG[:, b, :], t.source[:, bass.ds(blk * P, P)]).then_inc(t.staged, 1)
                for z in zero:
                    pool.memset(z, 0.0).then_inc(t.zeroed, 1)

            def gather(r):
                for b in range(2):
                    pool.wait_ge(r.table.stored[b], 16 * r.table.stores)
                with pool.Fori(0, BATCHES // 2) as i:
                    for b in range(2):
                        k = 2 * i + b
                        pool.wait_ge(r.idx_staged, k + 1)
                        if r.kind == "gat":
                            pool.wait_ge(g_dve, at(G_DVE, k - 2, "m"))
                        else:
                            pool.wait_ge(r.agg_ready, k * G + G)
                        pool.sem_inc(r.begun, 1)
                        for j in range(G):
                            pool.indirect_dma_start(
                                out=GB[:, b, j * r.width:(j + 1) * r.width], out_offset=None,
                                in_=r.table.dram[:, :],
                                in_offset=bass.IndirectOffsetOnAxis(ap=IDX[:, b, j:j + 1], axis=0),
                            ).then_inc(r.gathered[b], 16)

            stage_table(t_l0a, [])
            gather(r_l0a)
            stage_table(t_l0b, [sums])
            gather(r_l0b)
            stage_table(t_gat, [sums, aux[0:2 * HEADS, :], PEN])
            gather(r_gat)
            stage_table(t_l2, [sums])
            gather(r_l2)
            stage_table(t_l3a, [sums])
            gather(r_l3a)
            stage_table(t_l3b, [sums])
            gather(r_l3b)

        @block.scalar
        def _(act):
            act.sem_inc(n_l0b.act, 1)
            act.sem_inc(n_l1.act, 1)
            act.sem_inc(n_l2b.act, 1)
            act.sem_inc(n_l3a.act, 1)
            act.sem_inc(n_l3b.act, 1)
            act.sem_inc(g_act, 2 * len(G_ACT))
            act.sem_inc(g_pen, 1)
            for t in (t_l0a, t_l0b, t_gat, t_l2, t_l3a, t_l3b):
                act.sem_inc(t.out_a, 2)
            act.dma_start(WT[:, :].rearrange("d (r h) -> d r h", r=R16),
                          a["L0_gnn_W1"].rearrange("r d h -> d r h")).then_inc(w_in, 16)
            for n, name in enumerate(MATS):
                act.dma_start(mats[:, n, :], a[name]).then_inc(w_in, 16)
            for n, name in enumerate(VECS):
                act.dma_start(vecs[:, n:n + 1], a[name].rearrange("(p o) -> p o", o=1)).then_inc(w_in, 16)
            for n, name in enumerate(("L1_gnn_att_src", "L1_gnn_att_dst")):
                act.dma_start(vecs[:, len(VECS) + n:len(VECS) + n + 1],
                              a[name].rearrange("o h (k u) -> (o h k) u", u=1)).then_inc(w_in, 16)
            act.dma_start(wcomp[:, :], a["L2_gnn_w_comp"].rearrange("r b -> (r b)").unsqueeze(0)
                          .to_broadcast([P, R8 * R8])).then_inc(w_in, 16)
            act.dma_start(WR[:, 0:2048].rearrange("d (r h) -> d r h", r=R16),
                          a["L0_gnn_W2"].rearrange("r d h -> d r h")).then_inc(w2_in, 16)

            def copy_table(t):
                def two_groups(i):
                    for n in range(2 * t.group):
                        blk, group, b = i * (2 * t.group) + n, n // t.group, n % 2
                        act.wait_ge(t.made, blk + 3)
                        if n % t.group == 0 and not isinstance(i, int):
                            act.wait_ge(t.stored[group], i * 16)
                        ps = PS[:, t.banks * b:t.banks * b + 4, :].rearrange("p a n -> p (a n)")
                        if t is t_gat:
                            act.copy(LOGITS[:, bass.ds(blk * NL, NL)], ps[:, GATW:GATW + NL])
                        at_column = n % t.group * t.part
                        act.copy(TOUT[:, group, at_column:at_column + t.part], ps[:, 0:t.part]).then_inc(t.out_a, 1)

                two_groups(0)
                with act.Fori(1, t.stores) as i:
                    two_groups(i)

            def stage_indices(r):
                with act.Fori(0, BATCHES // 2) as i:
                    for b in range(2):
                        k = 2 * i + b
                        act.wait_ge(r.agg_ready, k * G + G)
                        act.copy(IDX[:, b, :], r.idx[:, bass.ds(k * G, G)]).then_inc(r.idx_staged, 1)

            def variance(st, i, pe_step):
                for h in range(2):
                    act.wait_ge(st.pe, st.pe_at(i, pe_step, h))
                    act.activation(T3[h], bank(1, h), ACT.Square).then_inc(st.act, 1)
                for h in range(2):
                    act.copy(T5[h], bank(1, h)).then_inc(st.act, 1)
                for h in range(2):
                    act.wait_ge(st.pe, st.pe_at(i, pe_step + 1, h))
                    act.activation(DEV[:, h, :], bank(2, h)[0:QUARTER, 0:4], ACT.Sqrt, bias=eps[0:QUARTER, 0:1]).then_inc(st.act, 1)

            def load_root(n):
                act.activation(unused[:, n:n + 1], one[:, :], ACT.Sqrt)

            def stage_degrees(st, i):
                act.wait_ge(st.pe, st.pe_at(i, 0))
                for h in range(2):
                    act.copy(INVD[:, h, :], inv_degree[:, bass.ds(i * 8 + 4 * h, 4)]).then_inc(st.act, 1)

            def variances(st, pe_step):
                with act.Fori(0, PAIRS) as i:
                    variance(st, i, pe_step)

            act.wait_ge(turn_sb, TURNS)
            copy_table(t_l0a)
            stage_indices(r_l0a)
            copy_table(t_l0b)
            stage_indices(r_l0b)
            load_root(0)
            variances(n_l0b, 2)
            copy_table(t_gat)

            def starts_of(k, b):
                act.copy(starts[:, :, :], mid(start[:, bass.ds(k * G, G)], HEADS)).then_inc(g_starts, 1)
                act.copy(CUTS[:, b, 0:HEADS * SLOTS].rearrange("o (h x) -> o h x", x=SLOTS)[:, :, 1:SLOTS],
                         SEG[:, bass.ds(k, 1), 1:SLOTS].to_broadcast([1, HEADS, SLOTS - 1])).then_inc(g_cuts, 1)

            def turn(k):
                for h in range(2):
                    act.wait_ge(g_turned_ps, 2 * k + (1 + h))
                    act.copy(OHT[:, 4 * h:4 * h + 4, :].rearrange("p j e -> p (j e)"), PS[:, 6 + h, :]).then_inc(g_turned, 1)

            def penalties(k, b):
                act.wait_ge(g_look, k + 1)
                look = PS[:, 6, 0:3 * NL * G].rearrange("p (j s h) -> p j s h", j=G, s=3)
                act.copy(AD[:, b, :, :], look[:, :, 0, :])
                act.mul(PEN[:, b, 1:P], PS[0:TH, 7, 1:P], -BIG).then_inc(g_pen, 1)

            def attend(k, b):
                starts_of(k + 1, 1 - b)
                act.wait_ge(g_pe, at(G_PE, k, "row"))
                act.copy(ROW[:, 0, :].rearrange("o (x a) -> o a x", a=2),
                         PS[0:1, 5, 0:2 * TH].rearrange("o (a x) -> o a x", a=2)).then_inc(g_act, 1)
                turn(k + 1)
                penalties(k + 1, 1 - b)
                act.wait_ge(g_dve, at(G_DVE, k, "diff"))
                act.activation(WE[:, b, :, :, :].rearrange("p j t h -> p t j h"), ZD[:, :, :, :], ACT.Exp).then_inc(g_act, 1)
                act.wait_ge(g_dve, at(G_DVE, k, "scaled_diff"))
                act.activation(RE[:, 0:P].rearrange("o (h c) -> o h c", c=HD), last(RD[:, :], HD), ACT.Exp).then_inc(g_act, 1)
                act.activation(RE[:, P:P + 2 * HEADS].rearrange("o (t h) -> o t h", t=2), mid(RD[:, :], 2), ACT.Exp)\
                    .then_inc(g_act, 1)
                act.copy(IDX[:, b, :], r_gat.idx[:, bass.ds((k + 2) * G, G)]).then_inc(r_gat.idx_staged, 1)

            act.activation(RE[:, 0:1], one[:, :], ACT.Exp)
            act.wait_ge(seg_in, 16)
            act.wait_ge(t_gat.zeroed, 3)
            for k in range(2):
                act.copy(IDX[:, k, :], r_gat.idx[:, k * G:(k + 1) * G]).then_inc(r_gat.idx_staged, 1)
            starts_of(0, 0)
            turn(0)
            penalties(0, 0)
            with act.Fori(0, BATCHES // 2) as i:
                for b in range(2):
                    attend(2 * i + b, b)

            load_root(1)
            with act.Fori(0, PAIRS) as i:
                for h in range(2):
                    act.wait_ge(n_l1.pe, n_l1.pe_at(i, 1, h))
                    act.copy(T0[h], bank(0, h)).then_inc(n_l1.act, 1)
                for h in range(2):
                    act.wait_ge(n_l1.dve, n_l1.dve_at(i, 5, h))
                    act.activation(T3[h], T1[h], ACT.Identity, bias=vec("L1_gnn_gat_bias")).then_inc(n_l1.act, 1)
                for h in range(2):
                    act.wait_ge(n_l1.pe, n_l1.pe_at(i, 2, h))
                    act.activation(T2[h], bank(0, h), ACT.Identity, bias=vec("L1_gnn_proj_b")).then_inc(n_l1.act, 1)
                variance(n_l1, i, 3)
                for h in range(2):
                    act.wait_ge(n_l1.dve, n_l1.dve_at(i, 7, h))
                    act.activation(T2[h], T0[h], ACT.Identity, bias=vec("L1_gnn_ln_beta"), scale=vec("L1_gnn_ln_gamma"))\
                        .then_inc(n_l1.act, 1)
                variance(n_l1, i, 6)
            copy_table(t_l2)
            stage_indices(r_l2)
            act.wait_ge(norm_d, 1 + CHUNKS + 1)
            act.activation(bnv[:, 2:3], bnv[:, 1:2], ACT.Sqrt, bias=eps[:, 0:1]).then_inc(norm_a, 1)
            variances(n_l2b, 1)
            copy_table(t_l3a)
            stage_indices(r_l3a)
            with act.Fori(0, PAIRS) as i:
                stage_degrees(n_l3a, i)
            copy_table(t_l3b)
            stage_indices(r_l3b)
            with act.Fori(0, PAIRS) as i:
                stage_degrees(n_l3b, i)
                variance(n_l3b, i, 2)

        @block.tensor
        def _(pe):
            for r in (count, r_l0a, r_l0b, r_gat, r_l2, r_l3a, r_l3b):
                pe.sem_inc(r.agg_ready, TWO)
            for t in (t_l0a, t_l0b, t_gat, t_l2, t_l3a, t_l3b):
                pe.sem_inc(t.made, 2)
            for st in (n_l0a, n_l0b, n_l1, n_l2a, n_l2b, n_l3a, n_l3b):
                pe.sem_inc(st.pe, 1)
            pe.sem_inc(g_pe, 2 * len(G_PE))

            pe.wait_ge(prep, ENDS)
            nc.tensor.matmul(PS[:, 7, 0:ROWB], sel_first[:, :], ends[:, 0], start=True, stop=True)
            nc.tensor.matmul(PS[:, 7, ROWB:2 * ROWB], sel_last[:, :], ends[:, 1], start=True, stop=True).then_inc(ends_ps, 1)
            pe.wait_ge(prep, N_PREP)
            for n in range(N_COLS):
                if n >= 4:
                    pe.wait_ge(turn_sb, n - 3)
                for q in range(ROWB):
                    ins = nc.tensor.transpose(PS[:, 2 * (n % 4) + q // 4, (q % 4) * P:(q % 4 + 1) * P],
                                              rows_f[:, n, q, :], ident[:, :])
                ins.then_inc(turn_ps, 1)
            pe.wait_ge(x_in, 32)
            for n in range(N_XG):
                pe.wait_ge(turn_sb, max(n - 7, 0) + N_COLS)
                for q in range(4 * n, min(4 * n + 4, XBLOCKS)):
                    ins = nc.tensor.transpose(PS[:, n % 8, (q % 4) * P:(q % 4 + 1) * P], x_rows[:, q, :], ident[:, :])
                ins.then_inc(turn_ps, 1)
            pe.wait_ge(w_in, 16 * N_W_IN)
            pe.wait_ge(turn_sb, N_COLS + N_XG)
            for n in range(N_MATG):
                for q in range(4 * n, min(4 * n + 4, len(TURNED))):
                    ins = nc.tensor.transpose(PS[:, n, (q % 4) * P:(q % 4 + 1) * P], mat(TURNED[q]), ident[:, :])
                ins.then_inc(turn_ps, 1)
            nc.tensor.matmul(PS[:, 2, 0:P + 3 * HEADS], mat("L1_gnn_lin_w"), cat_rhs[:, :],
                             start=True, stop=True).then_inc(turn_ps, 1)

            def multiply_table(t):
                for s, n in t.ready:
                    pe.wait_ge(s, n)
                with pe.Fori(0, BLOCKS // 2) as i:
                    for b in range(2):
                        blk = 2 * i + b
                        pe.wait_ge(t.staged, blk + 1)
                        pe.wait_ge(t.out_a, blk + 1)
                        if t.width > 512:
                            pe.wait_ge(t.out_d, blk + 1)
                        for c in range(0, t.width, 512):
                            w = min(512, t.width - c)
                            ins = nc.tensor.matmul(PS[:, 4 * b + c // 512, 0:w], STG[:, b, :], t.weights[:, c:c + w],
                                                   start=True, stop=True)
                        ins.then_inc(t.made, 1)
                pe.wait_ge(t.out_a, 2 + BLOCKS)
                if t.width > 512:
                    pe.wait_ge(t.out_d, 2 + BLOCKS)

            def sum_tile(r, b, j, bank, first, final):
                at = dict(start=first, stop=final)
                if r.kind == "count":
                    return nc.tensor.matmul(PS[0:R16, 4 + bank, 0:P], OHR[:, b, j, :], oh16(b)[:, j, :], **at)
                if r.kind == "gat":
                    hot = oh_gat(b)[:, j, :]
                    nc.tensor.matmul(PS[0:2 * HEADS, 2 + bank, 0:P],
                                     WE[:, b % 2, j, :, :].rearrange("p t h -> p (t h)"), hot, **at)
                    return nc.tensor.matmul(PS[:, bank, 0:P], M[:, b % 2, j, :], hot, **at)
                return nc.tensor.matmul(PS[:, bank, 0:P], GB[:, b, j * r.width:j * r.width + P], oh(b, j), **at)

            def sum_tiles(r, k, b, ready, look=None, bank=None, flag=None):
                bank = b if bank is None else bank
                if look:
                    flag, base = meta_of(pe, k, 0, 2)
                elif flag is None:
                    flag, = meta_of(pe, k, 0, 1)
                with pe.If(flag > 0):
                    if look:
                        look([base] * G)
                    for s, n in ready:
                        pe.wait_ge(s, n)
                    pe.wait_ge(r.agg_free, k * G + G)
                    for j in range(G):
                        ins = sum_tile(r, b, j, bank, j == 0, j == G - 1)
                    ins.then_inc(r.agg_ready, G)
                with pe.Else():
                    if look:
                        look(meta_of(pe, k, META - G, G))
                    for s, n in ready:
                        pe.wait_ge(s, n)
                    for j in range(G):
                        pe.wait_ge(r.agg_free, k * G + (TWO + j))
                        sum_tile(r, b, j, bank, True, True).then_inc(r.agg_ready, 1)

            def sum_round(r):
                with pe.Fori(0, BATCHES // 2) as i:
                    for b in range(2):
                        k = 2 * i + b
                        ready = [(r.oh_ready, k + 1)]
                        if r.table:
                            ready.append((r.gathered[b], (i + 1) * (16 * G)))
                        sum_tiles(r, k, b, ready)

            def edges_done(r):
                return (r.agg_free, TWO + TILES)

            def node_products(st, first, later, after, ready=None):
                for s, n in after:
                    pe.wait_ge(s, n)
                with pe.Fori(0, PAIRS) as i:
                    if not later:
                        pe.wait_ge(st.dve, st.dve_at(i, 0))
                    for h in range(2):
                        for to, w, v in first:
                            ins = nc.tensor.matmul(bank(to, h)[0:w.shape[1]], w, v[:, chunk(i, h)], start=True, stop=True)
                        if ready:
                            pe.wait_ge(st.act, st.act_at(i, 1, h))
                            ins = spread(2, INVD, h)
                        if first:
                            ins.then_inc(st.pe, 1)
                    for who, step, product in later:
                        for h in range(2):
                            if who == "dve":
                                pe.wait_ge(st.dve, st.dve_at(i, step, h))
                            else:
                                pe.wait_ge(st.act, st.act_at(i, step, h))
                            product(h).then_inc(st.pe, 1)

            def spread(to, values, h):
                for q in range(4):
                    ins = nc.tensor.matmul(bank(to, h)[:, q * QUARTER:(q + 1) * QUARTER],
                                           values[:, h, q:q + 1].to_broadcast([QUARTER, P]),
                                           ident[0:QUARTER, 0:QUARTER], start=True, stop=True)
                return ins

            def product(to, w, v):
                return lambda h: nc.tensor.matmul(bank(to, h), w, v[h], start=True, stop=True)

            def mean_square(h):
                for q in range(4):
                    ins = nc.tensor.matmul(bank(2, h)[0:QUARTER, q:q + 1], T3[h][:, q * QUARTER:(q + 1) * QUARTER],
                                           mean_mat[:, 0:1], start=True, stop=True)
                return ins

            def layer_norm(who, step, v, act_step, dve_step):
                return [(who, step, product(1, center_mat[:, :], v)), ("act", act_step, mean_square),
                        ("dve", dve_step, lambda h: spread(3, INV, h))]

            for s, n in t_l0a.ready:
                pe.wait_ge(s, n)
            pe.wait_ge(base_in, 80)
            with pe.Fori(0, BLOCKS // 2) as i:
                for b in range(2):
                    blk = 2 * i + b
                    flag_1, _, flag_0 = meta_of(pe, 4 * i + (2 * b + 1), 0, 3)
                    pe.wait_ge(t_l0a.staged, blk + 1)
                    pe.wait_ge(t_l0a.out_a, blk + 2)
                    pe.wait_ge(t_l0a.out_d, blk + 2)
                    for c in range(4):
                        ins = nc.tensor.matmul(PS[:, c, :], STG[:, b, :], t_l0a.weights[:, 512 * c:512 * (c + 1)],
                                               start=True, stop=True)
                    ins.then_inc(t_l0a.made, 1)
                    for c in range(2):
                        k = 4 * i + (2 * b + c)
                        sum_tiles(count, k, c, [(count.oh_ready, k + 1)], flag=(flag_0, flag_1)[c])
            for k in range(2 * BLOCKS, BATCHES):
                sum_tiles(count, k, k % 2, [(count.oh_ready, k + 1)])
            pe.wait_ge(t_l0a.out_a, 2 + BLOCKS)
            pe.wait_ge(t_l0a.out_d, 2 + BLOCKS)
            pe.wait_ge(*edges_done(count))
            for q in range(NODES_P // QUARTER):
                ins = nc.tensor.matmul(PS[0:QUARTER, 0, q:q + 1], aux[0:R16, q * QUARTER:(q + 1) * QUARTER],
                                       ones_mat[0:R16, 0:1], start=True, stop=True)
            ins.then_inc(degree_ps, 1)
            pe.wait_ge(rt_ready, 2)
            with pe.Fori(0, BATCHES // 2) as i:
                for b in range(2):
                    k = 2 * i + b

                    def look(bases):
                        pe.wait_ge(et_hot, k + 1)
                        for j in range(G):
                            pe.wait_ge(look_free, k * G + (j + 1))
                            pe.sem_inc(looking, 1)
                            nc.tensor.matmul(PS[:, 4 + j % LOOKS, 0:P], ETR[:, b, j * P:(j + 1) * P],
                                             aux[0:R16, bass.ds(bases[j], P)], start=True, stop=True).then_inc(look_ready, 1)

                    sum_tiles(r_l0a, k, b, [(look_free, k * G + (LOOKS + G)), (r_l0a.gathered[b], (i + 1) * (16 * G))], look)
            node_products(n_l0a, [(0, mat("L0_gnn_root1"), X)], [], [edges_done(r_l0a)])
            multiply_table(t_l0b)
            sum_round(r_l0b)
            node_products(n_l0b, [(0, mat("L0_gnn_root2"), H)],
                          layer_norm("dve", 2, T1, 1, 3), [edges_done(r_l0b)])
            multiply_table(t_gat)
            def absorb(s, n):
                pe.wait_ge(s, n)
                pe.sem_inc(g_passed, 1)

            def turn(k, c, h):
                if h == 0:
                    pe.wait_ge(r_gat.oh_ready, k + 1)
                    pe.wait_ge(g_pen, k + 1)
                for j in range(4):
                    ins = nc.tensor.transpose(PS[:, 6 + h, j * P:(j + 1) * P], oh_gat(c)[:, 4 * h + j, :], ident[:, :])
                ins.then_inc(g_turned_ps, 1)

            def look_up(k, c, i1, flag):
                absorb(g_starts, k + 1)
                absorb(g_turned, 2 * k + 2)
                nc.tensor.transpose(PS[0:TH, 7, 0:P], starts[:, :, :].rearrange("p h j -> p (h j)"), ident[:, :])
                absorb(g_in[c % 2], i1 * (16 * G))

                def products(windows):
                    for j, window in enumerate(windows):
                        ins = nc.tensor.matmul(PS[:, 6, j * 3 * NL:(j + 1) * 3 * NL], OHT[:, j, :],
                                               AW[:, c % 2, window, :, :].rearrange("p s h -> p (s h)"), start=True, stop=True)
                    ins.then_inc(g_look, 1)

                with pe.If(flag > 0):
                    products([0] * G)
                with pe.Else():
                    products(range(G))

            def attend(i, c):
                k, b = 4 * i + c, c % 2
                before = not (isinstance(i, int) and c == 0)
                if before:
                    flag_before, = meta_of(pe, k - 1, 0, 1)
                flag_next, = meta_of(pe, k + 1, 0, 1)

                def sum_part(part):
                    if not before:
                        return
                    with pe.If(flag_before > 0):
                        if part == 0:
                            pe.wait_ge(g_dve, at(G_DVE, k - 1, "m"))
                            pe.wait_ge(r_gat.agg_free, (k - 1) * G + G)
                        for j in (2 * part, 2 * part + 1):
                            ins = sum_tile(r_gat, (c - 1) % 4, j, 1 - b, j == 0, j == G - 1)
                        if part == 3:
                            ins.then_inc(r_gat.agg_ready, G)
                    if part == 3:
                        with pe.Else():
                            pe.wait_ge(g_dve, at(G_DVE, k - 1, "m"))
                            for j in range(G):
                                pe.wait_ge(r_gat.agg_free, (k - 1) * G + (TWO + j))
                                sum_tile(r_gat, (c - 1) % 4, j, 1 - b, True, True).then_inc(r_gat.agg_ready, 1)

                absorb(g_dve, at(G_DVE, k, "xs"))
                nc.tensor.transpose(PS[0:TH, 4, 0:P], XS[:, :, :].rearrange("p h j -> p (h j)"), ident[:, :]).then_inc(g_pe, 1)
                turn(k + 1, (c + 1) % 4, 0)
                absorb(g_dve, at(G_DVE, k, "segment"))
                for n, part in enumerate((seg_max[:, 0:1], local_max[:, P - 1:P])):
                    ins = nc.tensor.matmul(PS[0:1, 5, n * TH:(n + 1) * TH], part, ident[0:TH, 0:TH], start=True, stop=True)
                ins.then_inc(g_pe, 1)
                turn(k + 1, (c + 1) % 4, 1)
                sum_part(0)
                absorb(g_dve, at(G_DVE, k, "row_back"))
                for n in range(2):
                    ins = nc.tensor.matmul(PS[0:TH, 5, P + n:P + n + 1], ROW[:, 2, n::2],
                                           one[:, :], start=True, stop=True)
                ins.then_inc(g_pe, 1)
                look_up(k + 1, (c + 1) % 4, 2 * i + ((c + 1) // 2 + 1), flag_next)
                absorb(g_dve, at(G_DVE, k, "back"))
                nc.tensor.transpose(PS[:, 4, 0:TH], all_max, ident[0:TH, 0:TH]).then_inc(g_pe, 1)
                sum_part(1)
                sum_part(2)
                absorb(g_act, at(G_ACT, k, "scale2"))
                nc.tensor.matmul(PS[:, 5, 256:257], RE[:, 0:P], one[:, :], start=True, stop=True)
                nc.tensor.matmul(PS[0:2 * HEADS, 5, 258:259], RE[:, P:P + 2 * HEADS], one[:, :],
                                 start=True, stop=True).then_inc(g_pe, 1)
                sum_part(3)

            flag_first, = meta_of(pe, 0, 0, 1)
            turn(0, 0, 0)
            turn(0, 0, 1)
            look_up(0, 0, 1, flag_first)
            for c in range(4):
                attend(0, c)
            with pe.Fori(1, BATCHES // 4) as i:
                for c in range(4):
                    attend(i, c)
            sum_tiles(r_gat, BATCHES - 1, 3, [(g_dve, at(G_DVE, BATCHES - 1, "m"))], bank=1)
            node_products(n_l1, [(0, lin_cat[:, 0:P], X), (1, den_mat[:, :], aux[0:2 * HEADS, :]),
                                 (2, own_mat[:, :], aux[0:2 * HEADS, :])],
                          [("act", 2, product(0, mat_t("L1_gnn_proj_w"), T3))] + layer_norm("act", 3, T2, 4, 6)
                          + layer_norm("dve", 8, T1, 8, 9), [edges_done(r_gat)])
            multiply_table(t_l2)
            sum_round(r_l2)
            node_products(n_l2a, [(0, mat("L2_gnn_loop_w"), X), (1, mat("L2_gnn_res_w"), X)], [],
                          [edges_done(r_l2)])
            node_products(n_l2b, [], layer_norm("dve", 2, T1, 1, 3), [])
            multiply_table(t_l3a)
            sum_round(r_l3a)
            node_products(n_l3a, [(0, mat_t("L3_gnn_W1_r"), X)], [], [edges_done(r_l3a)], True)
            multiply_table(t_l3b)
            sum_round(r_l3b)
            node_products(n_l3b, [(0, mat_t("L3_gnn_W2_r"), H)],
                          layer_norm("dve", 3, T1, 2, 4), [edges_done(r_l3b)], True)
            pe.wait_ge(*n_l3b.end())
            for n in range(N_XG):
                if n >= 8:
                    pe.wait_ge(out_sb, n - 7)
                for q in range(4 * n, min(4 * n + 4, XBLOCKS)):
                    ins = nc.tensor.transpose(PS[:, n % 8, (q % 4) * P:(q % 4 + 1) * P], X[:, q * P:(q + 1) * P], ident[:, :])
                ins.then_inc(out_ps, 1)

        @block.vector
        def _(dve):
            for r in (count, r_l0a, r_l0b, r_gat, r_l2, r_l3a, r_l3b):
                dve.sem_inc(r.agg_free, TWO)
            for t in (t_l0a, t_l0b, t_gat, t_l2, t_l3a, t_l3b):
                dve.sem_inc(t.out_d, 2)
            for st in (n_l0a, n_l0b, n_l1, n_l2a, n_l2b, n_l3a, n_l3b):
                dve.sem_inc(st.dve, 1)
            dve.sem_inc(look_free, LOOKS)
            dve.sem_inc(g_dve, 2 * len(G_DVE))
            dve.sem_inc(norm_d, 1)

            preps = [0]

            def link(ins):
                preps[0] += 1
                ins.then_inc(prep, 1)
                dve.wait_ge(prep, preps[0])

            dve.wait_ge(cleared, 1)
            link(dve.tensor_scalar(ident[:, :], iota_f[:, :], pidx[:, 0:1], None, ALU.is_equal))
            link(dve.tensor_tensor(center_mat[:, :], ident[:, :], mean_mat[:, :], ALU.subtract))
            link(dve.tensor_scalar(below[:, 0:HEADS], head_iota[:, :], pidx[:, 0:1], 0.0, ALU.subtract, ALU.is_le))
            link(dve.tensor_scalar(hsel[:, :], head_iota[:, :], pidx[:, 0:1], -float(HD), ALU.subtract, ALU.is_gt))
            link(dve.tensor_tensor(hsel[:, :], hsel[:, :], below[:, 0:HEADS], ALU.mult))
            link(dve.tensor_scalar(shift[:, 0:1], pidx[:, 0:1], float(HD), None, ALU.mult))
            link(dve.tensor_scalar(shift[:, 1:2], pidx[:, 0:1], float(HD), -float(HD * HEADS), ALU.mult, ALU.add))
            for m, rows, s in ((own_mat[:, :], 2 * HEADS, 1), (den_mat[:, :], 2 * HEADS, 0)):
                link(dve.tensor_scalar(below[0:rows, :], iota_f[0:rows, :], shift[0:rows, s:s + 1], 0.0, ALU.subtract, ALU.is_ge))
                link(dve.tensor_scalar(m, iota_f[0:rows, :], shift[0:rows, s:s + 1], float(HD), ALU.subtract, ALU.is_lt))
                link(dve.tensor_tensor(m, m, below[0:rows, :], ALU.mult))
            link(dve.tensor_tensor(den_mat[:, :], den_mat[:, :], own_mat[:, :], ALU.add))
            dve.wait_ge(w_in, 16 * N_W_IN)
            link(dve.tensor_copy(cat_rhs[:, 0:P], ident[:, :]))
            for n, att in enumerate((att_src, att_dst, att_src)):
                link(dve.tensor_scalar(cat_rhs[:, P + n * HEADS:P + (n + 1) * HEADS], hsel[:, :], att, None, ALU.mult))
            link(dve.tensor_scalar(sel_first[:, :], batch_first[:, :], pidx[:, 0:1], None, ALU.is_equal))
            link(dve.tensor_scalar(sel_last[:, :], batch_first[:, :], float(G - 1), pidx[:, 0:1], ALU.add, ALU.is_equal))
            dve.wait_ge(rows_in, 16 * N_ROWS_IN)
            link(dve.tensor_copy(ends[:, 0], base_i[:, :]))
            link(dve.tensor_copy(ends[:, 1], rows_i[:, DST, :, P - 1]))
            assert preps[0] == ENDS, preps
            dve.wait_ge(ends_ps, 1)
            link(dve.tensor_copy(bends[:, :, :].rearrange("p a b -> p (a b)"), PS[:, 7, 0:2 * ROWB]))
            link(dve.tensor_tensor(spans[:, 0], bends[:, 1], bends[:, 0], ALU.subtract))
            link(dve.tensor_scalar(spans[:, 1], spans[:, 0], float(P), None, ALU.is_lt))
            link(dve.tensor_tensor(spans[:, 0], bends[:, 0], ends[:, 0], ALU.subtract))
            link(dve.tensor_tensor(spans[:, 0], spans[:, 0], spans[:, 1], ALU.mult))
            link(dve.tensor_tensor(spans[:, 2], spans[:, 0], ends[:, 0], ALU.add))
            link(dve.tensor_copy(flag_i[:, :], spans[:, 1]))
            link(dve.tensor_copy(first_i[:, :], spans[:, 2]))
            link(dve.tensor_tensor(rows_f[:, F_LOCAL], rows_i[:, DST], last(first_i[:, :], P), ALU.subtract))
            for f, v, types in ((F_IDX16, R16, ET16), (F_IDX8, R8, ET8)):
                link(dve.scalar_tensor_tensor(rows_f[:, f], rows_i[:, SRC], float(v), rows_i[:, types], ALU.mult, ALU.add))
            link(dve.tensor_copy(rows_f[:, F_SRC], rows_i[:, SRC]))
            link(dve.tensor_copy(rows_f[:, F_ET], rows_i[:, ET16]))
            link(dve.tensor_tensor(rows_f[:, F_START, :, 1:P], rows_i[:, DST, :, 1:P], rows_i[:, DST, :, 0:P - 1], ALU.not_equal))
            link(dve.tensor_tensor(rows_f[:, F_START, :, 0], rows_i[:, DST, :, 0], prev_last[:, :], ALU.not_equal))
            link(dve.tensor_scalar(rows_f[:, F_PEN], rows_f[:, F_START], -BIG, None, ALU.mult))
            link(dve.tensor_copy(seg[:, :, 0], rows_f[:, F_PEN, :, 0]))
            link(dve.tensor_tensor(seg[:, :, 1], ends[:, 0], ends[:, 1], ALU.not_equal))
            link(dve.tensor_scalar(seg[:, :, 1], seg[:, :, 1], -BIG, None, ALU.mult))
            assert preps[0] == N_PREP, preps

            cols = (local, idx16, idx8, idx1, etype, start)
            for n, col in enumerate(cols):
                dve.wait_ge(turn_ps, n + 1)
                ps = PS[:, 2 * (n % 4):2 * (n % 4) + 2, :].rearrange("p a n -> p (a n)")
                dve.tensor_copy(col[:, :], ps[:, 0:ROWB * P]).then_inc(turn_sb, 1)
            for n in range(N_XG):
                dve.wait_ge(turn_ps, N_COLS + n + 1)
                w = min(512, XBLOCKS * P - 512 * n)
                dve.tensor_copy(X[:, 512 * n:512 * n + w], PS[:, n % 8, 0:w]).then_inc(turn_sb, 1)
            for n in range(N_MATG):
                dve.wait_ge(turn_ps, N_COLS + N_XG + n + 1)
                m = min(4, len(TURNED) - 4 * n)
                dve.tensor_copy(turned[:, 4 * n:4 * n + m, :].rearrange("p q n -> p (q n)"), PS[:, n, 0:m * P])\
                    .then_inc(turn_sb, 1)
            dve.wait_ge(turn_ps, TURNS)
            dve.tensor_copy(lin_cat[:, :], PS[:, 2, 0:P + 3 * HEADS]).then_inc(turn_sb, 1)

            def copy_block(t, i, b):
                blk = 2 * i + b
                dve.wait_ge(t.made, blk + 3)
                if not isinstance(i, int):
                    dve.wait_ge(t.stored[b], i * 16)
                ps = PS[:, t.banks * b:t.banks * b + 4, :].rearrange("p a n -> p (a n)")
                dve.tensor_copy(TOUT[:, b, t.part:t.width], ps[:, t.part:t.width]).then_inc(t.out_d, 1)

            def copy_table(t):
                if t.width <= 512:
                    return
                for b in range(2):
                    copy_block(t, 0, b)
                with dve.Fori(1, BLOCKS // 2) as i:
                    for b in range(2):
                        copy_block(t, i, b)

            def add_window(r, base, bank):
                if r.kind == "count":
                    dst = aux[0:R16, bass.ds(base, P)]
                    return dve.tensor_tensor(dst, dst, PS[0:R16, 4 + bank, 0:P], ALU.add)
                if r.kind == "gat":
                    dst = aux[0:2 * HEADS, bass.ds(base, P)]
                    dve.tensor_tensor(dst, dst, PS[0:2 * HEADS, 2 + bank, 0:P], ALU.add)
                dst = sums[:, bass.ds(base, P)]
                return dve.tensor_tensor(dst, dst, PS[:, bank, 0:P], ALU.add)

            def add_tiles(r, k, b, ready=(), meta_k=None):
                flag, base = meta_k or meta_of(dve, k, 0, 2)
                with dve.If(flag > 0):
                    for s, v in ready:
                        dve.wait_ge(s, v)
                    dve.wait_ge(r.agg_ready, k * G + (TWO + G))
                    dve.wait_ge(r.agg_free, k * G + TWO)
                    add_window(r, base, b).then_inc(r.agg_free, G)
                with dve.Else():
                    bases = meta_of(dve, k, META - G, G)
                    for s, v in ready:
                        dve.wait_ge(s, v)
                    for j in range(G):
                        dve.wait_ge(r.agg_ready, k * G + (TWO + j + 1))
                        dve.wait_ge(r.agg_free, k * G + (TWO + j))
                        add_window(r, bases[j], b).then_inc(r.agg_free, 1)

            def one_hot(r, k, b):
                dve.wait_ge(r.agg_ready, k * G + G)
                dve.tensor_tensor(OH[:, b, :].rearrange("p (j d) -> p j d", j=G), mid(iota_f[:, :], G),
                                  last(local[:, bass.ds(k * G, G)], P), ALU.is_equal).then_inc(r.oh_ready, 1)

            def sum_round(r):
                with dve.Fori(0, BATCHES // 2) as i:
                    for b in range(2):
                        k = 2 * i + b
                        one_hot(r, k, b)
                        add_tiles(r, k, b)

            def layer_norm(st, i, d, p, s, out):
                for h in range(2):
                    dve.wait_ge(st.act, st.act_at(i, s + 3, h))
                    dve.reciprocal(INV[:, h, :], DEV[:, h, :]).then_inc(st.dve, 1)
                for h in range(2):
                    dve.wait_ge(st.pe, st.pe_at(i, p + 3, h))
                    dve.tensor_tensor(out(h), bank(3, h), T5[h], ALU.mult).then_inc(st.dve, 1)

            dve.wait_ge(scratch, 64)
            dve.wait_ge(base_in, 80)
            dve.memset(sums, 0.0)
            dve.memset(aux[0:R16, :], 0.0)
            def relation_hot(k, b):
                dve.wait_ge(count.agg_ready, k * G + G)
                dve.tensor_tensor(OHR[:, b, :, :], mid(iota_f[:, 0:R16], G), last(etype[:, bass.ds(k * G, G)], R16), ALU.is_equal)
                dve.tensor_tensor(oh16(b), mid(iota_f[:, :], G), last(local[:, bass.ds(k * G, G)], P),
                                  ALU.is_equal).then_inc(count.oh_ready, 1)

            def count_batch(k, b, meta_k=None):
                add_tiles(count, k, b, meta_k=meta_k)
                relation_hot(k + 2, b)

            def copy_and_count(i, b):
                flag_1, base_1, flag_0, base_0 = meta_of(dve, 4 * i + (2 * b + 1), 0, 4)
                copy_block(t_l0a, i, b)
                for c, meta_k in enumerate(((flag_0, base_0), (flag_1, base_1))):
                    count_batch(4 * i + (2 * b + c), c, meta_k)

            relation_hot(0, 0)
            relation_hot(1, 1)
            for b in range(2):
                copy_and_count(0, b)
            with dve.Fori(1, BLOCKS // 2) as i:
                for b in range(2):
                    copy_and_count(i, b)
            for k in range(2 * BLOCKS, BATCHES):
                count_batch(k, k % 2)
            dve.wait_ge(degree_ps, 1)
            dve.tensor_scalar(inv_degree[:, :], PS[0:QUARTER, 0, 0:NODES_P // QUARTER], 1.0, None, ALU.max).then_inc(degree, 1)
            dve.wait_ge(degree, 1)
            dve.reciprocal(inv_degree[:, :], inv_degree[:, :]).then_inc(degree, 1)
            dve.tensor_scalar(aux[0:R16, :], aux[0:R16, :], 1.0, None, ALU.max).then_inc(rt_ready, 1)
            dve.wait_ge(rt_ready, 1)
            dve.reciprocal(aux[0:R16, :], aux[0:R16, :]).then_inc(rt_ready, 1)
            def etype_hot(b, times):
                dve.wait_ge(et_in[b], times * 16)
                dve.tensor_scalar(ETR[:, b, :], ETR[:, b, :], pidx[0:R16, 0:1], None, ALU.is_equal).then_inc(et_hot, 1)

            etype_hot(0, 1)
            with dve.Fori(0, BATCHES // 2) as i:
                for b in range(2):
                    k = 2 * i + b
                    dve.wait_ge(r_l0a.agg_ready, k * G + G)
                    for j in range(G):
                        n = k * G + j
                        dve.wait_ge(look_ready, n + 1)
                        dve.scalar_tensor_tensor(oh(b, j), iota_f[:, :], local[:, bass.ds(n, 1)], PS[:, 4 + j % LOOKS, 0:P],
                                                 ALU.is_equal, ALU.mult, accum_out=wstage[:, b, j:j + 1]).then_inc(look_free, 1)
                    dve.wait_ge(look_free, k * G + (LOOKS + G))
                    dve.tensor_copy(wcol[:, bass.ds(k * G, G)], wstage[:, b, :]).then_inc(w_added, 1)
                    etype_hot(1 - b, i + (1 + b))
                    add_tiles(r_l0a, k, b)
            with dve.Fori(0, PAIRS) as i:
                st = n_l0a
                for h in range(2):
                    dve.wait_ge(st.pe, st.pe_at(i, 1, h))
                    dve.scalar_tensor_tensor(T0[h], bank(0, h), vec("L0_gnn_b1"), sums[:, chunk(i, h)], ALU.add, ALU.add).then_inc(st.dve, 1)
                for h in range(2):
                    dve.wait_ge(st.dve, st.dve_at(i, 1, h))
                    dve.tensor_scalar(H[:, chunk(i, h)], T0[h], 0.0, None, ALU.max).then_inc(st.dve, 1)
            copy_table(t_l0b)
            dve.wait_ge(t_l0b.zeroed, 1)
            dve.wait_ge(w_added, BATCHES)
            with dve.Fori(0, BATCHES // 2) as i:
                for b in range(2):
                    k = 2 * i + b
                    dve.wait_ge(r_l0b.agg_ready, k * G + G)
                    for j in range(G):
                        n = k * G + j
                        ins = dve.tensor_scalar(oh(b, j), iota_f[:, :], local[:, bass.ds(n, 1)], wcol[:, bass.ds(n, 1)],
                                                ALU.is_equal, ALU.mult)
                    ins.then_inc(r_l0b.oh_ready, 1)
                    add_tiles(r_l0b, k, b)
            with dve.Fori(0, PAIRS) as i:
                st = n_l0b
                for h in range(2):
                    dve.wait_ge(st.pe, st.pe_at(i, 1, h))
                    dve.scalar_tensor_tensor(T0[h], bank(0, h), vec("L0_gnn_b2"), sums[:, chunk(i, h)], ALU.add, ALU.add).then_inc(st.dve, 1)
                for h in range(2):
                    dve.wait_ge(st.dve, st.dve_at(i, 1, h))
                    dve.tensor_tensor(T1[h], T0[h], X[:, chunk(i, h)], ALU.add).then_inc(st.dve, 1)
                layer_norm(st, i, 2, 1, 0, lambda h: X[:, chunk(i, h)])
            copy_table(t_gat)
            dve.wait_ge(basis_in, 16)
            for q in range(R8):
                for r in range(R8):
                    w = wcomp[:, r * R8 + q:r * R8 + q + 1]
                    to, of = MIXED[:, r * P:(r + 1) * P], BASIS[:, q * P:(q + 1) * P]
                    if q == 0:
                        dve.tensor_scalar(to, of, w, None, ALU.mult).then_inc(mixed, 1)
                    else:
                        dve.wait_ge(mixed, (q - 1) * R8 + r + 1)
                        dve.scalar_tensor_tensor(to, of, w, to, ALU.mult, ALU.add).then_inc(mixed, 1)
            dve.wait_ge(t_gat.zeroed, 3)

            for b in range(2):
                dve.wait_ge(t_gat.stored[b], 16 * t_gat.stores)
            dve.wait_ge(seg_in, 16)

            dve.wait_ge(t_gat.out_a, 2 + BLOCKS)
            logits = LOGITS.rearrange("p (k h) -> p k h", h=NL)
            dve.tensor_copy(SPLIT[:, :, 0, :], logits).then_inc(split, 1)
            for n in range(2):
                dve.wait_ge(split, 2 * n + 1)
                dve.tensor_tensor(logits, logits, SPLIT[:, :, n, :], ALU.subtract).then_inc(split, 1)
                dve.wait_ge(split, 2 * n + 2)
                dve.tensor_copy(SPLIT[:, :, n + 1, :], logits).then_inc(split, 1)

            def one_hot_gat(k, c):
                dve.tensor_tensor(oh_gat(c), mid(iota_f[:, :], G), last(local[:, bass.ds(k * G, G)], P),
                                  ALU.is_equal).then_inc(r_gat.oh_ready, 1)

            def target_logits(k, b, n):
                look = PS[:, 6, 0:3 * NL * G].rearrange("p (j s h) -> p j s h", j=G, s=3)
                if n == 1:
                    dve.wait_ge(g_pen, k + 2)
                else:
                    dve.wait_ge(g_dve_ahead, 2 * k + 1)
                dve.tensor_tensor(AD[:, b, :, :], AD[:, b, :, :], look[:, :, n, :], ALU.add).then_inc(g_dve_ahead, 1)

            def attend(i, c):
                k, b = 4 * i + c, c % 2
                r = r_gat

                def own(step):
                    dve.wait_ge(g_dve, at(G_DVE, k, step))

                rows = GB[:, b, :].rearrange("p (j w) -> p j w", w=GATW)
                s_logit = rows[:, :, P:GATW]
                t_logit, loop_logit = AD[:, b, :, 0:HEADS], AD[:, b, :, HEADS:2 * HEADS]
                row, row_f, row_b = (ROW[:, n, :] for n in range(3))
                final_first, final_last = row_b[:, 0::SLOTS], row_b[:, SLOTS - 1::SLOTS]
                dve.wait_ge(g_pen, k + 2)
                dve.wait_ge(g_dve_ahead, 2 * (k + 1))
                dve.wait_ge(r.gathered[b], 2 * (16 * G) * i + (c // 2 + 1) * (16 * G))
                dve.tensor_tensor(XS[:, :, :].rearrange("p h j -> p j h"), s_logit, loop_logit, ALU.max).then_inc(g_dve, 1)
                dve.tensor_tensor(ZL[:, 0], s_logit, t_logit, ALU.add).then_inc(g_dve, 1)
                dve.tensor_tensor(ZL[:, 1], loop_logit, t_logit, ALU.add).then_inc(g_dve, 1)
                dve.wait_ge(g_pe, at(G_PE, k, "xs_rows"))
                dve.tensor_tensor_scan(local_max, PEN[:, b, 0:P], PS[0:TH, 4, 0:P], -BIG, ALU.add, ALU.max).then_inc(g_dve, 1)
                own("local")
                dve.tensor_tensor_scan(seg_max[:, ::-1], PEN[:, b, 1:P + 1][:, ::-1], local_max[:, ::-1], -BIG,
                                       ALU.add, ALU.max).then_inc(g_dve, 1)
                one_hot_gat(k + 2, (c + 2) % 4)
                base, *meta_before = meta_of(dve, k, 1, 3)
                dve.wait_ge(g_cuts, k + 1)
                dve.wait_ge(g_act, at(G_ACT, k, "row"))
                dve.scalar_tensor_tensor(row[:, 0::SLOTS], CARRY[:, :], SEG[:, bass.ds(k, 1), 0], row[:, 0::SLOTS],
                                         ALU.add, ALU.max).then_inc(g_dve, 1)
                own("first")
                dve.tensor_tensor_scan(row_f, CUTS[:, b, 0:HEADS * SLOTS], row, -BIG, ALU.add, ALU.max).then_inc(g_dve, 1)
                own("row")
                dve.tensor_tensor_scan(row_b[:, ::-1], CUTS[:, b, 1:HEADS * SLOTS + 1][:, ::-1], row_f[:, ::-1], -BIG,
                                       ALU.add, ALU.max).then_inc(g_dve, 1)
                dve.wait_ge(g_pe, at(G_PE, k, "ends"))
                dve.tensor_copy(ENDM[:, :], PS[0:TH, 5, P:P + 2]).then_inc(g_dve, 1)
                dve.tensor_tensor(RZ[:, 0], CARRY[:, :], final_first, ALU.min).then_inc(g_dve, 1)
                own("ends")
                dve.tensor_tensor_scan(from_before, PEN[:, b, 0:P], seg_max, ENDM[:, 0:1], ALU.add, ALU.max).then_inc(g_dve, 1)
                dve.tensor_copy(RZ[:, 1], final_first).then_inc(g_dve, 1)
                own("forward")
                dve.tensor_tensor_scan(all_max[:, ::-1], PEN[:, b, 1:P + 1][:, ::-1], from_before[:, ::-1], ENDM[:, 1:2],
                                       ALU.add, ALU.max).then_inc(g_dve, 1)
                own("old")
                dve.tensor_copy(CARRY[:, :], final_last).then_inc(g_dve, 1)

                def shifted(n, before):
                    own(before)
                    dve.tensor_tensor(RZ[:, :, :], RZ[:, :, :], mid(AW[0:1, b, 0, n, 0:HEADS], 2), ALU.add).then_inc(g_dve, 1)

                dve.wait_ge(g_pe, at(G_PE, k, "maxima"))
                dve.tensor_tensor(ZL[:, 2], PS[:, 4, 0:TH].rearrange("p (h j) -> p j h", h=HEADS), t_logit,
                                  ALU.add).then_inc(g_dve, 1)
                shifted(0, "new")
                own("max_logit")
                z = ZL[:, :, :, :].rearrange("p t j h -> p (t j h)")
                dve.scalar_tensor_tensor(z, z, SLOPE, z, ALU.mult, ALU.max).then_inc(g_dve, 1)
                shifted(1, "logit_a")
                own("lrelu")
                zf = ZL[:, :, :, :].rearrange("p t j h -> p t (j h)")
                dve.tensor_tensor(ZD[:, :, :, :].rearrange("p t j h -> p t (j h)"), zf[:, 0:2], mid(zf[:, 2], 2),
                                  ALU.subtract).then_inc(g_dve, 1)
                shifted(2, "logit_b")
                own("scaled_logits")
                dve.scalar_tensor_tensor(RL[:, :, :], RZ[:, :, :], SLOPE, RZ[:, :, :], ALU.mult, ALU.max).then_inc(g_dve, 1)
                own("scaled_lrelu")
                dve.tensor_tensor(RD[:, :], RL[:, 0], RL[:, 1], ALU.subtract).then_inc(g_dve, 1)
                target_logits(k + 1, 1 - b, 1)
                target_logits(k + 1, 1 - b, 2)
                dve.wait_ge(g_act, at(G_ACT, k, "weights"))
                dve.tensor_tensor(WE[:, b, :, 1, :], WE[:, b, :, 1, :], last(start[:, bass.ds(k * G, G)], HEADS), ALU.mult)\
                    .then_inc(g_dve, 1)
                dve.tensor_tensor(M[:, b, :, :].rearrange("p j (h c) -> p j h c", c=HD),
                                  rows[:, :, 0:P].rearrange("p j (h c) -> p j h c", c=HD),
                                  WE[:, b, :, 0, :].unsqueeze(3).to_broadcast([P, G, HEADS, HD]), ALU.mult).then_inc(g_dve, 1)
                dve.wait_ge(g_pe, at(G_PE, k, "scale"))
                dve.tensor_copy(RS[:, 0:2], PS[:, 5, 256:260:2]).then_inc(g_dve, 1)
                if not (isinstance(i, int) and c == 0):
                    add_tiles(r, k - 1, 1 - b, [(g_dve, at(G_DVE, k - 1, "aux"))], meta_before)
                    dve.wait_ge(r.agg_free, k * G + TWO)
                own("scale")
                dve.tensor_scalar(sums[:, bass.ds(base, 1)], sums[:, bass.ds(base, 1)], RS[:, 0:1], None, ALU.mult)\
                    .then_inc(g_dve, 1)
                dve.tensor_scalar(aux[0:2 * HEADS, bass.ds(base, 1)], aux[0:2 * HEADS, bass.ds(base, 1)],
                                  RS[0:2 * HEADS, 1:2], None, ALU.mult).then_inc(g_dve, 1)

            one_hot_gat(0, 0)
            one_hot_gat(1, 1)
            for n in (1, 2):
                target_logits(0, 0, n)
            for c in range(4):
                attend(0, c)
            with dve.Fori(1, BATCHES // 4) as i:
                for c in range(4):
                    attend(i, c)
            dve.wait_ge(g_dve, at(G_DVE, BATCHES - 1, "aux"))
            add_tiles(r_gat, BATCHES - 1, 1)

            with dve.Fori(0, PAIRS) as i:
                st = n_l1
                for h in range(2):
                    dve.wait_ge(st.pe, st.pe_at(i, 1, h))
                    dve.wait_ge(st.act, st.act_at(i, 1, h))
                    dve.tensor_tensor(T1[h], bank(2, h), T0[h], ALU.mult).then_inc(st.dve, 1)
                for h in range(2):
                    dve.tensor_scalar(T3[h], bank(1, h), 1e-30, None, ALU.max).then_inc(st.dve, 1)
                for h in range(2):
                    dve.wait_ge(st.dve, st.dve_at(i, 2, h))
                    dve.tensor_tensor(T2[h], T1[h], sums[:, chunk(i, h)], ALU.add).then_inc(st.dve, 1)
                for h in range(2):
                    dve.reciprocal(T5[h], T3[h]).then_inc(st.dve, 1)
                for h in range(2):
                    dve.wait_ge(st.dve, st.dve_at(i, 4, h))
                    dve.tensor_tensor(T1[h], T2[h], T5[h], ALU.mult).then_inc(st.dve, 1)
                layer_norm(st, i, 5, 2, 3, lambda h: T0[h])
                for h in range(2):
                    dve.wait_ge(st.act, st.act_at(i, 7, h))
                    dve.tensor_tensor(T1[h], T2[h], X[:, chunk(i, h)], ALU.add).then_inc(st.dve, 1)
                layer_norm(st, i, 8, 5, 7, lambda h: X[:, chunk(i, h)])

            copy_table(t_l2)
            dve.wait_ge(t_l2.zeroed, 1)
            sum_round(r_l2)
            with dve.Fori(0, PAIRS) as i:
                st = n_l2a
                for h in range(2):
                    dve.wait_ge(st.pe, st.pe_at(i, 1, h))
                    dve.scalar_tensor_tensor(T0[h], bank(0, h), vec("L2_gnn_bias"), sums[:, chunk(i, h)], ALU.add, ALU.add).then_inc(st.dve, 1)
                for h in range(2):
                    dve.tensor_scalar(T1[h], bank(1, h), vec("L2_gnn_res_b"), 0.0, ALU.add, ALU.max).then_inc(st.dve, 1)
                for h in range(2):
                    dve.wait_ge(st.dve, st.dve_at(i, 2, h))
                    dve.scalar_tensor_tensor(H[:, chunk(i, h)], T0[h], 0.0, T1[h], ALU.max, ALU.add).then_inc(st.dve, 1)
            dve.wait_ge(*n_l2a.end())
            for c in range(CHUNKS):
                w = min(CHUNK, NODES - c * CHUNK)
                dve.bn_stats(bn[:, c, :], H[:, c * CHUNK:c * CHUNK + w]).then_inc(norm_d, 1)
            dve.wait_ge(norm_d, 1 + CHUNKS)
            dve.bn_aggr(bnv[:, 0:2], bn[:, :, :].rearrange("p c s -> p (c s)")).then_inc(norm_d, 1)
            dve.wait_ge(norm_a, 1)
            dve.reciprocal(bnv[:, 3:4], bnv[:, 2:3]).then_inc(norm_d, 1)
            dve.wait_ge(norm_d, CHUNKS + 3)
            dve.tensor_tensor(bnv[:, 4:5], bnv[:, 3:4], vec("L2_gnn_bn_gamma"), ALU.mult).then_inc(norm_d, 1)
            dve.wait_ge(norm_d, CHUNKS + 4)
            dve.tensor_tensor(bnv[:, 5:6], bnv[:, 0:1], bnv[:, 4:5], ALU.mult).then_inc(norm_d, 1)
            dve.wait_ge(norm_d, CHUNKS + 5)
            dve.tensor_tensor(bnv[:, 6:7], vec("L2_gnn_bn_beta"), bnv[:, 5:6], ALU.subtract).then_inc(norm_d, 1)
            dve.wait_ge(norm_d, CHUNKS + 6)
            with dve.Fori(0, PAIRS) as i:
                st = n_l2b
                for h in range(2):
                    dve.scalar_tensor_tensor(T0[h], H[:, chunk(i, h)], bnv[:, 4:5], X[:, chunk(i, h)], ALU.mult, ALU.add).then_inc(st.dve, 1)
                for h in range(2):
                    dve.wait_ge(st.dve, st.dve_at(i, 1, h))
                    dve.tensor_scalar(T1[h], T0[h], bnv[:, 6:7], None, ALU.add).then_inc(st.dve, 1)
                layer_norm(st, i, 2, 0, 0, lambda h: X[:, chunk(i, h)])
            copy_table(t_l3a)
            dve.wait_ge(t_l3a.zeroed, 1)
            sum_round(r_l3a)
            with dve.Fori(0, PAIRS) as i:
                st = n_l3a
                for h in range(2):
                    dve.wait_ge(st.pe, st.pe_at(i, 1, h))
                    dve.tensor_tensor(T0[h], sums[:, chunk(i, h)], bank(2, h), ALU.mult).then_inc(st.dve, 1)
                for h in range(2):
                    dve.wait_ge(st.dve, st.dve_at(i, 1, h))
                    dve.scalar_tensor_tensor(T1[h], bank(0, h), vec("L3_gnn_b1"), T0[h], ALU.add, ALU.add).then_inc(st.dve, 1)
                for h in range(2):
                    dve.wait_ge(st.dve, st.dve_at(i, 2, h))
                    dve.tensor_scalar(H[:, chunk(i, h)], T1[h], 0.0, None, ALU.max).then_inc(st.dve, 1)
            copy_table(t_l3b)
            dve.wait_ge(t_l3b.zeroed, 1)
            sum_round(r_l3b)
            dve.wait_ge(r_l3b.agg_free, TWO + TILES)
            with dve.Fori(0, PAIRS) as i:
                st = n_l3b
                for h in range(2):
                    dve.wait_ge(st.pe, st.pe_at(i, 1, h))
                    dve.tensor_tensor(T0[h], sums[:, chunk(i, h)], bank(2, h), ALU.mult).then_inc(st.dve, 1)
                for h in range(2):
                    dve.wait_ge(st.dve, st.dve_at(i, 1, h))
                    dve.scalar_tensor_tensor(T2[h], bank(0, h), vec("L3_gnn_b2"), T0[h], ALU.add, ALU.add).then_inc(st.dve, 1)
                for h in range(2):
                    dve.wait_ge(st.dve, st.dve_at(i, 2, h))
                    dve.tensor_tensor(T1[h], T2[h], X[:, chunk(i, h)], ALU.add).then_inc(st.dve, 1)
                layer_norm(st, i, 3, 1, 1, lambda h: X[:, chunk(i, h)])
            for n in range(N_XG):
                dve.wait_ge(out_ps, n + 1)
                w = min(512, XBLOCKS * P - 512 * n)
                dve.tensor_copy(H[:, 512 * n:512 * n + w], PS[:, n % 8, 0:w]).then_inc(out_sb, 1)


def kernel(**inputs):
    import numpy as _np
    import concourse.bacc as _bacc
    from concourse.bass_utils import run_bass_kernel_spmd as _run

    nc = _bacc.Bacc("TRN2", target_bir_lowering=False, num_devices=1)
    arrays, aps = {}, {}
    for name, value in inputs.items():
        v = _np.ascontiguousarray(value)
        arrays["in_" + name] = v
        aps[name] = nc.dram_tensor("in_" + name, v.shape, mybir.dt.from_np(v.dtype), kind="ExternalInput").ap()
    out = nc.dram_tensor("out_x", (NODES, P), FP32, kind="ExternalOutput").ap()
    build(nc, aps, out)
    r = _run(nc, [arrays], core_ids=[0])
    return r.results[0]["out_x"]
```
